# Optimizing a Trainium2 kernel written in Bass

```python
import numpy as np
import jax
import jax.numpy as jnp

def _softmax(x, axis=-1):
    return jax.nn.softmax(x, axis=axis)

def _gelu(x):
    return jax.nn.gelu(x, approximate=True)

def _silu(x):
    return jax.nn.silu(x)

def _sigmoid(x):
    return jax.nn.sigmoid(x)

def _layernorm(x, axis=-1, eps=1e-05):
    m = jnp.mean(x, axis=axis, keepdims=True)
    v = jnp.var(x, axis=axis, keepdims=True)
    return (x - m) / jnp.sqrt(v + eps)

def _scatter_add(tgt, idx, src, axis=0):
    return tgt.at[idx].add(src)

def _segment_sum(src, seg, n):
    return jax.ops.segment_sum(src, seg, n)
kernel_name = 'mk_prb_d1_jaxref_r2_45f734'

def setup_inputs(seed: int=0):
    np.random.seed(seed)
    _w = jnp.asarray

    def _L0_attn_setup():
        import jax, jax.numpy as jnp
        import numpy as np
        NUM_HEADS = 16
        WINDOW = 64

        def _rel_pos_bias(rel_bias, window):
            coords = jnp.arange(window)
            rel = coords[:, None] - coords[None, :] + (window - 1)
            bias = rel_bias[rel]
            return jnp.transpose(bias, (2, 0, 1))
        key = jax.random.key(seed)
        ks = jax.random.split(key, 5)
        B, S, D = (8, 2048, 512)
        x = jax.random.normal(ks[0], (B, S, D), dtype=jnp.float32)
        qkv_w = jax.random.normal(ks[1], (D, 3 * D), dtype=jnp.float32) * (1.0 / np.sqrt(D))
        qkv_b = jnp.zeros((3 * D,), dtype=jnp.float32)
        proj_w = jax.random.normal(ks[2], (D, D), dtype=jnp.float32) * (1.0 / np.sqrt(D))
        proj_b = jnp.zeros((D,), dtype=jnp.float32)
        rel_bias = jax.random.normal(ks[3], (2 * WINDOW - 1, NUM_HEADS), dtype=jnp.float32) * 0.02
        return {'x': x, 'qkv_w': qkv_w, 'qkv_b': qkv_b, 'proj_w': proj_w, 'proj_b': proj_b, 'rel_bias': rel_bias}
    _L0_attn_in = _L0_attn_setup()

    def _L0_ffn_setup():
        import jax, jax.numpy as jnp
        import numpy as np
        B, T, C, H, E = (4, 1024, 512, 1024, 8)
        CAPACITY_FACTOR = 1.0
        key = jax.random.key(seed)
        ks = jax.random.split(key, 5)
        scale = 0.02
        return {'x': jax.random.normal(ks[0], (B, T, C), dtype=jnp.float32), 'Wg': jax.random.normal(ks[1], (E, C), dtype=jnp.float32) * scale, 'W1': jax.random.normal(ks[2], (E, H, C), dtype=jnp.float32) * scale, 'W2': jax.random.normal(ks[3], (E, C, H), dtype=jnp.float32) * scale, 'W3': jax.random.normal(ks[4], (E, H, C), dtype=jnp.float32) * scale}
    _L0_ffn_in = _L0_ffn_setup()
    _d = {'L0_attn_x': _L0_attn_in['x'], 'L0_attn_qkv_w': _L0_attn_in['qkv_w'], 'L0_attn_qkv_b': _L0_attn_in['qkv_b'], 'L0_attn_proj_w': _L0_attn_in['proj_w'], 'L0_attn_proj_b': _L0_attn_in['proj_b'], 'L0_attn_rel_bias': _L0_attn_in['rel_bias'], 'L0_ffn_Wg': _L0_ffn_in['Wg'], 'L0_ffn_W1': _L0_ffn_in['W1'], 'L0_ffn_W2': _L0_ffn_in['W2'], 'L0_ffn_W3': _L0_ffn_in['W3']}
    _x0 = _d['L0_attn_x']
    _d['L0_attn_x'] = jax.random.normal(jax.random.fold_in(jax.random.key(seed), 1), (2, 4096, 512), dtype=_x0.dtype)
    del _x0
    return _d

def reference(L0_attn_x, L0_attn_qkv_w, L0_attn_qkv_b, L0_attn_proj_w, L0_attn_proj_b, L0_attn_rel_bias, L0_ffn_Wg, L0_ffn_W1, L0_ffn_W2, L0_ffn_W3):

    def _L0_attn_ref(x, qkv_w, qkv_b, proj_w, proj_b, rel_bias):
        import jax, jax.numpy as jnp
        import numpy as np
        NUM_HEADS = 16
        WINDOW = 64

        def _rel_pos_bias(rel_bias, window):
            coords = jnp.arange(window)
            rel = coords[:, None] - coords[None, :] + (window - 1)
            bias = rel_bias[rel]
            return jnp.transpose(bias, (2, 0, 1))
        B, S, D = x.shape
        H, W = (NUM_HEADS, WINDOW)
        hd = D // H
        nW = S // W
        scale = 1.0 / np.sqrt(hd)
        xw = x.reshape(B, nW, W, D)
        qkv = xw @ qkv_w + qkv_b
        qkv = qkv.reshape(B, nW, W, 3, H, hd)
        q, k, v = (qkv[..., 0, :, :], qkv[..., 1, :, :], qkv[..., 2, :, :])
        attn = jnp.einsum('bnqhd,bnkhd->bnhqk', q, k) * scale
        attn = attn + _rel_pos_bias(rel_bias, W)[None, None]
        attn = jax.nn.softmax(attn, axis=-1)
        out = jnp.einsum('bnhqk,bnkhd->bnqhd', attn, v)
        out = out.reshape(B, S, D)
        return out @ proj_w + proj_b

    def _L0_ffn_ref(x, Wg, W1, W2, W3):
        import jax, jax.numpy as jnp
        import numpy as np
        B, T, C, H, E = (4, 1024, 512, 1024, 8)
        CAPACITY_FACTOR = 1.0
        b, t, c = x.shape
        e = Wg.shape[0]
        n = b * t
        capacity = max(1, int(CAPACITY_FACTOR * n / e))
        x_flat = x.reshape(n, c)
        scores = (x_flat @ Wg.T).T
        top_vals, token_idx = jax.lax.top_k(scores, capacity)
        token_w = jax.nn.softmax(top_vals, axis=-1)
        xg = x_flat[token_idx]
        h = jax.nn.silu(jnp.einsum('eic,ehc->eih', xg, W1)) * jnp.einsum('eic,ehc->eih', xg, W3)
        y = jnp.einsum('eih,ech->eic', h, W2) * token_w[..., None]
        out = jnp.zeros_like(x_flat).at[token_idx.reshape(-1)].add(y.reshape(-1, c))
        return out.reshape(b, t, c)
    x = L0_attn_x
    xn = _layernorm(x, axis=-1)
    x = x + _L0_attn_ref(xn, L0_attn_qkv_w, L0_attn_qkv_b, L0_attn_proj_w, L0_attn_proj_b, L0_attn_rel_bias) + _L0_ffn_ref(xn, L0_ffn_Wg, L0_ffn_W1, L0_ffn_W2, L0_ffn_W3)
    return x

_drawn_inputs = setup_inputs


def setup_inputs(seed=0):
    import zlib

    import numpy as np

    out = dict(_drawn_inputs(seed))
    spreads = {'L0_attn_qkv_b': (0.0, 0.1), 'L0_attn_proj_b': (0.0, 0.1)}
    factors = {'L0_attn_rel_bias': 27.386,
     'L0_ffn_Wg': 8.0,
     'L0_ffn_W1': 8.0,
     'L0_ffn_W2': 8.0,
     'L0_ffn_W3': 8.0}
    for name, (base, spread) in spreads.items():
        noise = np.random.default_rng([zlib.crc32(name.encode()), seed]).standard_normal(out[name].shape)
        drawn = base * np.exp(spread * noise) if base else spread * noise
        out[name] = jnp.asarray(drawn.astype(out[name].dtype))
    for name, factor in factors.items():
        out[name] = (out[name] * factor).astype(out[name].dtype)
    return out
```

```python
from contextlib import ExitStack

import concourse.bass as bass
from concourse import mybir
from concourse.alu_op_type import AluOpType as ALU

ACT = mybir.ActivationFunctionType
AX = mybir.AxisListType
F32 = mybir.dt.float32
F32R = mybir.dt.float32r
BF16 = mybir.dt.bfloat16
I32 = mybir.dt.int32
U32 = mybir.dt.uint32

P = 128
N = 8192
C = 512
KC = C // P
T = 512
NCH = N // T
TT = T // P
W = 64
HD = 32
H = C // HD
G = 4
E = 8
F = 1024
FM = F // P
CAP = N // E
NT = N // P
NS = CAP // P
SCALE = HD ** -0.5
EPS = 1e-5


def split3(nc, out, w_hi, w_lo, x_hi, x_lo, start, stop):
    nc.tensor.matmul(out, w_hi, x_hi, start=start, stop=False)
    nc.tensor.matmul(out, w_hi, x_lo, start=False, stop=False)
    return nc.tensor.matmul(out, w_lo, x_hi, start=False, stop=stop)


def attention_block(nc, d, keep):
    ctx = ExitStack()
    with ctx:
        def sb(name, shape, dt=F32):
            return ctx.enter_context(nc.sbuf_tensor(name, shape, dt))

        def sem(name):
            return ctx.enter_context(nc.semaphore(name))

        wq_hi, wq_lo = sb("wq_hi", [P, KC, 3 * C], F32R), sb("wq_lo", [P, KC, 3 * C], F32R)
        wp_hi, wp_lo = sb("wp_hi", [P, KC, C], F32R), sb("wp_lo", [P, KC, C], F32R)
        wg_hi, wg_lo = sb("wg_hi", [P, KC, E], F32R), sb("wg_lo", [P, KC, E], F32R)
        wg_raw = sb("wg_raw", [P, KC, E])
        rel = sb("rel", [P, H, W])
        qk_bias, v_bias, p_bias = sb("qk_bias", [P, 2 * G]), sb("v_bias", [P, C]), sb("p_bias", [P, C])
        ident = sb("ident", [P, P])
        x_in, x_res, xn = sb("x_in", [P, TT, C]), sb("x_res", [P, TT, C]), sb("xn", [P, TT, C])
        stats, mv = sb("stats", [P, TT, 6]), sb("mv", [P, TT, 2])
        veps, rstd, power = sb("veps", [P, TT]), sb("rstd", [P, TT]), sb("power", [P, TT])
        xt_hi, xt_lo = sb("xt_hi", [P, KC, T], F32R), sb("xt_lo", [P, KC, T], F32R)
        q_sb = sb("q_sb", [P, T])
        k_diag = sb("k_diag", [P, T // W, G, W])
        v_sb = sb("v_sb", [P, TT, 2, C // 2])
        s_sb = sb("s_sb", [P, TT, 4, W])
        p_sb = sb("p_sb", [P, TT, 4, W])
        pn_sb = sb("pn_sb", [P, TT, 4, W])
        pt_sb = sb("pt_sb", [P, TT, 2, P])
        s_max, s_sum, s_rec = sb("s_max", [P, 16]), sb("s_sum", [P, 16]), sb("s_rec", [P, 16])
        ot_hi, ot_lo = sb("ot_hi", [P, G, T], F32R), sb("ot_lo", [P, G, T], F32R)
        g_sb = sb("g_sb", [E, T])
        stage = x_in[:, :, :].rearrange("p a b -> p (a b)")
        stage2 = x_res[:, :, :].rearrange("p a b -> p (a b)")
        ps = ctx.enter_context(nc.psum_tensor("ps", [P, 8, 512], F32))
        QB, KB, SP, OT = 0, 1, 2, 4
        V_BANK, P_BANK, X_BANK, G_BANK = (5, 6, 7, 5), (6, 7, 5, 6), (7, 5, 6, 7), 5
        s_bank = ps[:, SP:SP + 2, :].rearrange("p b (t h k) -> p (b t) h k", t=2, h=4)

        const_in = sem("const_in")
        raw_in = [sem(f"raw_in_{i}") for i in range(2)]
        raw_hi, raw_lo = sem("raw_hi"), sem("raw_lo")
        consts = sem("consts")
        x_loaded, xn_ready, xn_stored = sem("x_loaded"), sem("xn_ready"), sem("xn_stored")
        stat_ready, mv_ready, veps_ready, rstd_ready = sem("stat_ready"), sem("mv_ready"), sem("veps_ready"), sem("rstd_ready")
        xt_mm, xt_hi_ready, xt_ready = sem("xt_mm"), sem("xt_hi_ready"), sem("xt_ready")
        gate_mm, gate_sb_ready, gate_t_mm, gate_kept = sem("gate_mm"), sem("gate_sb_ready"), sem("gate_t_mm"), sem("gate_kept")
        q_mm, k_mm, q_ready = sem("q_mm"), sem("k_mm"), sem("q_ready")
        ka_ready, kb_ready = sem("ka_ready"), sem("kb_ready")
        v_mm, v_ready = sem("v_mm"), sem("v_ready")
        s_mm, s_ready, max_ready, sub_ready = sem("s_mm"), sem("s_ready"), sem("max_ready"), sem("sub_ready")
        exp_ready, sum_ready, rec_ready, norm_ready = sem("exp_ready"), sem("sum_ready"), sem("rec_ready"), sem("norm_ready")
        pt_mm, pta_ready, ptb_ready = sem("pt_mm"), sem("pta_ready"), sem("ptb_ready")
        o_mm, o_hi_ready, o_ready = sem("o_mm"), sem("o_hi_ready"), sem("o_ready")
        p_mm, out_ready, out_stored = sem("p_mm"), sem("out_ready"), sem("out_stored")
        res_loaded, res_ready = sem("res_loaded"), sem("res_ready")

        def raw_units():
            wqf = [w[:, :, :].rearrange("p a b -> p (a b)") for w in (wq_hi, wq_lo)]
            wpf = [w[:, :, :].rearrange("p a b -> p (a b)") for w in (wp_hi, wp_lo)]
            for u in range(3):
                s = slice(2048 * u, 2048 * (u + 1))
                yield d["wqkv"][:, s], wqf[0][:, s], wqf[1][:, s]
            yield d["wp"], wpf[0][:, :], wpf[1][:, :]

        units = list(raw_units())
        RAW = [stage, stage2]

        block = ctx.enter_context(nc.Block())

        @block.sync
        def _(sp):
            for dst, src in ((wg_raw[:, :, :], d["wg"]), (rel[:, :, :], d["rel"]), (qk_bias[:, :], d["qkb"]),
                             (v_bias[:, :], d["vb"]), (p_bias[:, :], d["pb"])):
                sp.dma_start(dst, src).then_inc(const_in, 16)
            for u, (src, _, _) in enumerate(units):
                if u >= 2:
                    sp.wait_ge(raw_lo, u - 1)
                sp.dma_start(RAW[u % 2], src).then_inc(raw_in[u % 2], 16)
            sp.wait_ge(raw_lo, 3)
            sp.dma_start(x_in[:, :, :], d["x"][0]).then_inc(x_loaded, 16)

            def keep_xn(c):
                sp.wait_ge(xn_ready, TT * (c + 1))
                sp.dma_start(d["xn"][c], xn[:, :, :]).then_inc(xn_stored, 16)

            def load_x(c):
                sp.dma_start(x_in[:, :, :], d["x"][c]).then_inc(x_loaded, 16)

            def store_out(c):
                sp.wait_ge(out_ready, TT * (c + 1))
                sp.dma_start(d["out"][c], x_res[:, :, :]).then_inc(out_stored, 16)
                sp.wait_ge(out_stored, 16 * (c + 1))

            def load_res(c):
                sp.dma_start(x_res[:, :, :], d["x"][c]).then_inc(res_loaded, 16)

            keep_xn(0)
            load_x(1)
            sp.wait_ge(raw_lo, 4)
            load_res(0)
            keep_xn(1)
            load_x(2)
            with sp.Fori(1, NCH - 2) as c:
                keep_xn(c + 1)
                load_x(c + 2)
                store_out(c - 1)
                load_res(c)
            keep_xn(NCH - 1)
            for c in (NCH - 3, NCH - 2):
                store_out(c)
                load_res(c + 1)
            store_out(NCH - 1)
            sp.wait_ge(xn_stored, 16 * NCH)

        @block.gpsimd
        def _(pool):
            nc.gpsimd.memset(ident[:, :], 0.0).then_inc(consts, 1)
            nc.gpsimd.memset(power[:, :], -0.5).then_inc(consts, 1)
            nc.gpsimd.memset(k_diag[:, :, :, :], 0.0).then_inc(consts, 1)
            pool.wait_ge(consts, 3)
            nc.gpsimd.affine_select(out=ident[:, :], in_=ident[:, :], compare_op=ALU.not_equal, fill=1.0,
                                    base=0, pattern=[[-1, P]], channel_multiplier=1).then_inc(consts, 1)

            def layernorm_rstd(c):
                pool.wait_ge(veps_ready, c + 1)
                nc.gpsimd.tensor_tensor(rstd[:, :], veps[:, :], power[:, :], ALU.pow).then_inc(rstd_ready, 1)

            def residual(c):
                pool.wait_ge(res_loaded, 16 * (c + 1))
                nc.gpsimd.tensor_tensor(x_res[:, :, :], x_res[:, :, :],
                                        p_bias[:, :].unsqueeze(1).to_broadcast([P, TT, C]), ALU.add).then_inc(res_ready, 1)

            def softmax(s):
                pool.wait_ge(max_ready, s + 1)
                nc.gpsimd.tensor_tensor(s_sb[:, :, :, :], s_sb[:, :, :, :],
                                        s_max[:, :].rearrange("p (t h) -> p t h", t=TT).unsqueeze(3)
                                        .to_broadcast([P, TT, 4, W]), ALU.subtract).then_inc(sub_ready, 1)
                pool.wait_ge(rec_ready, s + 1)
                if not isinstance(s, int) or s >= 1:
                    pool.wait_ge(pt_mm, 2 * s)
                nc.gpsimd.tensor_tensor(pn_sb[:, :, :, :], p_sb[:, :, :, :],
                                        s_rec[:, :].rearrange("p (t h) -> p t h", t=TT).unsqueeze(3)
                                        .to_broadcast([P, TT, 4, W]), ALU.mult).then_inc(norm_ready, 1)

            def chunk(c, first=False, last=False):
                if not first:
                    softmax(G * c - 1)
                if not last:
                    layernorm_rstd(c + 1)
                softmax(G * c)
                if not first:
                    pool.wait_ge(const_in, 80)
                    residual(c - 1)
                softmax(G * c + 1)
                softmax(G * c + 2)

            pool.wait_ge(consts, 4)
            layernorm_rstd(0)
            chunk(0, first=True)
            with pool.Fori(1, NCH - 1) as c:
                chunk(c)
            chunk(NCH - 1, last=True)
            softmax(G * NCH - 1)
            residual(NCH - 1)

        @block.scalar
        def _(act):
            for u, (_, hi, _) in enumerate(units):
                act.wait_ge(raw_in[u % 2], 16 * (u // 2 + 1))
                nc.scalar.activation(hi, RAW[u % 2], ACT.Copy).then_inc(raw_hi, 1)
                if u == 0:
                    act.wait_ge(const_in, 80)
                    nc.scalar.activation(wg_hi[:, :, :], wg_raw[:, :, :], ACT.Copy).then_inc(raw_hi, 1)

            def xt_hi_part(c):
                for k in range(KC):
                    act.wait_ge(xt_mm, KC * c + k + 1)
                    nc.scalar.activation(xt_hi[:, k, :], ps[:, X_BANK[k], :], ACT.Copy).then_inc(xt_hi_ready, 1)

            def step(s, g, c, scores, qk, pv, next_x):
                if qk:
                    act.wait_ge(q_mm, s + 1)
                    if scores:
                        act.wait_ge(s_mm, 2 * s)
                    nc.scalar.activation(q_sb[:, :], ps[:, QB, :], ACT.Identity, bias=qk_bias[:, g:g + 1]).then_inc(q_ready, 1)
                if pv:
                    act.wait_ge(pt_mm, 2 * (s - 2) + 1)
                    if not isinstance(s, int) or s >= 3:
                        act.wait_ge(o_mm, s - 2)
                    nc.scalar.activation(pt_sb[:, 0:2, :, :].rearrange("p t h q -> p (t h q)"), ps[:, SP, :],
                                         ACT.Copy).then_inc(pta_ready, 1)
                if scores:
                    act.wait_ge(sub_ready, s)
                    nc.scalar.activation(p_sb[:, :, :, :], s_sb[:, :, :, :], ACT.Exp).then_inc(exp_ready, 1)
                if qk:
                    act.wait_ge(k_mm, s + 1)
                    for h in range(2):
                        r = slice(HD * h, HD * (h + 1))
                        i = nc.scalar.activation(k_diag[r, :, h, :], ps[r, KB, :].rearrange("p (w k) -> p w k", k=W),
                                                 ACT.Identity, bias=qk_bias[r, G + g:G + g + 1])
                    i.then_inc(ka_ready, 1)
                if next_x:
                    xt_hi_part(c + 1)
                if pv:
                    act.wait_ge(o_mm, s - 1)
                    m = (g + 2) % G
                    if m == 0 and not (isinstance(s, int) and s < 6):
                        act.wait_ge(p_mm, TT * (c if g == 2 else c + 1))
                    nc.scalar.activation(ot_hi[:, m, :], ps[:, OT, :], ACT.Copy).then_inc(o_hi_ready, 1)

            def chunk(c, first=False, last=False):
                for g in range(G):
                    s = G * c + g
                    step(s, g, c, scores=not (first and g == 0), qk=True, pv=not (first and g < 2),
                         next_x=(g == 3 and not last))

            act.wait_ge(consts, 4)
            xt_hi_part(0)
            chunk(0, first=True)
            with act.Fori(1, NCH - 1) as c:
                chunk(c)
            chunk(NCH - 1, last=True)
            step(G * NCH, 0, NCH, scores=True, qk=False, pv=True, next_x=False)
            step(G * NCH + 1, 1, NCH, scores=False, qk=False, pv=True, next_x=False)

        @block.tensor
        def _(pe):
            def xt(c):
                pe.wait_ge(xn_ready, TT * (c + 1))
                for k in range(KC):
                    if isinstance(c, int) and c <= 1:
                        if c == 1:
                            pe.wait_ge(v_ready, TT)
                        if k == 3:
                            pe.wait_ge(xt_ready, KC * c + 1)
                    else:
                        if k < 3:
                            pe.wait_ge(out_ready, TT * (c - 2) + k + 2)
                        else:
                            pe.wait_ge(xt_ready, KC * c + 1)
                    for t in range(TT):
                        i = nc.tensor.transpose(ps[:, X_BANK[k], P * t:P * (t + 1)], xn[:, t, P * k:P * (k + 1)], ident[:, :])
                    i.then_inc(xt_mm, 1)

            def gate(c):
                pe.wait_ge(xt_ready, KC * (c + 1))
                for k in range(KC):
                    i = split3(nc, ps[0:E, G_BANK, :], wg_hi[:, k, :], wg_lo[:, k, :], xt_hi[:, k, :], xt_lo[:, k, :],
                               k == 0, k == KC - 1)
                i.then_inc(gate_mm, 1)

            def gate_transposes(c):
                pe.wait_ge(gate_sb_ready, c + 1)
                pe.nop(nofuse=True)
                for t in range(TT):
                    i = nc.tensor.transpose(ps[:, G_BANK, E * t:E * (t + 1)], g_sb[:, P * t:P * (t + 1)], ident[0:E, 0:E])
                i.then_inc(gate_t_mm, 1)

            def scores(s):
                pe.wait_ge(q_ready, s + 1)
                pe.wait_ge(ka_ready, s + 1)
                pe.wait_ge(kb_ready, s + 1)
                if not isinstance(s, int) or s >= 2:
                    pe.wait_ge(pta_ready, s - 1)
                    pe.wait_ge(ptb_ready, s - 1)
                for t in range(TT):
                    for j in range(4):
                        w = 2 * t + j // 2
                        i = nc.tensor.matmul(ps[32 * j:32 * (j + 1), SP + t // 2, 256 * (t % 2):256 * (t % 2 + 1)],
                                             q_sb[:, P * t + 32 * j:P * t + 32 * (j + 1)],
                                             k_diag[:, w, :, :].rearrange("p h k -> p (h k)"), start=True, stop=True)
                    if t % 2:
                        i.then_inc(s_mm, 1)

            def project_q(s, g):
                if not isinstance(s, int) or s >= 1:
                    pe.wait_ge(q_ready, s)
                for k in range(KC):
                    sl = slice(P * g, P * (g + 1))
                    i = split3(nc, ps[:, QB, :], wq_hi[:, k, sl], wq_lo[:, k, sl], xt_hi[:, k, :], xt_lo[:, k, :],
                               k == 0, k == KC - 1)
                i.then_inc(q_mm, 1)

            def project_k(s, g):
                if not isinstance(s, int) or s >= 1:
                    pe.wait_ge(ka_ready, s)
                    pe.wait_ge(kb_ready, s)
                for k in range(KC):
                    sl = slice(C + P * g, C + P * (g + 1))
                    i = split3(nc, ps[:, KB, :], wq_hi[:, k, sl], wq_lo[:, k, sl], xt_hi[:, k, :], xt_lo[:, k, :],
                               k == 0, k == KC - 1)
                i.then_inc(k_mm, 1)

            def project_v(c):
                for t in range(TT):
                    if t == 0:
                        pe.wait_ge(gate_kept, c + 1)
                    if t == 3:
                        pe.wait_ge(v_ready, TT * c + 1)
                    for k in range(KC):
                        i = split3(nc, ps[:, V_BANK[t], :], xt_hi[:, k, P * t:P * (t + 1)], xt_lo[:, k, P * t:P * (t + 1)],
                                   wq_hi[:, k, 2 * C:], wq_lo[:, k, 2 * C:], k == 0, k == KC - 1)
                    i.then_inc(v_mm, 1)

            def probs_t(s):
                pe.wait_ge(norm_ready, s + 1)
                if isinstance(s, int) and s == G * NCH - 1:
                    pe.wait_ge(pta_ready, s)
                    pe.wait_ge(ptb_ready, s)
                else:
                    pe.wait_ge(s_ready, 2 * s + 4)
                for t in range(TT):
                    for hp in range(2):
                        i = nc.tensor.transpose(ps[:, SP + t // 2, 256 * (t % 2) + P * hp:256 * (t % 2) + P * (hp + 1)],
                                                pn_sb[:, t, 2 * hp:2 * hp + 2, :].rearrange("p h k -> p (h k)"), ident[:, :])
                    if t % 2:
                        i.then_inc(pt_mm, 1)

            def pv(s, m):
                pe.wait_ge(pta_ready, s + 1)
                pe.wait_ge(ptb_ready, s + 1)
                if not isinstance(s, int) or s >= 1:
                    pe.wait_ge(o_ready, s)
                pe.nop(nofuse=True)
                for t in range(TT):
                    for w in range(2):
                        for h in range(4):
                            r = slice(W * (h % 2), W * (h % 2 + 1))
                            col = HD * (2 * m + h // 2)
                            i = nc.tensor.matmul(ps[HD * h:HD * (h + 1), OT, P * t + W * w:P * t + W * (w + 1)],
                                                 v_sb[r, t, w, col:col + HD], pt_sb[r, t, h // 2, W * w:W * (w + 1)],
                                                 start=True, stop=True)
                i.then_inc(o_mm, 1)

            def project_out(c):
                pe.wait_ge(o_ready, G * (c + 1))
                for t in range(TT):
                    if t < 3:
                        pe.wait_ge(v_ready, TT * (c + 2) if not isinstance(c, int) or c < NCH - 1 else TT * NCH)
                    else:
                        pe.wait_ge(out_ready, TT * c + 1)
                    for k in range(KC):
                        i = split3(nc, ps[:, P_BANK[t], :], ot_hi[:, k, P * t:P * (t + 1)], ot_lo[:, k, P * t:P * (t + 1)],
                                   wp_hi[:, k, :], wp_lo[:, k, :], k == 0, k == KC - 1)
                    i.then_inc(p_mm, 1)

            def chunk(c, first=False, last=False):
                s = G * c
                if not first:
                    scores(s - 1)
                project_q(s, 0)
                gate_transposes(c)
                if not first:
                    probs_t(s - 2)
                project_k(s, 0)
                if not first:
                    pv(s - 2, 2)
                scores(s)
                project_q(s + 1, 1)
                if not first:
                    probs_t(s - 1)
                project_k(s + 1, 1)
                if not first:
                    pv(s - 1, 3)
                project_v(c)
                scores(s + 1)
                if not first:
                    project_out(c - 1)
                project_q(s + 2, 2)
                probs_t(s)
                project_k(s + 2, 2)
                pe.wait_ge(v_ready, TT * (c + 1))
                pv(s, 0)
                scores(s + 2)
                project_q(s + 3, 3)
                probs_t(s + 1)
                project_k(s + 3, 3)
                if not last:
                    xt(c + 1)
                pv(s + 1, 1)
                if not last:
                    gate(c + 1)

            pe.wait_ge(consts, 4)
            xt(0)
            pe.wait_ge(raw_lo, 5)
            gate(0)
            chunk(0, first=True)
            with pe.Fori(1, NCH - 1) as c:
                chunk(c)
            chunk(NCH - 1, last=True)
            s = G * NCH
            scores(s - 1)
            probs_t(s - 2)
            pv(s - 2, 2)
            probs_t(s - 1)
            pv(s - 1, 3)
            project_out(NCH - 1)

        @block.vector
        def _(dve):
            for u, (_, hi, lo) in enumerate(units):
                dve.wait_ge(raw_hi, u + 1 if u == 0 else u + 2)
                nc.vector.tensor_tensor(lo, RAW[u % 2], hi.bitcast(F32), ALU.subtract).then_inc(raw_lo, 1)
            nc.vector.tensor_tensor(wg_lo[:, :, :], wg_raw[:, :, :], wg_hi[:, :, :].bitcast(F32), ALU.subtract).then_inc(raw_lo, 1)

            def layernorm_stats(c):
                dve.wait_ge(x_loaded, 16 * (c + 1))
                for t in range(TT):
                    i = nc.vector.bn_stats(stats[:, t, :], x_in[:, t, :])
                i.then_inc(stat_ready, 1)
                dve.wait_ge(stat_ready, c + 1)
                dve.nop(nofuse=True)
                for t in range(TT):
                    i = nc.vector.bn_aggr(mv[:, t, :], stats[:, t, :])
                i.then_inc(mv_ready, 1)
                dve.wait_ge(mv_ready, c + 1)
                nc.vector.tensor_scalar(veps[:, :], mv[:, :, 1], EPS, None, ALU.add).then_inc(veps_ready, 1)

            def layernorm_apply(c):
                dve.wait_ge(rstd_ready, c + 1)
                if not isinstance(c, int) or c >= 1:
                    dve.wait_ge(xn_stored, 16 * c)
                    dve.wait_ge(xt_mm, KC * c)
                for t in range(TT):
                    nc.vector.tensor_scalar(xn[:, t, :], x_in[:, t, :], mv[:, t, 0:1], rstd[:, t:t + 1],
                                            ALU.subtract, ALU.mult).then_inc(xn_ready, 1)

            def xt_lo_part(c):
                for k in range(KC):
                    dve.wait_ge(xt_hi_ready, KC * c + k + 1)
                    nc.vector.tensor_tensor(xt_lo[:, k, :], ps[:, X_BANK[k], :], xt_hi[:, k, :].bitcast(F32),
                                            ALU.subtract).then_inc(xt_ready, 1)

            def gate_rows(c):
                dve.wait_ge(gate_mm, c + 1)
                nc.vector.tensor_copy(g_sb[:, :], ps[0:E, G_BANK, :]).then_inc(gate_sb_ready, 1)

            def gate_keep(c):
                dve.wait_ge(gate_t_mm, c + 1)
                nc.vector.tensor_copy(keep["scores"][:, :, bass.ds(TT * c, TT)],
                                      ps[:, G_BANK, 0:E * TT].rearrange("p (t e) -> p e t", e=E)).then_inc(gate_kept, 1)

            def scale_and_bias(s, m):
                for b in range(2):
                    dve.wait_ge(s_mm, 2 * s + b + 1)
                    if b == 0 and (not isinstance(s, int) or s >= 1):
                        dve.wait_ge(exp_ready, s)
                    nc.vector.scalar_tensor_tensor(
                        s_sb[:, 2 * b:2 * b + 2, :, :].rearrange("p t h k -> p t (h k)"),
                        ps[:, SP + b, :].rearrange("p (t n) -> p t n", t=2), SCALE,
                        rel[:, 4 * m:4 * m + 4, :].rearrange("p h k -> p (h k)").unsqueeze(1).to_broadcast([P, 2, 4 * W]),
                        ALU.mult, ALU.add).then_inc(s_ready, 1)
                dve.wait_ge(s_ready, 2 * s + 2)
                nc.vector.tensor_reduce(s_max[:, :], s_sb[:, :, :, :].rearrange("p t h k -> p (t h) k"), AX.X, ALU.max).then_inc(max_ready, 1)

            def normaliser(s):
                dve.wait_ge(exp_ready, s + 1)
                nc.vector.tensor_reduce(s_sum[:, :], p_sb[:, :, :, :].rearrange("p t h k -> p (t h) k"), AX.X, ALU.add).then_inc(sum_ready, 1)
                dve.wait_ge(sum_ready, s + 1)
                if not isinstance(s, int) or s >= 1:
                    dve.wait_ge(norm_ready, s)
                nc.vector.reciprocal(s_rec[:, :], s_sum[:, :]).then_inc(rec_ready, 1)

            def finish_rows(c):
                dve.wait_ge(res_ready, c + 1)
                for t in range(TT):
                    dve.wait_ge(p_mm, TT * c + t + 1)
                    nc.vector.tensor_tensor(x_res[:, t, :], ps[:, P_BANK[t], :], x_res[:, t, :], ALU.add).then_inc(out_ready, 1)

            def probs_t_part(s):
                dve.wait_ge(pt_mm, 2 * s + 2)
                if not isinstance(s, int) or s >= 1:
                    dve.wait_ge(o_mm, s)
                nc.vector.tensor_copy(pt_sb[:, 2:4, :, :].rearrange("p t h q -> p (t h q)"), ps[:, SP + 1, :]).then_inc(ptb_ready, 1)

            def k_part(s, g):
                dve.wait_ge(k_mm, s + 1)
                for h in (2, 3):
                    r = slice(HD * h, HD * (h + 1))
                    i = nc.vector.tensor_scalar(k_diag[r, :, h, :], ps[r, KB, :].rearrange("p (w k) -> p w k", k=W),
                                                qk_bias[r, G + g:G + g + 1], None, ALU.add)
                i.then_inc(kb_ready, 1)

            def v_part(c):
                dve.wait_ge(o_mm, G * c) if not isinstance(c, int) or c >= 1 else None
                for t in range(TT):
                    dve.wait_ge(v_mm, TT * c + t + 1)
                    for w in range(2):
                        for par in range(2):
                            src = slice(W * w, W * (w + 1))
                            heads = "p (hp par d) -> p par hp d"
                            i = nc.vector.tensor_tensor(
                                v_sb[W * par:W * (par + 1), t, w, :].rearrange("p (hp d) -> p hp d", d=HD),
                                ps[src, V_BANK[t], :].rearrange(heads, par=2, d=HD)[:, par],
                                v_bias[src, :].rearrange(heads, par=2, d=HD)[:, par], ALU.add)
                    i.then_inc(v_ready, 1)

            def o_lo_part(s, m):
                dve.wait_ge(o_hi_ready, s + 1)
                nc.vector.tensor_tensor(ot_lo[:, m, :], ps[:, OT, :], ot_hi[:, m, :].bitcast(F32), ALU.subtract).then_inc(o_ready, 1)

            def chunk(c, first=False, last=False):
                s = G * c
                if not first:
                    scale_and_bias(s - 1, 3)
                gate_keep(c)
                if not first:
                    probs_t_part(s - 2)
                k_part(s, 0)
                if not first:
                    normaliser(s - 1)
                if not last:
                    layernorm_stats(c + 1)
                if not first:
                    o_lo_part(s - 2, 2)
                scale_and_bias(s, 0)
                if not first:
                    probs_t_part(s - 1)
                k_part(s + 1, 1)
                normaliser(s)
                if not last:
                    layernorm_apply(c + 1)
                if not first:
                    o_lo_part(s - 1, 3)
                v_part(c)
                scale_and_bias(s + 1, 1)
                if not first:
                    finish_rows(c - 1)
                probs_t_part(s)
                k_part(s + 2, 2)
                normaliser(s + 1)
                o_lo_part(s, 0)
                scale_and_bias(s + 2, 2)
                probs_t_part(s + 1)
                k_part(s + 3, 3)
                normaliser(s + 2)
                if not last:
                    xt_lo_part(c + 1)
                o_lo_part(s + 1, 1)
                if not last:
                    gate_rows(c + 1)

            layernorm_stats(0)
            layernorm_apply(0)
            xt_lo_part(0)
            gate_rows(0)
            dve.wait_ge(const_in, 80)
            dve.wait_ge(consts, 4)
            chunk(0, first=True)
            with dve.Fori(1, NCH - 1) as c:
                chunk(c)
            chunk(NCH - 1, last=True)
            s = G * NCH
            scale_and_bias(s - 1, 3)
            probs_t_part(s - 2)
            normaliser(s - 1)
            o_lo_part(s - 2, 2)
            probs_t_part(s - 1)
            o_lo_part(s - 1, 3)
            finish_rows(NCH - 1)


def expert_block(nc, d, scores):
    ctx = ExitStack()
    with ctx:
        def sb(name, shape, dt=F32):
            return ctx.enter_context(nc.sbuf_tensor(name, shape, dt))

        def sem(name):
            return ctx.enter_context(nc.semaphore(name))

        HALVES = 2
        w13_hi, w13_lo = sb("w13_hi", [P, FM, 2, KC, P], F32R), sb("w13_lo", [P, FM, 2, KC, P], F32R)
        w2_hi, w2_lo = sb("w2_hi", [P, FM, C], F32R), sb("w2_lo", [P, FM, C], F32R)
        raw = sb("raw", [P, 2, 1024])
        h_hi, h_lo = sb("h_hi", [P, FM, T], F32R), sb("h_lo", [P, FM, T], F32R)
        xg = sb("xg", [P, TT, C])
        xgt_hi, xgt_lo = sb("xgt_hi", [P, KC, T], F32R), sb("xgt_lo", [P, KC, T], F32R)
        silu, hm = sb("silu", [P, 2, T]), sb("hm", [P, 2, T])
        y = sb("y", [P, TT, C])
        ident2 = sb("ident2", [P, P])
        ones_b, below_b = sb("ones_b", [P, P], BF16), sb("below_b", [P, P], BF16)
        ones_f = sb("ones_f", [P, P])
        iota_b, iota_8 = sb("iota_b", [P, P], BF16), sb("iota_8", [P, NS], BF16)
        iota_p, iota_t = sb("iota_p", [P, 1]), sb("iota_t", [P, NT], BF16)
        one_i, shift, key, cand, flip, thr = (sb(n, [P, E], I32) for n in ("one_i", "shift", "key", "cand", "flip", "thr"))
        count, room, top, total, rtotal, part = (sb(n, [P, E]) for n in ("count", "room", "top", "total", "rtotal", "part"))
        mask = sb("mask", [P, E, NT], BF16)
        eq = sb("eq", [P, E, NT], BF16)
        tmp, carry = sb("tmp", [P, E, NT]), sb("carry", [P, E, NT])
        pos_i = sb("pos_i", [P, E, NT], I32)
        slot_b, slot_a = sb("slot_b", [P, E, NT], BF16), sb("slot_a", [P, E, NT], BF16)
        vals = sb("vals", [P, E, NT, 5], BF16)
        hot_a = sb("hot_a", [P, NT, NS], BF16)
        hot_v = sb("hot_v", [P, NT, 5, NS], BF16)
        HG = 16
        hot_b = sb("hot_b", [P, 1, HG, P], BF16)
        got = sb("got", [P, 5, NS])
        idx_f = sb("idx_f", [P, NS])
        idx = [sb(f"idx_{i}", [P, NS], U32) for i in range(2)]
        weight = [sb(f"weight_{i}", [P, NS]) for i in range(2)]
        ps = ctx.enter_context(nc.psum_tensor("ps_e", [P, 8, 512], F32))
        DOWN = 4

        consts2 = sem("consts2")
        step_done = sem("step_done")
        count_mm, tie_mm, pos_mm, total_mm = sem("count_mm"), sem("tie_mm"), sem("pos_mm"), sem("total_mm")
        mask_ready, eq_ready, sel_ready, part_ready = sem("mask_ready"), sem("eq_ready"), sem("sel_ready"), sem("part_ready")
        top_part, top_all, shifted, expd = sem("top_part"), sem("top_all"), sem("shifted"), sem("expd")
        hot_ready, hot_mm, idx_ready = sem("hot_ready"), sem("hot_mm"), sem("idx_ready")
        got_ready = sem("got_ready")
        w_in = [sem(f"w_in_{i}") for i in range(2)]
        w_hi_ready, w_ready = sem("w_hi_ready"), sem("w_ready")
        xg_in = sem("xg_in")
        xgt_mm, xgt_hi_ready, xgt_ready = sem("xgt_mm"), sem("xgt_hi_ready"), sem("xgt_ready")
        up1_mm, up3_mm, silu_ready, hm_ready = sem("up1_mm"), sem("up3_mm"), sem("silu_ready"), sem("hm_ready")
        h_hi_ready, h_ready = sem("h_hi_ready"), sem("h_ready")
        down_mm, y_mm, y_ready, scattered = sem("down_mm"), sem("y_mm"), sem("y_ready"), sem("scattered")

        block = ctx.enter_context(nc.Block())
        UNITS = FM + FM // 2

        def unit_views(u):
            if u < FM:
                return [w[:, u, :, :, :].rearrange("p a b c -> p (a b c)") for w in (w13_hi, w13_lo)]
            v = 2 * (u - FM)
            return [w[:, v:v + 2, :].rearrange("p a b -> p (a b)") for w in (w2_hi, w2_lo)]


        @block.sync
        def _(sp):
            def load_unit(e, u):
                n = UNITS * e + u
                if not isinstance(n, int) or n >= 2:
                    sp.wait_ge(w_ready, n - 1)
                src = d["w13"][e, u] if u < FM else d["w2"][e, u - FM]
                sp.dma_start(raw[:, u % 2, :], src).then_inc(w_in[u % 2], 16)

            for u in range(UNITS):
                load_unit(0, u)
            with sp.Fori(1, E) as e:
                for u in range(UNITS):
                    load_unit(e, u)

        @block.gpsimd
        def _(pool):
            nc.gpsimd.memset(ident2[:, :], 0.0).then_inc(consts2, 1)
            nc.gpsimd.memset(ones_b[:, :], 1.0).then_inc(consts2, 1)
            nc.gpsimd.memset(ones_f[:, :], 1.0).then_inc(consts2, 1)
            nc.gpsimd.memset(one_i[:, :], 1).then_inc(consts2, 1)
            nc.gpsimd.memset(shift[:, :], 31).then_inc(consts2, 1)
            nc.gpsimd.memset(key[:, :], 0).then_inc(consts2, 1)
            pool.wait_ge(consts2, 6)
            nc.gpsimd.affine_select(out=ident2[:, :], in_=ident2[:, :], compare_op=ALU.not_equal, fill=1.0,
                                    base=0, pattern=[[-1, P]], channel_multiplier=1).then_inc(consts2, 1)
            nc.gpsimd.affine_select(out=below_b[:, :], in_=ones_b[:, :], compare_op=ALU.is_gt, fill=0.0,
                                    base=0, pattern=[[1, P]], channel_multiplier=-1).then_inc(consts2, 1)
            wide = dict(allow_small_or_imprecise_dtypes=True)
            nc.gpsimd.iota(iota_b[:, :], [[1, P]], 0, 0, **wide).then_inc(consts2, 1)
            nc.gpsimd.iota(iota_8[:, :], [[1, NS]], 0, 0, **wide).then_inc(consts2, 1)
            nc.gpsimd.iota(iota_t[:, :], [[1, NT]], 0, 0, **wide).then_inc(consts2, 1)
            nc.gpsimd.iota(iota_p[:, :], [[0, 1]], 0, 1, **wide).then_inc(consts2, 1)
            pool.wait_ge(top_part, 1)
            nc.gpsimd.partition_all_reduce(top[:, :], part[:, :], P, bass.bass_isa.ReduceOp.max).then_inc(top_all, 1)

            def gather(q, slot0, e_idx):
                pool.wait_ge(idx_ready, e_idx)
                if not isinstance(q, int) or q >= 1:
                    pool.wait_ge(xgt_mm, KC * q)
                pool.nop(nofuse=True)
                for t in range(TT):
                    nc.gpsimd.indirect_dma_start(
                        out=xg[:, t, :], out_offset=None, in_=d["xn"],
                        in_offset=bass.IndirectOffsetOnAxis(ap=slot0[1][:, slot0[0] + t:slot0[0] + t + 1], axis=0)
                    ).then_inc(xg_in, 16)

            def scatter(q, slot0):
                for t in range(TT):
                    pool.wait_ge(y_ready, TT * q + t + 1)
                    if not isinstance(q, int) or q >= 1 or t >= 1:
                        pool.wait_ge(scattered, 16 * (TT * q + t))
                    pool.nop(nofuse=True)
                    nc.gpsimd.indirect_dma_start(
                        out=d["out"], out_offset=bass.IndirectOffsetOnAxis(ap=slot0[1][:, slot0[0] + t:slot0[0] + t + 1], axis=0),
                        in_=y[:, t, :], in_offset=None, compute_op=ALU.add).then_inc(scattered, 16)

            gather(0, (0, idx[0]), 1)

            def expert(e, par, first=False, last=False):
                q = HALVES * e
                gather(q + 1, (TT, idx[par]), e + 1)
                if not first:
                    scatter(q - 1, (TT, idx[1 - par]))
                if not last:
                    gather(q + 2, (0, idx[1 - par]), e + 2)
                scatter(q, (0, idx[par]))

            expert(0, 0, first=True)
            expert(1, 1)
            with pool.Fori(1, E // 2 - 1) as i:
                expert(2 * i, 0)
                expert(2 * i + 1, 1)
            expert(E - 2, 0)
            expert(E - 1, 1, last=True)
            scatter(HALVES * E - 1, (TT, idx[1]))
            pool.wait_ge(scattered, 16 * TT * HALVES * E)

        @block.scalar
        def _(act):
            def split_hi(e, u):
                n = UNITS * e + u
                act.wait_ge(w_in[u % 2], 16 * (UNITS // 2 * e + u // 2 + 1))
                if not isinstance(e, int) or e >= 1:
                    if u < FM:
                        act.wait_ge(up3_mm, FM * (HALVES * e - 1) + u + 1)
                    else:
                        act.wait_ge(y_mm, TT * HALVES * e)
                nc.scalar.activation(unit_views(u)[0], raw[:, u % 2, :], ACT.Copy).then_inc(w_hi_ready, 1)

            def xgt_hi_part(q):
                for k in range(KC):
                    act.wait_ge(xgt_mm, KC * q + k + 1)
                    nc.scalar.activation(xgt_hi[:, k, :], ps[:, k, :], ACT.Copy).then_inc(xgt_hi_ready, 1)

            def half(e, q, hf, par, splits, last=False):
                for m in range(FM):
                    n = FM * q + m
                    act.wait_ge(up1_mm, n + 1)
                    if not isinstance(n, int) or n >= 2:
                        act.wait_ge(hm_ready, n - 1)
                    nc.scalar.activation(silu[:, m % 2, :], ps[:, 2 * (m % 2), :], ACT.Silu).then_inc(silu_ready, 1)
                    act.wait_ge(hm_ready, n + 1)
                    if not isinstance(q, int) or q >= 1:
                        if m < FM - 1:
                            act.wait_ge(down_mm, (FM - 1) * (q - 1) + m + 1)
                        else:
                            act.wait_ge(y_mm, TT * q)
                    nc.scalar.activation(h_hi[:, m, :], hm[:, m % 2, :], ACT.Copy).then_inc(h_hi_ready, 1)
                    if m < len(splits):
                        split_hi(*splits[m])
                if not last:
                    xgt_hi_part(q + 1)
                for t in range(TT):
                    act.wait_ge(y_mm, TT * q + t + 1)
                    if not isinstance(q, int) or q >= 1:
                        act.wait_ge(scattered, 16 * (TT * (q - 1) + t + 1))
                    s = TT * hf + t
                    nc.scalar.activation(y[:, t, :], ps[:, DOWN + t, :], ACT.Copy, scale=weight[par][:, s:s + 1]).then_inc(y_ready, 1)

            def expert(e, par, first=False, last=False):
                q = HALVES * e
                half(e, q, 0, par, [] if first else [(e, FM + i) for i in range(FM // 2)])
                half(e, q + 1, 1, par, [] if last else [(e + 1, i) for i in range(FM)], last=last)

            for u in range(UNITS):
                split_hi(0, u)
            act.wait_ge(shifted, 1)
            nc.scalar.activation(tmp[:, :, :], tmp[:, :, :], ACT.Exp).then_inc(expd, 1)
            xgt_hi_part(0)
            expert(0, 0, first=True)
            expert(1, 1)
            with act.Fori(1, E // 2 - 1) as i:
                expert(2 * i, 0)
                expert(2 * i + 1, 1)
            expert(E - 2, 0)
            expert(E - 1, 1, last=True)

        @block.tensor
        def _(pe):
            def columns(out, lhs, mask_):
                return nc.tensor.matmul(out, lhs[:, :], mask_[:, :, :].rearrange("p e t -> p (e t)"), start=True, stop=True)

            pe.wait_ge(consts2, 12)
            with pe.Fori(0, 33) as i:
                pe.wait_ge(mask_ready, i + 1)
                columns(ps[:, 0, :], ones_b, mask).then_inc(count_mm, 1)
            pe.wait_ge(eq_ready, 1)
            columns(ps[:, 1, :], below_b, eq).then_inc(tie_mm, 1)
            columns(ps[:, 2, :], ones_b, eq).then_inc(tie_mm, 1)
            pe.wait_ge(sel_ready, 1)
            columns(ps[:, 1, :], below_b, mask).then_inc(pos_mm, 1)
            columns(ps[:, 2, :], ones_b, mask).then_inc(pos_mm, 1)
            pe.wait_ge(part_ready, 1)
            nc.tensor.matmul(ps[:, 3, 0:E], ones_f[:, :], part[:, :], start=True, stop=True).then_inc(total_mm, 1)

            def compact(e):
                for g in range(NT // HG):
                    pe.wait_ge(hot_ready, (NT // HG) * e + g + 1)
                    for t in range(HG):
                        n = HG * g + t
                        i = nc.tensor.matmul(ps[:, 0, 0:5 * NS], hot_b[:, 0, t, :],
                                             hot_v[:, n, :, :].rearrange("p v a -> p (v a)"), start=(n == 0), stop=(n == NT - 1))
                    i.then_inc(hot_mm, 1)

            def xgt(q):
                pe.wait_ge(xg_in, 16 * TT * (q + 1))
                if not isinstance(q, int) or q >= 1:
                    pe.wait_ge(hm_ready, FM * q)
                for k in range(KC):
                    for t in range(TT):
                        i = nc.tensor.transpose(ps[:, k, P * t:P * (t + 1)], xg[:, t, P * k:P * (k + 1)], ident2[:, :])
                    i.then_inc(xgt_mm, 1)

            def up(q, e, first_half):
                pe.wait_ge(xgt_ready, KC * (q + 1))
                for m in range(FM):
                    if first_half:
                        pe.wait_ge(w_ready, UNITS * e + m + 1)
                    if m >= 2:
                        pe.wait_ge(hm_ready, FM * q + m - 1)
                    elif m == 0 and not first_half:
                        pe.wait_ge(got_ready, e + 2)
                    for j, s in ((0, up1_mm), (1, up3_mm)):
                        for k in range(KC):
                            i = split3(nc, ps[:, 2 * (m % 2) + j, :], w13_hi[:, m, j, k, :], w13_lo[:, m, j, k, :],
                                       xgt_hi[:, k, :], xgt_lo[:, k, :], k == 0, k == KC - 1)
                        i.then_inc(s, 1)

            def down(q, e, first_half):
                if not isinstance(q, int) or q >= 1:
                    pe.wait_ge(y_ready, TT * q)
                for k in range(FM):
                    pe.wait_ge(h_ready, FM * q + k + 1)
                    if first_half and k % 2 == 0:
                        pe.wait_ge(w_ready, UNITS * e + FM + k // 2 + 1)
                    for t in range(TT):
                        sl = slice(P * t, P * (t + 1))
                        i = split3(nc, ps[:, DOWN + t, :], h_hi[:, k, sl], h_lo[:, k, sl], w2_hi[:, k, :], w2_lo[:, k, :],
                                   k == 0, k == FM - 1)
                        if k == FM - 1:
                            i.then_inc(y_mm, 1)
                    if k < FM - 1:
                        i.then_inc(down_mm, 1)

            def expert(e, last=False):
                q = HALVES * e
                up(q, e, True)
                xgt(q + 1)
                if not last:
                    pe.wait_ge(xgt_ready, KC * (q + 1) + 1)
                    compact(e + 1)
                down(q, e, True)
                up(q + 1, e, last)
                if not last:
                    xgt(q + 2)
                down(q + 1, e, False)

            compact(0)
            pe.wait_ge(got_ready, 1)
            xgt(0)
            expert(0)
            with pe.Fori(1, E - 1) as e:
                expert(e)
            expert(E - 1, last=True)

        @block.vector
        def _(dve):
            v = nc.vector

            def over_tiles(a):
                return a.unsqueeze(2).to_broadcast([P, E, NT])

            steps = [0]

            def then(i):
                steps[0] += 1
                i.then_inc(step_done, 1)
                dve.wait_ge(step_done, steps[0])

            def split_lo(e, u):
                n = UNITS * e + u
                dve.wait_ge(w_hi_ready, n + 1)
                hi, lo = unit_views(u)
                v.tensor_tensor(lo, raw[:, u % 2, :], hi.bitcast(F32), ALU.subtract).then_inc(w_ready, 1)

            for u in range(UNITS):
                split_lo(0, u)

            v.tensor_reduce(part[:, :], scores[:, :, :], AX.X, ALU.max).then_inc(top_part, 1)
            dve.wait_ge(consts2, 12)

            CHAIN = 9

            def key_to_float(i):
                v.tensor_scalar(flip[:, :], cand[:, :], 31, 0x7FFFFFFF, ALU.arith_shift_right, ALU.bitwise_and).then_inc(step_done, 1)
                dve.wait_ge(step_done, i + 1)
                v.tensor_tensor(thr[:, :], cand[:, :], flip[:, :], ALU.bitwise_xor).then_inc(step_done, 1)
                dve.wait_ge(step_done, i + 2)
                v.tensor_scalar(thr[:, :], thr[:, :], -1, None, ALU.bitwise_xor).then_inc(step_done, 1)
                dve.wait_ge(step_done, i + 3)

            with dve.Fori(0, 32) as i:
                b = i * CHAIN
                v.tensor_tensor(cand[:, :], one_i[:, :], shift[:, :], ALU.logical_shift_left).then_inc(step_done, 1)
                dve.wait_ge(step_done, b + 1)
                v.tensor_tensor(cand[:, :], cand[:, :], key[:, :], ALU.bitwise_or).then_inc(step_done, 1)
                dve.wait_ge(step_done, b + 2)
                key_to_float(b + 2)
                v.tensor_tensor(mask[:, :, :], scores[:, :, :], over_tiles(thr[:, :].bitcast(F32)), ALU.is_ge).then_inc(mask_ready, 1)
                dve.wait_ge(count_mm, i + 1)
                v.tensor_reduce(count[:, :], ps[:, 0, :].rearrange("p (e t) -> p e t", e=E), AX.X, ALU.add).then_inc(step_done, 1)
                dve.wait_ge(step_done, b + 6)
                v.tensor_scalar(cand[:, :], count[:, :], float(CAP), None, ALU.is_ge).then_inc(step_done, 1)
                dve.wait_ge(step_done, b + 7)
                v.tensor_tensor(cand[:, :], cand[:, :], shift[:, :], ALU.logical_shift_left).then_inc(step_done, 1)
                dve.wait_ge(step_done, b + 8)
                v.tensor_scalar(shift[:, :], shift[:, :], -1, None, ALU.add)
                v.tensor_tensor(key[:, :], key[:, :], cand[:, :], ALU.bitwise_or).then_inc(step_done, 1)
                dve.wait_ge(step_done, b + 9)
            steps[0] = 32 * CHAIN
            then(v.tensor_copy(cand[:, :], key[:, :]))
            key_to_float(steps[0])
            steps[0] += 3

            thr_f = over_tiles(thr[:, :].bitcast(F32))
            v.tensor_tensor(mask[:, :, :], scores[:, :, :], thr_f, ALU.is_gt).then_inc(mask_ready, 1)
            v.tensor_tensor(eq[:, :, :], scores[:, :, :], thr_f, ALU.is_equal).then_inc(eq_ready, 1)
            dve.wait_ge(count_mm, 33)
            then(v.tensor_reduce(count[:, :], ps[:, 0, :].rearrange("p (e t) -> p e t", e=E), AX.X, ALU.add))
            then(v.tensor_scalar(room[:, :], count[:, :], -1.0, float(CAP), ALU.mult, ALU.add))

            def ranks(mm):
                dve.wait_ge(mm, 2)
                then(v.memset(tmp[:, :, :], 0.0))
                then(v.tensor_copy(tmp[:, :, 1:NT], ps[:, 2, :].rearrange("p (e t) -> p e t", e=E)[:, :, 0:NT - 1]))
                then(v.tensor_tensor_scan(tmp[:, :, :].rearrange("p e t -> p (e t)"), carry[:, :, :].rearrange("p e t -> p (e t)"),
                                          tmp[:, :, :].rearrange("p e t -> p (e t)"), 0.0, ALU.mult, ALU.add))
                then(v.tensor_tensor(tmp[:, :, :], ps[:, 1, :].rearrange("p (e t) -> p e t", e=E), tmp[:, :, :], ALU.add))

            then(v.memset(carry[:, :, :], 1.0))
            then(v.memset(carry[:, :, 0:1], 0.0))
            ranks(tie_mm)
            then(v.tensor_tensor(tmp[:, :, :], tmp[:, :, :], over_tiles(room[:, :]), ALU.is_lt))
            then(v.tensor_tensor(tmp[:, :, :], tmp[:, :, :], eq[:, :, :], ALU.mult))
            v.tensor_tensor(mask[:, :, :], mask[:, :, :], tmp[:, :, :], ALU.add).then_inc(sel_ready, 1)
            ranks(pos_mm)
            then(v.tensor_scalar(tmp[:, :, :], tmp[:, :, :], float(N), None, ALU.subtract))
            then(v.tensor_tensor(tmp[:, :, :], tmp[:, :, :], mask[:, :, :], ALU.mult))
            then(v.tensor_scalar(tmp[:, :, :], tmp[:, :, :], float(N), None, ALU.add))
            then(v.tensor_copy(pos_i[:, :, :], tmp[:, :, :]))
            tmp_i = tmp[:, :, :].bitcast(I32)
            then(v.tensor_scalar(tmp_i, pos_i[:, :, :], P - 1, None, ALU.bitwise_and))
            then(v.tensor_copy(slot_b[:, :, :], tmp_i))
            then(v.tensor_scalar(tmp_i, pos_i[:, :, :], 7, None, ALU.logical_shift_right))
            then(v.tensor_copy(slot_a[:, :, :], tmp_i))

            dve.wait_ge(top_all, 1)
            v.tensor_tensor(tmp[:, :, :], scores[:, :, :], over_tiles(top[:, :]), ALU.subtract).then_inc(shifted, 1)
            dve.wait_ge(expd, 1)
            then(v.tensor_tensor(tmp[:, :, :], tmp[:, :, :], mask[:, :, :], ALU.mult))
            v.tensor_reduce(part[:, :], tmp[:, :, :], AX.X, ALU.add).then_inc(part_ready, 1)
            dve.wait_ge(total_mm, 1)
            then(v.tensor_copy(total[:, :], ps[:, 3, 0:E]))
            then(v.reciprocal(rtotal[:, :], total[:, :]))
            then(v.tensor_tensor(tmp[:, :, :], tmp[:, :, :], over_tiles(rtotal[:, :]), ALU.mult))
            then(v.tensor_copy(vals[:, :, :, 2], tmp[:, :, :]))
            then(v.tensor_tensor(tmp[:, :, :], tmp[:, :, :], vals[:, :, :, 2], ALU.subtract))
            then(v.tensor_copy(vals[:, :, :, 3], tmp[:, :, :]))
            then(v.tensor_tensor(tmp[:, :, :], tmp[:, :, :], vals[:, :, :, 3], ALU.subtract))
            then(v.tensor_copy(vals[:, :, :, 4], tmp[:, :, :]))
            then(v.memset(vals[:, :, :, 0], 1.0))
            then(v.tensor_scalar(vals[:, :, :, 0], vals[:, :, :, 0], iota_p[:, 0:1], None, ALU.mult))
            then(v.tensor_copy(vals[:, :, :, 1], iota_t[:, :].unsqueeze(1).to_broadcast([P, E, NT])))
            base = steps[0]
            PER = 6

            def compact(e, par):
                b = base + e * PER
                dve.wait_ge(hot_mm, (NT // HG) * e) if not isinstance(e, int) or e >= 1 else None
                v.tensor_tensor(hot_a[:, :, :], slot_a[:, bass.ds(e, 1), :].rearrange("p o t -> p (o t)").unsqueeze(2).to_broadcast([P, NT, NS]),
                                iota_8[:, :].unsqueeze(1).to_broadcast([P, NT, NS]), ALU.is_equal).then_inc(step_done, 1)
                dve.wait_ge(step_done, b + 1)
                for j in range(5):
                    v.tensor_tensor(hot_v[:, :, j, :], hot_a[:, :, :],
                                    vals[:, bass.ds(e, 1), :, j].rearrange("p o t -> p (o t)").unsqueeze(2).to_broadcast([P, NT, NS]),
                                    ALU.mult)
                for g in range(NT // HG):
                    if not isinstance(e, int) or e >= 1 or g >= 1:
                        dve.wait_ge(hot_mm, (NT // HG) * e + g)
                    v.tensor_tensor(hot_b[:, 0, :, :],
                                    slot_b[:, bass.ds(e, 1), HG * g:HG * (g + 1)].rearrange("p o t -> p (o t)").unsqueeze(2).to_broadcast([P, HG, P]),
                                    iota_b[:, :].unsqueeze(1).to_broadcast([P, HG, P]), ALU.is_equal).then_inc(hot_ready, 1)
                dve.wait_ge(hot_mm, (NT // HG) * (e + 1))
                v.tensor_copy(got[:, :, :].rearrange("p v a -> p (v a)"), ps[:, 0, 0:5 * NS]).then_inc(got_ready, 1)
                dve.wait_ge(got_ready, e + 1)
                if not isinstance(e, int) or e >= 2:
                    dve.wait_ge(scattered, 16 * TT * HALVES * (e - 1))
                v.scalar_tensor_tensor(idx_f[:, :], got[:, 1, :], float(P), got[:, 0, :], ALU.mult, ALU.add).then_inc(step_done, 1)
                dve.wait_ge(step_done, b + 2)
                v.tensor_copy(idx[par][:, :], idx_f[:, :]).then_inc(step_done, 1)
                v.tensor_tensor(got[:, 2, :], got[:, 2, :], got[:, 3, :], ALU.add).then_inc(step_done, 1)
                dve.wait_ge(step_done, b + 4)
                v.tensor_tensor(weight[par][:, :], got[:, 2, :], got[:, 4, :], ALU.add).then_inc(step_done, 1)
                dve.wait_ge(step_done, b + 5)
                v.tensor_copy(idx_f[:, :], weight[par][:, :]).then_inc(step_done, 1)
                dve.wait_ge(step_done, b + 6)
                v.tensor_copy(idx_f[:, :], idx_f[:, :]).then_inc(idx_ready, 1)

            def xgt_lo_part(q):
                for k in range(KC):
                    dve.wait_ge(xgt_hi_ready, KC * q + k + 1)
                    v.tensor_tensor(xgt_lo[:, k, :], ps[:, k, :], xgt_hi[:, k, :].bitcast(F32), ALU.subtract).then_inc(xgt_ready, 1)

            def half(q, splits):
                def lo(m):
                    n = FM * q + m
                    dve.wait_ge(h_hi_ready, n + 1)
                    v.tensor_tensor(h_lo[:, m, :], hm[:, m % 2, :], h_hi[:, m, :].bitcast(F32), ALU.subtract).then_inc(h_ready, 1)

                for m in range(FM):
                    n = FM * q + m
                    dve.wait_ge(silu_ready, n + 1)
                    dve.wait_ge(up3_mm, n + 1)
                    v.tensor_tensor(hm[:, m % 2, :], ps[:, 2 * (m % 2) + 1, :], silu[:, m % 2, :], ALU.mult).then_inc(hm_ready, 1)
                    lo(m)
                    if m < len(splits):
                        split_lo(*splits[m])

            def expert(e, par, first=False, last=False):
                q = HALVES * e
                half(q, [] if first else [(e, FM + i) for i in range(FM // 2)])
                xgt_lo_part(q + 1)
                if not last:
                    compact(e + 1, 1 - par)
                half(q + 1, [] if last else [(e + 1, i) for i in range(FM)])
                if not last:
                    xgt_lo_part(q + 2)

            compact(0, 0)
            xgt_lo_part(0)
            expert(0, 0, first=True)
            expert(1, 1)
            with dve.Fori(1, E // 2 - 1) as i:
                expert(2 * i, 0)
                expert(2 * i + 1, 1)
            expert(E - 2, 0)
            expert(E - 1, 1, last=True)


def build_kernel(nc, x, wqkv, wp, wg, rel, qkb, vb, pb, w13, w2, out):
    ctx = ExitStack()
    with ctx:
        scores = ctx.enter_context(nc.sbuf_tensor("scores", [P, E, NT], F32))
        xn = nc.dram_tensor("xn_rows", [N, C], F32, kind="Internal").ap()
        rows = "(c t p) n -> c p t n"
        d = {"x": x.rearrange(rows, t=TT, p=P), "out": out.rearrange(rows, t=TT, p=P),
             "xn": xn.rearrange(rows, t=TT, p=P), "wqkv": wqkv, "wp": wp, "wg": wg, "rel": rel,
             "qkb": qkb, "vb": vb, "pb": pb}
        attention_block(nc, d, {"scores": scores})
        expert_block(nc, {"xn": xn, "out": out, "w13": w13, "w2": w2}, scores)


def kernel(L0_attn_x, L0_attn_qkv_w, L0_attn_qkv_b, L0_attn_proj_w, L0_attn_proj_b, L0_attn_rel_bias,
           L0_ffn_Wg, L0_ffn_W1, L0_ffn_W2, L0_ffn_W3):
    import numpy as np
    import concourse.bacc as bacc
    from concourse.bass_utils import run_bass_kernel_spmd

    def rows(w):
        return np.ascontiguousarray(np.asarray(w).reshape(KC, P, -1).transpose(1, 0, 2))

    x = np.asarray(L0_attn_x)
    qkv_b = np.asarray(L0_attn_qkv_b)
    dist = np.arange(W)[:, None] - np.arange(W)[None, :] + W - 1
    rel = np.asarray(L0_attn_rel_bias)[dist].transpose(0, 2, 1)
    w13 = np.stack([np.asarray(L0_ffn_W1), np.asarray(L0_ffn_W3)], 1)
    w13 = w13.reshape(E, 2, FM, P, KC, P).transpose(0, 2, 5, 1, 4, 3)
    w2 = np.asarray(L0_ffn_W2).reshape(E, C, FM // 2, 2, P).transpose(0, 2, 4, 3, 1)
    arrays = {
        "x": x.reshape(N, C),
        "wqkv": rows(L0_attn_qkv_w).reshape(P, -1),
        "wp": rows(L0_attn_proj_w).reshape(P, -1),
        "wg": rows(np.asarray(L0_ffn_Wg).T),
        "rel": np.concatenate([rel, rel], 0),
        "qkb": qkv_b[:2 * C].reshape(2 * G, P).T,
        "vb": np.broadcast_to(qkv_b[2 * C:], (P, C)),
        "pb": np.broadcast_to(np.asarray(L0_attn_proj_b), (P, C)),
        "w13": w13.reshape(E, FM, P, 2 * KC * P),
        "w2": w2.reshape(E, FM // 2, P, 2 * C),
    }
    nc = bacc.Bacc("TRN2", target_bir_lowering=False, num_devices=1)
    arrays = {f"in_{name}": np.ascontiguousarray(a) for name, a in arrays.items()}
    args = [nc.dram_tensor(name, a.shape, mybir.dt.from_np(a.dtype), kind="ExternalInput").ap()
            for name, a in arrays.items()]
    args.append(nc.dram_tensor("out_rows", (N, C), F32, kind="ExternalOutput").ap())
    build_kernel(nc, *args)
    result = run_bass_kernel_spmd(nc, [arrays], core_ids=[0])
    return result.results[0]["out_rows"].reshape(x.shape)
```

```python
from contextlib import ExitStack

import concourse.bass as bass
from concourse import mybir
from concourse.alu_op_type import AluOpType as ALU

ACT = mybir.ActivationFunctionType
AX = mybir.AxisListType
F32 = mybir.dt.float32
F32R = mybir.dt.float32r
BF16 = mybir.dt.bfloat16
I32 = mybir.dt.int32
U32 = mybir.dt.uint32

P = 128
N = 8192
C = 512
KC = C // P
T = 512
NCH = N // T
TT = T // P
W = 64
HD = 32
H = C // HD
G = 4
E = 8
F = 1024
FM = F // P
CAP = N // E
NT = N // P
NS = CAP // P
HG = 16
GROUPS = NT // HG
SCALE = HD ** -0.5
EPS = 1e-5


def split3(nc, out, w_hi, w_lo, x_hi, x_lo, start, stop):
    nc.tensor.matmul(out, w_hi, x_hi, start=start, stop=False)
    nc.tensor.matmul(out, w_hi, x_lo, start=False, stop=False)
    return nc.tensor.matmul(out, w_lo, x_hi, start=False, stop=stop)


class Lists:

    def __init__(self, nc, ctx):
        def sb(name, shape, dt=F32):
            return ctx.enter_context(nc.sbuf_tensor(name, shape, dt))

        def sem(name):
            return ctx.enter_context(nc.semaphore(name))

        self.slot_a, self.slot_b = sb("slot_a", [P, E, NT], BF16), sb("slot_b", [P, E, NT], BF16)
        self.wgt, self.wgt_parts = sb("wgt", [P, E, NT]), sb("wgt_parts", [P, E, NT, 3], BF16)
        self.ident = sb("ident", [P, P])
        self.iota_b, self.iota_a = sb("iota_b", [P, P], BF16), sb("iota_a", [P, NS], BF16)
        self.iota_p, self.iota_t = sb("iota_p", [P, 1]), sb("iota_t", [P, NT], BF16)
        self.hot_a, self.hot_v = sb("hot_a", [P, NT, NS], BF16), sb("hot_v", [P, NT, 5, NS], BF16)
        self.got, self.idx_f = sb("got", [P, 5, NS]), sb("idx_f", [P, NS])
        self.idx = [sb(f"idx_{i}", [P, NS], U32) for i in range(2)]
        self.weight = [sb(f"weight_{i}", [P, NS]) for i in range(2)]
        self.x_in, self.x_res, self.xn = (sb(n, [P, TT, C]) for n in ("x_in", "x_res", "xn"))
        self.hot_b = self.xn[:, 0:2, :].bitcast(BF16).rearrange("p a (t b) -> p (a t) b", b=P)
        self.list_step = sem("list_step")
        self.hot_ready, self.hot_mm, self.got_ready, self.idx_ready = (sem(n) for n in (
            "hot_ready", "hot_mm", "got_ready", "idx_ready"))
        self.xg_in, self.out_stored = sem("xg_in"), sem("out_stored")


STEPS = 4


def slots_one_hot_a(nc, dve, k, e):
    v = nc.vector
    if not isinstance(e, int) or e >= 1:
        dve.wait_ge(k.hot_mm, GROUPS * e)

    def column(a):
        return a.rearrange("p o t -> p (o t)").unsqueeze(2).to_broadcast([P, NT, NS])

    v.tensor_tensor(k.hot_a[:, :, :], column(k.slot_a[:, bass.ds(e, 1), :]),
                    k.iota_a[:, :].unsqueeze(1).to_broadcast([P, NT, NS]), ALU.is_equal).then_inc(k.list_step, 1)
    dve.wait_ge(k.list_step, STEPS * e + 1)
    v.tensor_scalar(k.hot_v[:, :, 0, :], k.hot_a[:, :, :], k.iota_p[:, 0:1], None, ALU.mult)
    v.tensor_tensor(k.hot_v[:, :, 1, :], k.hot_a[:, :, :], k.iota_t[:, :].unsqueeze(2).to_broadcast([P, NT, NS]), ALU.mult)
    for j in range(3):
        v.tensor_tensor(k.hot_v[:, :, 2 + j, :], k.hot_a[:, :, :], column(k.wgt_parts[:, bass.ds(e, 1), :, j]), ALU.mult)


def slots_one_hot_b(nc, dve, k, e, g):
    if not isinstance(e, int) or e >= 1 or g >= 1:
        dve.wait_ge(k.hot_mm, GROUPS * e + g)
    nc.vector.tensor_tensor(k.hot_b[:, :, :],
                            k.slot_b[:, bass.ds(e, 1), HG * g:HG * (g + 1)].rearrange("p o t -> p (o t)").unsqueeze(2).to_broadcast([P, HG, P]),
                            k.iota_b[:, :].unsqueeze(1).to_broadcast([P, HG, P]), ALU.is_equal).then_inc(k.hot_ready, 1)


def compact(nc, pe, k, bank, e, g):
    pe.wait_ge(k.hot_ready, GROUPS * e + g + 1)
    for t in range(HG):
        n = HG * g + t
        i = nc.tensor.matmul(bank[:, 0:5 * NS], k.hot_b[:, t, :], k.hot_v[:, n, :, :].rearrange("p v a -> p (v a)"),
                             start=(n == 0), stop=(n == NT - 1))
    i.then_inc(k.hot_mm, 1)


def expert_list(nc, dve, k, bank, e, par, scattered=None):
    v = nc.vector
    dve.wait_ge(k.hot_mm, GROUPS * (e + 1))
    v.tensor_copy(k.got[:, :, :].rearrange("p v a -> p (v a)"), bank[:, 0:5 * NS]).then_inc(k.got_ready, 1)
    dve.wait_ge(k.got_ready, e + 1)
    if not isinstance(e, int) or e >= 2:
        dve.wait_ge(scattered, 16 * TT * 2 * (e - 1))
    v.scalar_tensor_tensor(k.idx_f[:, :], k.got[:, 1, :], float(P), k.got[:, 0, :], ALU.mult, ALU.add).then_inc(k.list_step, 1)
    v.tensor_tensor(k.got[:, 2, :], k.got[:, 2, :], k.got[:, 3, :], ALU.add).then_inc(k.list_step, 1)
    dve.wait_ge(k.list_step, STEPS * e + 3)
    v.tensor_copy(k.idx[par][:, :], k.idx_f[:, :]).then_inc(k.idx_ready, 1)
    v.tensor_tensor(k.weight[par][:, :], k.got[:, 2, :], k.got[:, 4, :], ALU.add).then_inc(k.list_step, 1)


def gather(nc, pool, k, xn_rows, par, tile0):
    pool.nop(nofuse=True)
    for t in range(TT):
        nc.gpsimd.indirect_dma_start(
            out=k.x_in[:, t, :], out_offset=None, in_=xn_rows,
            in_offset=bass.IndirectOffsetOnAxis(ap=k.idx[par][:, tile0 + t:tile0 + t + 1], axis=0)).then_inc(k.xg_in, 16)


def attention_block(nc, d, lists):
    ctx = ExitStack()
    with ctx:
        def sb(name, shape, dt=F32):
            return ctx.enter_context(nc.sbuf_tensor(name, shape, dt))

        def sem(name):
            return ctx.enter_context(nc.semaphore(name))

        wqk_hi, wqk_lo = sb("wqk_hi", [P, 2 * G, KC, P], F32R), sb("wqk_lo", [P, 2 * G, KC, P], F32R)
        wv_hi, wv_lo = sb("wv_hi", [P, KC, C], F32R), sb("wv_lo", [P, KC, C], F32R)
        wp_hi, wp_lo = sb("wp_hi", [P, KC, C], F32R), sb("wp_lo", [P, KC, C], F32R)
        wg_hi, wg_lo = sb("wg_hi", [P, KC, P], F32R), sb("wg_lo", [P, KC, P], F32R)
        rel = sb("rel", [P, H, W])
        qk_bias, v_bias, p_bias = sb("qk_bias", [P, 2 * G]), sb("v_bias", [P, C]), sb("p_bias", [P, C])
        ident, x_in, x_res, xn = lists.ident, lists.x_in, lists.x_res, lists.xn
        stats, mv = sb("stats", [P, TT, 6]), sb("mv", [P, TT, 2])
        veps, rstd, power = sb("veps", [P, TT]), sb("rstd", [P, TT]), sb("power", [P, TT])
        xt_hi, xt_lo = sb("xt_hi", [P, KC, T], F32R), sb("xt_lo", [P, KC, T], F32R)
        q_sb = sb("q_sb", [P, T])
        k_diag = sb("k_diag", [P, T // W, G, W])
        v_sb = sb("v_sb", [P, TT, 2, C // 2])
        s_sb = sb("s_sb", [P, TT, 4, W])
        p_sb = sb("p_sb", [P, TT, 4, W])
        pn_sb = sb("pn_sb", [P, TT, 4, W])
        pt_sb = sb("pt_sb", [P, TT, 2, P])
        s_max, s_sum, s_rec = sb("s_max", [P, 16]), sb("s_sum", [P, 16]), sb("s_rec", [P, 16])
        ot_hi, ot_lo = sb("ot_hi", [P, G, T], F32R), sb("ot_lo", [P, G, T], F32R)
        g_sb = sb("g_sb", [E, T])
        gate_s, above, ties, upto, pos, exps = (sb(n, [P, T]) for n in ("gate_s", "above", "ties", "upto", "pos", "exps"))
        hits = sb("hits", [P, 3, T], BF16)
        ones_row = sb("ones_row", [P, T])
        same, earlier = sb("same", [P, P]), sb("earlier", [P, P])
        top, top_e, top_row, one = sb("top", [P, 1]), sb("top_e", [1, E]), sb("top_row", [1, P]), sb("one", [1, 1])
        pattern, cand, flip, thr = (sb(n, [P, 3], I32) for n in ("pattern", "cand", "flip", "thr"))
        key, kept_i, kept, reach = sb("key", [P, 1], I32), sb("kept_i", [P, 1], I32), sb("kept", [P, 1]), sb("reach", [P, 3])
        cnt, room, esum = sb("cnt", [P, 3]), sb("room", [P, 2]), sb("esum", [P, 1])
        pos_i, part_i = sb("pos_i", [P, T], I32), sb("part_i", [P, T], I32)
        RAW = [x_res[:, 0:2, :].rearrange("p a b -> p (a b)"), x_res[:, 2:4, :].rearrange("p a b -> p (a b)"),
               pn_sb[:, :, :, :].rearrange("p t h k -> p (t h k)")]
        ps = ctx.enter_context(nc.psum_tensor("ps", [P, 8, 512], F32))
        QB, KB, SP, OT = 0, 1, 2, 4
        V_BANK, P_BANK, X_BANK, G_BANK = (5, 6, 7, 5), (6, 7, 5, 6), (7, 5, 6, QB), 5
        LAST_BANK = (6, 7, 6, 7)
        SEARCH, TOTAL, POS_T, WGT_T = 5, 6, KB, QB
        s_bank = ps[:, SP:SP + 2, :].rearrange("p b (t h k) -> p (b t) h k", t=2, h=4)

        const_in = sem("const_in")
        raw_in = [sem(f"raw_in_{i}") for i in range(3)]
        raw_hi, raw_lo = sem("raw_hi"), sem("raw_lo")
        consts = sem("consts")
        x_loaded, xn_ready, xn_stored = sem("x_loaded"), sem("xn_ready"), sem("xn_stored")
        stat_ready, mv_ready, veps_ready, rstd_ready = sem("stat_ready"), sem("mv_ready"), sem("veps_ready"), sem("rstd_ready")
        xt_mm, xt_hi_ready, xt_ready = sem("xt_mm"), sem("xt_hi_ready"), sem("xt_ready")
        gate_mm, gate_sb_ready, gate_stored, scores_in = sem("gate_mm"), sem("gate_sb_ready"), sem("gate_stored"), sem("scores_in")
        top_rows, top_t_mm, top_row_ready, top_mm, top_ready = (sem(n) for n in (
            "top_rows", "top_t_mm", "top_row_ready", "top_mm", "top_ready"))
        exps_ready, select_step, part_counts, count_mm, gt_eq_ready, room_mm = (sem(n) for n in (
            "exps_ready", "select_step", "part_counts", "count_mm", "gt_eq_ready", "room_mm"))
        chosen_ready, base_mm, total_part, total_mm, pos_ready, wgt_ready, pos_t_mm, wgt_t_mm = (sem(n) for n in (
            "chosen_ready", "base_mm", "total_part", "total_mm", "pos_ready", "wgt_ready", "pos_t_mm", "wgt_t_mm"))
        q_mm, k_mm, q_ready = sem("q_mm"), sem("k_mm"), sem("q_ready")
        ka_ready, kb_ready = sem("ka_ready"), sem("kb_ready")
        v_mm, v_ready = sem("v_mm"), sem("v_ready")
        s_mm, s_ready, max_ready, sub_ready = sem("s_mm"), sem("s_ready"), sem("max_ready"), sem("sub_ready")
        exp_ready, sum_ready, rec_ready, norm_ready = sem("exp_ready"), sem("sum_ready"), sem("rec_ready"), sem("norm_ready")
        pt_mm, pta_ready, ptb_ready = sem("pt_mm"), sem("pta_ready"), sem("ptb_ready")
        o_mm, o_hi_ready, o_ready = sem("o_mm"), sem("o_hi_ready"), sem("o_ready")
        p_mm, out_ready, out_stored = sem("p_mm"), sem("out_ready"), lists.out_stored
        res_loaded, res_ready = sem("res_loaded"), sem("res_ready")

        def raw_units():
            wqk, wv, wp, wg = ([w[...].rearrange(r) for w in ws] for ws, r in (
                ((wqk_hi, wqk_lo), "p g a b -> p (g a b)"), ((wv_hi, wv_lo), "p a b -> p (a b)"),
                ((wp_hi, wp_lo), "p a b -> p (a b)"), ((wg_hi, wg_lo), "p a b -> p (a b)")))
            order = [(wg, d["wg"], 0), (wqk, d["wqk"], 0), (wqk, d["wqk"], 1), (wv, d["wv"], 0), (wv, d["wv"], 1),
                     (wqk, d["wqk"], 2), (wqk, d["wqk"], 3), (wp, d["wp"], 0), (wp, d["wp"], 1)]
            for (hi, lo), src, u in order:
                c0 = slice(1024 * u, min(1024 * (u + 1), src.shape[1]))
                yield src[:, c0], hi[:, c0], lo[:, c0], c0.stop - c0.start

        units = list(raw_units())
        GATE_SPLIT, Q0_SPLIT, V_SPLIT, ALL_SPLIT = 1, 2, 5, len(units)

        block = ctx.enter_context(nc.Block())

        @block.sync
        def _(sp):
            sp.dma_start(x_in[:, :, :], d["x"][0]).then_inc(x_loaded, 16)
            for u, (src, _, _, n) in enumerate(units):
                if u == 1:
                    for dst, const in ((rel[:, :, :], d["rel"]), (qk_bias[:, :], d["qkb"]),
                                       (v_bias[:, :], d["vb"]), (p_bias[:, :], d["pb"]),
                                       (same[:, :], d["same"]), (earlier[:, :], d["earlier"])):
                        sp.dma_start(dst, const).then_inc(const_in, 16)
                if u >= 3:
                    sp.wait_ge(raw_lo, u - 2)
                sp.dma_start(RAW[u % 3][:, 0:n], src).then_inc(raw_in[u % 3], 16)

            def keep_xn(c):
                sp.wait_ge(xn_ready, TT * (c + 1))
                sp.dma_start(d["xn"][c], xn[:, :, :]).then_inc(xn_stored, 16)

            def keep_scores(c):
                sp.wait_ge(gate_sb_ready, c + 1)
                sp.dma_start(d["gate"][bass.ds(E * c, E), :], g_sb[:, :]).then_inc(gate_stored, 16)

            def load_x(c):
                sp.dma_start(x_in[:, :, :], d["x"][c]).then_inc(x_loaded, 16)

            def store_out(c):
                sp.wait_ge(out_ready, TT * (c + 1))
                sp.dma_start(d["out"][c], x_res[:, :, :]).then_inc(out_stored, 16)
                if not isinstance(c, int) or c < NCH - 1:
                    sp.wait_ge(out_stored, 16 * (c + 1))

            def load_res(c):
                sp.dma_start(x_res[:, :, :], d["x"][c]).then_inc(res_loaded, 16)

            keep_xn(0)
            load_x(1)
            sp.wait_ge(raw_lo, ALL_SPLIT)
            load_res(0)
            keep_scores(0)
            keep_xn(1)
            load_x(2)
            with sp.Fori(1, NCH - 2) as c:
                keep_scores(c)
                keep_xn(c + 1)
                load_x(c + 2)
                store_out(c - 1)
                load_res(c)
            keep_scores(NCH - 2)
            keep_xn(NCH - 1)
            store_out(NCH - 3)
            load_res(NCH - 2)
            keep_scores(NCH - 1)
            sp.wait_ge(gate_stored, 16 * NCH)
            sp.dma_start(gate_s[:, :], d["gate"]).then_inc(scores_in, 16)
            store_out(NCH - 2)
            load_res(NCH - 1)
            store_out(NCH - 1)
            sp.wait_ge(xn_stored, 16 * NCH)

        @block.gpsimd
        def _(pool):
            nc.gpsimd.memset(ident[:, :], 0.0).then_inc(consts, 1)
            nc.gpsimd.memset(power[:, :], -0.5).then_inc(consts, 1)
            nc.gpsimd.memset(k_diag[:, :, :, :], 0.0).then_inc(consts, 1)
            nc.gpsimd.memset(ones_row[:, :], 1.0).then_inc(consts, 1)
            nc.gpsimd.memset(one[:, :], 1.0).then_inc(consts, 1)
            nc.gpsimd.memset(key[:, :], 0).then_inc(consts, 1)
            for j in range(3):
                nc.gpsimd.memset(pattern[:, j:j + 1], j + 1).then_inc(consts, 1)
            wide = dict(allow_small_or_imprecise_dtypes=True)
            nc.gpsimd.iota(lists.iota_b[:, :], [[1, P]], 0, 0, **wide).then_inc(consts, 1)
            nc.gpsimd.iota(lists.iota_a[:, :], [[1, NS]], 0, 0, **wide).then_inc(consts, 1)
            nc.gpsimd.iota(lists.iota_t[:, :], [[1, NT]], 0, 0, **wide).then_inc(consts, 1)
            nc.gpsimd.iota(lists.iota_p[:, :], [[0, 1]], 0, 1, **wide).then_inc(consts, 1)
            pool.wait_ge(consts, 9)
            nc.gpsimd.affine_select(out=ident[:, :], in_=ident[:, :], compare_op=ALU.not_equal, fill=1.0,
                                    base=0, pattern=[[-1, P]], channel_multiplier=1).then_inc(consts, 1)

            def layernorm_rstd(c):
                pool.wait_ge(veps_ready, c + 1)
                nc.gpsimd.tensor_tensor(rstd[:, :], veps[:, :], power[:, :], ALU.pow).then_inc(rstd_ready, 1)

            def residual(c):
                pool.wait_ge(res_loaded, 16 * (c + 1))
                nc.gpsimd.tensor_tensor(x_res[:, :, :], x_res[:, :, :],
                                        p_bias[:, :].unsqueeze(1).to_broadcast([P, TT, C]), ALU.add).then_inc(res_ready, 1)

            def softmax(s):
                pool.wait_ge(max_ready, s + 1)
                nc.gpsimd.tensor_tensor(s_sb[:, :, :, :], s_sb[:, :, :, :],
                                        s_max[:, :].rearrange("p (t h) -> p t h", t=TT).unsqueeze(3)
                                        .to_broadcast([P, TT, 4, W]), ALU.subtract).then_inc(sub_ready, 1)
                pool.wait_ge(rec_ready, s + 1)
                if not isinstance(s, int) or s >= 1:
                    pool.wait_ge(pt_mm, 2 * s)
                nc.gpsimd.tensor_tensor(pn_sb[:, :, :, :], p_sb[:, :, :, :],
                                        s_rec[:, :].rearrange("p (t h) -> p t h", t=TT).unsqueeze(3)
                                        .to_broadcast([P, TT, 4, W]), ALU.mult).then_inc(norm_ready, 1)

            def chunk(c, first=False, last=False):
                if not first:
                    softmax(G * c - 1)
                if not last:
                    layernorm_rstd(c + 1)
                softmax(G * c)
                if not first:
                    pool.wait_ge(const_in, 96)
                    residual(c - 1)
                softmax(G * c + 1)
                softmax(G * c + 2)

            pool.wait_ge(consts, 14)
            layernorm_rstd(0)
            pool.wait_ge(raw_lo, ALL_SPLIT)
            chunk(0, first=True)
            with pool.Fori(1, NCH - 1) as c:
                chunk(c)
            chunk(NCH - 1, last=True)
            softmax(G * NCH - 1)
            residual(NCH - 1)
            pool.wait_ge(xn_ready, TT * NCH)
            pool.wait_ge(lists.idx_ready, 1)
            gather(nc, pool, lists, d["xn_rows"], 0, 0)

        @block.scalar
        def _(act):
            def split_hi(u):
                _, hi, _, n = units[u]
                act.wait_ge(raw_in[u % 3], 16 * (u // 3 + 1))
                nc.scalar.activation(hi, RAW[u % 3][:, 0:n], ACT.Copy).then_inc(raw_hi, 1)

            def xt_hi_part(c):
                for k in range(KC):
                    act.wait_ge(xt_mm, KC * c + k + 1)
                    nc.scalar.activation(xt_hi[:, k, :], ps[:, X_BANK[k], :], ACT.Copy).then_inc(xt_hi_ready, 1)

            def step(s, g, c, scores, qk, pv, next_x):
                if qk:
                    act.wait_ge(q_mm, s + 1)
                    if scores:
                        act.wait_ge(s_mm, 2 * s)
                    nc.scalar.activation(q_sb[:, :], ps[:, QB, :], ACT.Identity, bias=qk_bias[:, g:g + 1]).then_inc(q_ready, 1)
                if pv:
                    act.wait_ge(pt_mm, 2 * (s - 2) + 1)
                    if not isinstance(s, int) or s >= 3:
                        act.wait_ge(o_mm, s - 2)
                    nc.scalar.activation(pt_sb[:, 0:2, :, :].rearrange("p t h q -> p (t h q)"), ps[:, SP, :],
                                         ACT.Copy).then_inc(pta_ready, 1)
                if scores:
                    act.wait_ge(sub_ready, s)
                    nc.scalar.activation(p_sb[:, :, :, :], s_sb[:, :, :, :], ACT.Exp).then_inc(exp_ready, 1)
                if qk:
                    act.wait_ge(k_mm, s + 1)
                    for h in range(2):
                        r = slice(HD * h, HD * (h + 1))
                        i = nc.scalar.activation(k_diag[r, :, h, :], ps[r, KB, :].rearrange("p (w k) -> p w k", k=W),
                                                 ACT.Identity, bias=qk_bias[r, G + g:G + g + 1])
                    i.then_inc(ka_ready, 1)
                if next_x:
                    xt_hi_part(c + 1)
                if pv:
                    act.wait_ge(o_mm, s - 1)
                    m = (g + 2) % G
                    if m == 0 and not (isinstance(s, int) and s < 6):
                        act.wait_ge(p_mm, TT * (c if g == 2 else c + 1))
                    nc.scalar.activation(ot_hi[:, m, :], ps[:, OT, :], ACT.Copy).then_inc(o_hi_ready, 1)

            def chunk(c, first=False):
                for g in range(G):
                    s = G * c + g
                    step(s, g, c, scores=not (first and g == 0), qk=True, pv=not (first and g < 2), next_x=(g == 3))

            for u in range(V_SPLIT):
                split_hi(u)
            xt_hi_part(0)
            for u in range(V_SPLIT, ALL_SPLIT):
                split_hi(u)
            act.wait_ge(const_in, 96)
            act.wait_ge(consts, 14)
            chunk(0, first=True)
            with act.Fori(1, NCH - 1) as c:
                chunk(c)
            for g in range(G):
                step(G * (NCH - 1) + g, g, NCH - 1, scores=True, qk=True, pv=True, next_x=False)
                if g == 1:
                    act.wait_ge(top_ready, 1)
                    nc.scalar.activation(exps[:, :], gate_s[:, :], ACT.Exp, bias=top[:, 0:1]).then_inc(exps_ready, 1)
            step(G * NCH, 0, NCH, scores=True, qk=False, pv=True, next_x=False)
            step(G * NCH + 1, 1, NCH, scores=False, qk=False, pv=True, next_x=False)

        @block.tensor
        def _(pe):
            def xt(c):
                pe.wait_ge(xn_ready, TT * (c + 1))
                for k in range(KC):
                    if isinstance(c, int) and c == 1 and k == 0:
                        pe.wait_ge(v_ready, TT)
                    if k < 3 and (not isinstance(c, int) or c >= 2):
                        pe.wait_ge(out_ready, TT * (c - 2) + k + 2)
                    if k == 3 and (not isinstance(c, int) or c >= 1):
                        pe.wait_ge(q_ready, G * c)
                    for t in range(TT):
                        i = nc.tensor.transpose(ps[:, X_BANK[k], P * t:P * (t + 1)], xn[:, t, P * k:P * (k + 1)], ident[:, :])
                    i.then_inc(xt_mm, 1)

            def gate(c):
                pe.wait_ge(xt_ready, KC * (c + 1))
                for k in range(KC):
                    i = split3(nc, ps[:, G_BANK, :], wg_hi[:, k, :], wg_lo[:, k, :], xt_hi[:, k, :], xt_lo[:, k, :],
                               k == 0, k == KC - 1)
                i.then_inc(gate_mm, 1)

            def scores(s):
                pe.wait_ge(q_ready, s + 1)
                pe.wait_ge(ka_ready, s + 1)
                pe.wait_ge(kb_ready, s + 1)
                if not isinstance(s, int) or s >= 2:
                    pe.wait_ge(pta_ready, s - 1)
                    pe.wait_ge(ptb_ready, s - 1)
                for t in range(TT):
                    for j in range(4):
                        w = 2 * t + j // 2
                        i = nc.tensor.matmul(ps[32 * j:32 * (j + 1), SP + t // 2, 256 * (t % 2):256 * (t % 2 + 1)],
                                             q_sb[:, P * t + 32 * j:P * t + 32 * (j + 1)],
                                             k_diag[:, w, :, :].rearrange("p h k -> p (h k)"), start=True, stop=True)
                    if t % 2:
                        i.then_inc(s_mm, 1)

            def project_q(s, g):
                if not isinstance(s, int) or s >= 1:
                    pe.wait_ge(q_ready, s)
                for k in range(KC):
                    i = split3(nc, ps[:, QB, :], wqk_hi[:, 2 * g, k, :], wqk_lo[:, 2 * g, k, :], xt_hi[:, k, :], xt_lo[:, k, :],
                               k == 0, k == KC - 1)
                i.then_inc(q_mm, 1)

            def project_k(s, g):
                if not isinstance(s, int) or s >= 1:
                    pe.wait_ge(ka_ready, s)
                    pe.wait_ge(kb_ready, s)
                for k in range(KC):
                    i = split3(nc, ps[:, KB, :], wqk_hi[:, 2 * g + 1, k, :], wqk_lo[:, 2 * g + 1, k, :], xt_hi[:, k, :], xt_lo[:, k, :],
                               k == 0, k == KC - 1)
                i.then_inc(k_mm, 1)

            def project_v(c, t, last=False):
                bank = (LAST_BANK if last else V_BANK)[t]
                if t == 0:
                    pe.wait_ge(gate_sb_ready, c + 1)
                if last and t >= 2:
                    pe.wait_ge(v_ready, TT * c + t - 1)
                elif t == 3:
                    pe.wait_ge(v_ready, TT * c + 1)
                for k in range(KC):
                    i = split3(nc, ps[:, bank, :], xt_hi[:, k, P * t:P * (t + 1)], xt_lo[:, k, P * t:P * (t + 1)],
                               wv_hi[:, k, :], wv_lo[:, k, :], k == 0, k == KC - 1)
                i.then_inc(v_mm, 1)

            def probs_t(s):
                pe.wait_ge(norm_ready, s + 1)
                if isinstance(s, int) and s == G * NCH - 1:
                    pe.wait_ge(pta_ready, s)
                    pe.wait_ge(ptb_ready, s)
                else:
                    pe.wait_ge(s_ready, 2 * s + 4)
                for t in range(TT):
                    for hp in range(2):
                        i = nc.tensor.transpose(ps[:, SP + t // 2, 256 * (t % 2) + P * hp:256 * (t % 2) + P * (hp + 1)],
                                                pn_sb[:, t, 2 * hp:2 * hp + 2, :].rearrange("p h k -> p (h k)"), ident[:, :])
                    if t % 2:
                        i.then_inc(pt_mm, 1)

            def pv(s, m):
                pe.wait_ge(pta_ready, s + 1)
                pe.wait_ge(ptb_ready, s + 1)
                if not isinstance(s, int) or s >= 1:
                    pe.wait_ge(o_ready, s)
                pe.nop(nofuse=True)
                for t in range(TT):
                    for w in range(2):
                        for h in range(4):
                            r = slice(W * (h % 2), W * (h % 2 + 1))
                            col = HD * (2 * m + h // 2)
                            i = nc.tensor.matmul(ps[HD * h:HD * (h + 1), OT, P * t + W * w:P * t + W * (w + 1)],
                                                 v_sb[r, t, w, col:col + HD], pt_sb[r, t, h // 2, W * w:W * (w + 1)],
                                                 start=True, stop=True)
                i.then_inc(o_mm, 1)

            def project_out(c, t, last=False):
                bank = (LAST_BANK if last else P_BANK)[t]
                if t == 0:
                    pe.wait_ge(o_ready, G * (c + 1))
                    if isinstance(c, int) and c == NCH - 1:
                        pe.wait_ge(out_ready, TT * c)
                    else:
                        pe.wait_ge(v_ready, TT * (c + 2))
                elif last and t >= 2:
                    pe.wait_ge(out_ready, TT * c + t - 1)
                elif t == 3:
                    pe.wait_ge(out_ready, TT * c + 1)
                for k in range(KC):
                    i = split3(nc, ps[:, bank, :], ot_hi[:, k, P * t:P * (t + 1)], ot_lo[:, k, P * t:P * (t + 1)],
                               wp_hi[:, k, :], wp_lo[:, k, :], k == 0, k == KC - 1)
                i.then_inc(p_mm, 1)

            def chunk(c, first=False):
                s = G * c
                if not first:
                    scores(s - 1)
                gate(c)
                if first:
                    pe.wait_ge(raw_lo, Q0_SPLIT)
                project_q(s, 0)
                if not first:
                    probs_t(s - 2)
                project_k(s, 0)
                if not first:
                    pv(s - 2, 2)
                scores(s)
                project_q(s + 1, 1)
                if not first:
                    probs_t(s - 1)
                project_k(s + 1, 1)
                if not first:
                    pv(s - 1, 3)
                if first:
                    pe.wait_ge(raw_lo, ALL_SPLIT)
                for t in range(TT):
                    project_v(c, t)
                scores(s + 1)
                if not first:
                    for t in range(TT):
                        project_out(c - 1, t)
                project_q(s + 2, 2)
                probs_t(s)
                project_k(s + 2, 2)
                pe.wait_ge(v_ready, TT * (c + 1))
                pv(s, 0)
                scores(s + 2)
                project_q(s + 3, 3)
                probs_t(s + 1)
                project_k(s + 3, 3)
                xt(c + 1)
                pv(s + 1, 1)

            def row_matmul(out, lhs, rhs):
                return nc.tensor.matmul(out, lhs, rhs, start=True, stop=True)

            def count(i):
                pe.wait_ge(part_counts, i + 1)
                row_matmul(ps[:, SEARCH, 0:3], same[:, :], cnt[:, :]).then_inc(count_mm, 1)

            def last_chunk():
                c, s = NCH - 1, G * (NCH - 1)
                scores(s - 1)
                gate(c)
                project_q(s, 0)
                probs_t(s - 2)
                project_k(s, 0)
                pv(s - 2, 2)
                pe.wait_ge(top_rows, 1)
                nc.tensor.transpose(ps[0:1, SEARCH, 0:P], top[:, 0:1], ident[:, :]).then_inc(top_t_mm, 1)
                scores(s)
                project_q(s + 1, 1)
                pe.wait_ge(top_row_ready, 1)
                row_matmul(ps[:, SEARCH, 0:1], top_row[0:1, :], one[0:1, 0:1]).then_inc(top_mm, 1)
                probs_t(s - 1)
                project_k(s + 1, 1)
                count(0)
                pv(s - 1, 3)
                count(1)
                for t in range(TT):
                    project_v(c, t, last=True)
                    count(2 + t)
                scores(s + 1)
                count(6)
                for t in range(TT):
                    project_out(c - 1, t, last=True)
                    count(7 + t)
                project_q(s + 2, 2)
                count(11)
                probs_t(s)
                project_k(s + 2, 2)
                count(12)
                pe.wait_ge(v_ready, TT * (c + 1))
                pv(s, 0)
                count(13)
                scores(s + 2)
                project_q(s + 3, 3)
                count(14)
                probs_t(s + 1)
                project_k(s + 3, 3)
                count(15)
                pv(s + 1, 1)
                scores(s + 3)
                pe.wait_ge(gt_eq_ready, 2)
                row_matmul(ps[:, SEARCH, 0:1], same[:, :], cnt[:, 0:1]).then_inc(room_mm, 1)
                row_matmul(ps[:, SEARCH, 1:2], earlier[:, :], cnt[:, 1:2]).then_inc(room_mm, 1)
                probs_t(s + 2)
                pv(s + 2, 2)
                pe.wait_ge(chosen_ready, 1)
                row_matmul(ps[:, SEARCH, 2:3], earlier[:, :], cnt[:, 2:3]).then_inc(base_mm, 1)
                pe.wait_ge(ka_ready, G * NCH)
                pe.wait_ge(kb_ready, G * NCH)
                pe.wait_ge(pos_ready, 1)
                for t in range(TT):
                    i = nc.tensor.transpose(ps[:, POS_T, P * t:P * (t + 1)], pos[:, P * t:P * (t + 1)], ident[:, :])
                i.then_inc(pos_t_mm, 1)
                probs_t(s + 3)
                pe.wait_ge(total_part, 1)
                pe.wait_ge(out_ready, TT * c)
                row_matmul(ps[:, TOTAL, 0:1], same[:, :], esum[:, :]).then_inc(total_mm, 1)
                pv(s + 3, 3)
                pe.wait_ge(wgt_ready, 1)
                for t in range(TT):
                    i = nc.tensor.transpose(ps[:, WGT_T, P * t:P * (t + 1)], exps[:, P * t:P * (t + 1)], ident[:, :])
                i.then_inc(wgt_t_mm, 1)
                for t in range(TT):
                    project_out(c, t, last=True)
                    if t == 1:
                        for g in range(GROUPS):
                            compact(nc, pe, lists, ps[:, SEARCH, :], 0, g)

            pe.wait_ge(consts, 14)
            xt(0)
            pe.wait_ge(raw_lo, GATE_SPLIT)
            chunk(0, first=True)
            with pe.Fori(1, NCH - 1) as c:
                chunk(c)
            last_chunk()

        @block.vector
        def _(dve):
            def split_lo(u):
                _, hi, lo, n = units[u]
                dve.wait_ge(raw_hi, u + 1)
                nc.vector.tensor_tensor(lo, RAW[u % 3][:, 0:n], hi.bitcast(F32), ALU.subtract).then_inc(raw_lo, 1)

            def layernorm_stats(c):
                dve.wait_ge(x_loaded, 16 * (c + 1))
                for t in range(TT):
                    i = nc.vector.bn_stats(stats[:, t, :], x_in[:, t, :])
                i.then_inc(stat_ready, 1)
                dve.wait_ge(stat_ready, c + 1)
                dve.nop(nofuse=True)
                for t in range(TT):
                    i = nc.vector.bn_aggr(mv[:, t, :], stats[:, t, :])
                i.then_inc(mv_ready, 1)
                dve.wait_ge(mv_ready, c + 1)
                nc.vector.tensor_scalar(veps[:, :], mv[:, :, 1], EPS, None, ALU.add).then_inc(veps_ready, 1)

            def layernorm_apply(c):
                dve.wait_ge(rstd_ready, c + 1)
                if not isinstance(c, int) or c >= 1:
                    dve.wait_ge(xn_stored, 16 * c)
                    dve.wait_ge(xt_mm, KC * c)
                for t in range(TT):
                    nc.vector.tensor_scalar(xn[:, t, :], x_in[:, t, :], mv[:, t, 0:1], rstd[:, t:t + 1],
                                            ALU.subtract, ALU.mult).then_inc(xn_ready, 1)

            def xt_lo_part(c):
                for k in range(KC):
                    dve.wait_ge(xt_hi_ready, KC * c + k + 1)
                    nc.vector.tensor_tensor(xt_lo[:, k, :], ps[:, X_BANK[k], :], xt_hi[:, k, :].bitcast(F32),
                                            ALU.subtract).then_inc(xt_ready, 1)

            def gate_rows(c):
                dve.wait_ge(gate_mm, c + 1)
                if not isinstance(c, int) or c >= 1:
                    dve.wait_ge(gate_stored, 16 * c)
                nc.vector.tensor_copy(g_sb[:, :], ps[0:E, G_BANK, :]).then_inc(gate_sb_ready, 1)

            def scale_and_bias(s, m):
                for b in range(2):
                    dve.wait_ge(s_mm, 2 * s + b + 1)
                    if b == 0 and (not isinstance(s, int) or s >= 1):
                        dve.wait_ge(exp_ready, s)
                    nc.vector.scalar_tensor_tensor(
                        s_sb[:, 2 * b:2 * b + 2, :, :].rearrange("p t h k -> p t (h k)"),
                        ps[:, SP + b, :].rearrange("p (t n) -> p t n", t=2), SCALE,
                        rel[:, 4 * m:4 * m + 4, :].rearrange("p h k -> p (h k)").unsqueeze(1).to_broadcast([P, 2, 4 * W]),
                        ALU.mult, ALU.add).then_inc(s_ready, 1)
                dve.wait_ge(s_ready, 2 * s + 2)
                nc.vector.tensor_reduce(s_max[:, :], s_sb[:, :, :, :].rearrange("p t h k -> p (t h) k"), AX.X, ALU.max).then_inc(max_ready, 1)

            def normaliser(s):
                dve.wait_ge(exp_ready, s + 1)
                nc.vector.tensor_reduce(s_sum[:, :], p_sb[:, :, :, :].rearrange("p t h k -> p (t h) k"), AX.X, ALU.add).then_inc(sum_ready, 1)
                dve.wait_ge(sum_ready, s + 1)
                if not isinstance(s, int) or s >= 1:
                    dve.wait_ge(norm_ready, s)
                nc.vector.reciprocal(s_rec[:, :], s_sum[:, :]).then_inc(rec_ready, 1)

            def finish_rows(c, t, last=False):
                if t == 0:
                    dve.wait_ge(res_ready, c + 1)
                dve.wait_ge(p_mm, TT * c + t + 1)
                nc.vector.tensor_tensor(x_res[:, t, :], ps[:, (LAST_BANK if last else P_BANK)[t], :], x_res[:, t, :],
                                        ALU.add).then_inc(out_ready, 1)

            def probs_t_part(s):
                dve.wait_ge(pt_mm, 2 * s + 2)
                if not isinstance(s, int) or s >= 1:
                    dve.wait_ge(o_mm, s)
                nc.vector.tensor_copy(pt_sb[:, 2:4, :, :].rearrange("p t h q -> p (t h q)"), ps[:, SP + 1, :]).then_inc(ptb_ready, 1)

            def k_part(s, g):
                dve.wait_ge(k_mm, s + 1)
                for h in (2, 3):
                    r = slice(HD * h, HD * (h + 1))
                    i = nc.vector.tensor_scalar(k_diag[r, :, h, :], ps[r, KB, :].rearrange("p (w k) -> p w k", k=W),
                                                qk_bias[r, G + g:G + g + 1], None, ALU.add)
                i.then_inc(kb_ready, 1)

            def v_part(c, t, last=False):
                if t == 0 and (not isinstance(c, int) or c >= 1):
                    dve.wait_ge(o_mm, G * c)
                dve.wait_ge(v_mm, TT * c + t + 1)
                for w in range(2):
                    for par in range(2):
                        src = slice(W * w, W * (w + 1))
                        heads = "p (hp par d) -> p par hp d"
                        i = nc.vector.tensor_tensor(
                            v_sb[W * par:W * (par + 1), t, w, :].rearrange("p (hp d) -> p hp d", d=HD),
                            ps[src, (LAST_BANK if last else V_BANK)[t], :].rearrange(heads, par=2, d=HD)[:, par],
                            v_bias[src, :].rearrange(heads, par=2, d=HD)[:, par], ALU.add)
                i.then_inc(v_ready, 1)

            def o_lo_part(s, m):
                dve.wait_ge(o_hi_ready, s + 1)
                nc.vector.tensor_tensor(ot_lo[:, m, :], ps[:, OT, :], ot_hi[:, m, :].bitcast(F32), ALU.subtract).then_inc(o_ready, 1)

            def chunk(c, first=False):
                s = G * c
                if not first:
                    scale_and_bias(s - 1, 3)
                gate_rows(c)
                if not first:
                    probs_t_part(s - 2)
                    normaliser(s - 1)
                k_part(s, 0)
                if not first:
                    o_lo_part(s - 2, 2)
                layernorm_stats(c + 1)
                scale_and_bias(s, 0)
                if not first:
                    probs_t_part(s - 1)
                normaliser(s)
                k_part(s + 1, 1)
                layernorm_apply(c + 1)
                if not first:
                    o_lo_part(s - 1, 3)
                for t in range(TT):
                    v_part(c, t)
                scale_and_bias(s + 1, 1)
                if not first:
                    for t in range(TT):
                        finish_rows(c - 1, t)
                probs_t_part(s)
                normaliser(s + 1)
                k_part(s + 2, 2)
                o_lo_part(s, 0)
                scale_and_bias(s + 2, 2)
                probs_t_part(s + 1)
                normaliser(s + 2)
                k_part(s + 3, 3)
                xt_lo_part(c + 1)
                o_lo_part(s + 1, 1)

            steps = [0]

            def then(i):
                steps[0] += 1
                i.then_inc(select_step, 1)
                dve.wait_ge(select_step, steps[0])

            v = nc.vector

            def threshold_float():
                then(v.tensor_scalar(flip[:, :], cand[:, :], 31, 0x7FFFFFFF, ALU.arith_shift_right, ALU.bitwise_and))
                then(v.scalar_tensor_tensor(thr[:, :], cand[:, :], -1, flip[:, :], ALU.bitwise_xor, ALU.bitwise_xor))

            def take_bits(i):
                dve.wait_ge(count_mm, i + 1)
                then(v.tensor_scalar(reach[:, :], ps[:, SEARCH, 0:3], float(CAP), 0.0, ALU.is_ge, ALU.add, accum_out=kept[:, :]))
                then(v.tensor_copy(kept_i[:, :], kept[:, :]))
                then(v.scalar_tensor_tensor(key[:, :], kept_i[:, :], 30 - 2 * i, key[:, :], ALU.logical_shift_left, ALU.bitwise_or))

            def search(i):
                if i > 0:
                    take_bits(i - 1)
                then(v.scalar_tensor_tensor(cand[:, :], pattern[:, :], 30 - 2 * i, key[:, 0:1].to_broadcast([P, 3]),
                                            ALU.logical_shift_left, ALU.bitwise_or))
                threshold_float()
                for j in range(3):
                    n = v.tensor_scalar(hits[:, j, :], gate_s[:, :], thr[:, j:j + 1].bitcast(F32), 0.0, ALU.is_ge, ALU.add,
                                        accum_out=cnt[:, j:j + 1])
                n.then_inc(part_counts, 1)

            def last_chunk():
                c, s = NCH - 1, G * (NCH - 1)
                scale_and_bias(s - 1, 3)
                gate_rows(c)
                probs_t_part(s - 2)
                normaliser(s - 1)
                k_part(s, 0)
                dve.wait_ge(scores_in, 16)
                v.tensor_reduce(top[:, :], gate_s[:, :], AX.X, ALU.max).then_inc(top_rows, 1)
                o_lo_part(s - 2, 2)
                scale_and_bias(s, 0)
                dve.wait_ge(top_t_mm, 1)
                then(v.tensor_reduce(top_e[0:1, :], ps[0:1, SEARCH, 0:P].rearrange("p (c e) -> p e c", e=E), AX.X, ALU.max))
                v.tensor_copy(top_row[0:1, :].rearrange("p (c e) -> p c e", e=E),
                              top_e[0:1, :].unsqueeze(1).to_broadcast([1, NCH, E])).then_inc(top_row_ready, 1)
                probs_t_part(s - 1)
                dve.wait_ge(top_mm, 1)
                v.tensor_scalar(top[:, :], ps[:, SEARCH, 0:1], -1.0, None, ALU.mult).then_inc(top_ready, 1)
                search(0)
                normaliser(s)
                k_part(s + 1, 1)
                search(1)
                o_lo_part(s - 1, 3)
                search(2)
                for t in range(TT):
                    v_part(c, t, last=True)
                    search(3 + t)
                scale_and_bias(s + 1, 1)
                search(7)
                for t in range(TT):
                    finish_rows(c - 1, t, last=True)
                    search(8 + t)
                probs_t_part(s)
                search(12)
                normaliser(s + 1)
                k_part(s + 2, 2)
                search(13)
                o_lo_part(s, 0)
                search(14)
                scale_and_bias(s + 2, 2)
                probs_t_part(s + 1)
                search(15)
                normaliser(s + 2)
                k_part(s + 3, 3)
                take_bits(15)
                then(v.tensor_copy(cand[:, :], key[:, 0:1].to_broadcast([P, 3])))
                threshold_float()
                bound = thr[:, 0:1].bitcast(F32)
                v.tensor_scalar(above[:, :], gate_s[:, :], bound, 0.0, ALU.is_gt, ALU.add, accum_out=cnt[:, 0:1]).then_inc(gt_eq_ready, 1)
                v.tensor_scalar(ties[:, :], gate_s[:, :], bound, 0.0, ALU.is_equal, ALU.add, accum_out=cnt[:, 1:2]).then_inc(gt_eq_ready, 1)
                o_lo_part(s + 1, 1)
                scale_and_bias(s + 3, 3)
                dve.wait_ge(gt_eq_ready, 2)
                then(v.tensor_tensor_scan(upto[:, :], ones_row[:, :], ties[:, :], 0.0, ALU.mult, ALU.add))
                dve.wait_ge(room_mm, 2)
                then(v.tensor_scalar(room[:, 0:1], ps[:, SEARCH, 0:1], -1.0, float(CAP), ALU.mult, ALU.add))
                then(v.tensor_tensor(room[:, 1:2], room[:, 0:1], ps[:, SEARCH, 1:2], ALU.subtract))
                probs_t_part(s + 2)
                then(v.scalar_tensor_tensor(ties[:, :], upto[:, :], room[:, 1:2], ties[:, :], ALU.is_le, ALU.mult))
                v.scalar_tensor_tensor(above[:, :], above[:, :], 1.0, ties[:, :], ALU.mult, ALU.add,
                                       accum_out=cnt[:, 2:3]).then_inc(chosen_ready, 1)
                normaliser(s + 3)
                dve.wait_ge(chosen_ready, 1)
                then(v.tensor_tensor_scan(upto[:, :], ones_row[:, :], above[:, :], 0.0, ALU.mult, ALU.add))
                dve.wait_ge(base_mm, 1)
                then(v.tensor_scalar(room[:, 0:1], ps[:, SEARCH, 2:3], -1.0 - N, None, ALU.add))
                then(v.scalar_tensor_tensor(upto[:, :], upto[:, :], room[:, 0:1], above[:, :], ALU.add, ALU.mult))
                v.tensor_scalar(pos[:, :], upto[:, :], float(N), None, ALU.add).then_inc(pos_ready, 1)
                dve.wait_ge(exps_ready, 1)
                v.scalar_tensor_tensor(exps[:, :], exps[:, :], 1.0, above[:, :], ALU.mult, ALU.mult,
                                       accum_out=esum[:, :]).then_inc(total_part, 1)
                o_lo_part(s + 2, 2)
                by_expert = "p (j c e) -> p e c j"
                dve.wait_ge(pos_t_mm, 1)
                v.tensor_copy(pos_i[:, :], ps[:, POS_T, :]).then_inc(select_step, 1)
                probs_t_part(s + 3)
                steps[0] += 1
                dve.wait_ge(select_step, steps[0])
                then(v.tensor_scalar(part_i[:, :], pos_i[:, :], P - 1, None, ALU.bitwise_and))

                def to_experts(out, flat):
                    for e in range(E):
                        n = v.tensor_copy(out[:, e, :].rearrange("p (c j) -> p c j", j=TT),
                                          flat.rearrange(by_expert, j=TT, e=E)[:, e])
                    return n

                then(to_experts(lists.slot_b, part_i[:, :]))
                dve.wait_ge(total_mm, 1)
                dve.wait_ge(total_part, 1)
                then(v.tensor_copy(room[:, 1:2], ps[:, TOTAL, 0:1]))
                then(v.reciprocal(room[:, 1:2], room[:, 1:2]))
                v.tensor_scalar(exps[:, :], exps[:, :], room[:, 1:2], None, ALU.mult).then_inc(wgt_ready, 1)
                o_lo_part(s + 3, 3)
                then(v.tensor_scalar(part_i[:, :], pos_i[:, :], 7, None, ALU.logical_shift_right))
                then(to_experts(lists.slot_a, part_i[:, :]))
                wgt, parts = lists.wgt, lists.wgt_parts
                dve.wait_ge(wgt_t_mm, 1)
                then(to_experts(wgt, ps[:, WGT_T, :]))
                then(v.tensor_copy(parts[:, :, :, 0], wgt[:, :, :]))
                then(v.tensor_tensor(wgt[:, :, :], wgt[:, :, :], parts[:, :, :, 0], ALU.subtract))
                then(v.tensor_copy(parts[:, :, :, 1], wgt[:, :, :]))
                then(v.tensor_tensor(wgt[:, :, :], wgt[:, :, :], parts[:, :, :, 1], ALU.subtract))
                then(v.tensor_copy(parts[:, :, :, 2], wgt[:, :, :]))
                slots_one_hot_a(nc, dve, lists, 0)
                dve.wait_ge(xn_stored, 16 * NCH)
                dve.wait_ge(xt_mm, KC * NCH)
                for g in range(GROUPS):
                    slots_one_hot_b(nc, dve, lists, 0, g)
                expert_list(nc, dve, lists, ps[:, SEARCH, :], 0, 0)
                for t in range(TT):
                    finish_rows(c, t, last=True)

            layernorm_stats(0)
            split_lo(0)
            split_lo(1)
            layernorm_apply(0)
            for u in range(2, V_SPLIT):
                split_lo(u)
            xt_lo_part(0)
            for u in range(V_SPLIT, ALL_SPLIT):
                split_lo(u)
            dve.wait_ge(const_in, 96)
            dve.wait_ge(consts, 14)
            chunk(0, first=True)
            with dve.Fori(1, NCH - 1) as c:
                chunk(c)
            last_chunk()


def expert_block(nc, d, lists):
    ctx = ExitStack()
    with ctx:
        def sb(name, shape, dt=F32):
            return ctx.enter_context(nc.sbuf_tensor(name, shape, dt))

        def sem(name):
            return ctx.enter_context(nc.semaphore(name))

        HALVES = 2
        w13_hi, w13_lo = sb("w13_hi", [P, FM, 2, KC, P], F32R), sb("w13_lo", [P, FM, 2, KC, P], F32R)
        w2_hi, w2_lo = sb("w2_hi", [P, FM, C], F32R), sb("w2_lo", [P, FM, C], F32R)
        raw = sb("raw", [P, 2, 1024])
        h_hi, h_lo = sb("h_hi", [P, FM, T], F32R), sb("h_lo", [P, FM, T], F32R)
        xg, y, ident = lists.x_in, lists.x_res, lists.ident
        weight = lists.weight
        xgt_hi, xgt_lo = sb("xgt_hi", [P, KC, T], F32R), sb("xgt_lo", [P, KC, T], F32R)
        silu, hm = sb("silu", [P, 2, T]), sb("hm", [P, 2, T])
        ps = ctx.enter_context(nc.psum_tensor("ps_e", [P, 8, 512], F32))
        DOWN, LISTS = 4, 7

        w_in = [sem(f"w_in_{i}") for i in range(2)]
        w_hi_ready, w_ready = sem("w_hi_ready"), sem("w_ready")
        xgt_mm, xgt_hi_ready, xgt_ready = sem("xgt_mm"), sem("xgt_hi_ready"), sem("xgt_ready")
        up1_mm, up3_mm, silu_ready, hm_ready = sem("up1_mm"), sem("up3_mm"), sem("silu_ready"), sem("hm_ready")
        h_hi_ready, h_ready = sem("h_hi_ready"), sem("h_ready")
        down_mm, y_mm, y_ready, scattered = sem("down_mm"), sem("y_mm"), sem("y_ready"), sem("scattered")

        block = ctx.enter_context(nc.Block())
        UNITS = FM + FM // 2

        def unit_views(u):
            if u < FM:
                return [w[:, u, :, :, :].rearrange("p a b c -> p (a b c)") for w in (w13_hi, w13_lo)]
            v = 2 * (u - FM)
            return [w[:, v:v + 2, :].rearrange("p a b -> p (a b)") for w in (w2_hi, w2_lo)]

        AHEAD = UNITS - FM

        def first_splits(e):
            return [(e, u) for u in range(AHEAD, UNITS)]


        @block.sync
        def _(sp):
            def load_unit(e, u):
                n = UNITS * e + u
                if not isinstance(n, int) or n >= 2:
                    sp.wait_ge(w_ready, n - 1)
                src = d["w13"][e, u] if u < FM else d["w2"][e, u - FM]
                sp.dma_start(raw[:, u % 2, :], src).then_inc(w_in[u % 2], 16)

            for u in range(UNITS):
                load_unit(0, u)
            with sp.Fori(1, E) as e:
                for u in range(UNITS):
                    load_unit(e, u)

        @block.gpsimd
        def _(pool):
            def gather_half(q, par, tile0, e_idx):
                pool.wait_ge(lists.idx_ready, e_idx)
                pool.wait_ge(xgt_mm, KC * q)
                gather(nc, pool, lists, d["xn"], par, tile0)

            def scatter(q, par, tile0):
                for t in range(TT):
                    pool.wait_ge(y_ready, TT * q + t + 1)
                    if t == 0 and (not isinstance(q, int) or q >= 1):
                        pool.wait_ge(scattered, 16 * TT * q)
                    pool.nop(nofuse=True)
                    nc.gpsimd.indirect_dma_start(
                        out=d["out"], out_offset=bass.IndirectOffsetOnAxis(ap=lists.idx[par][:, tile0 + t:tile0 + t + 1], axis=0),
                        in_=y[:, t, :], in_offset=None, compute_op=ALU.add).then_inc(scattered, 16)

            pool.wait_ge(lists.out_stored, 16 * NCH)

            def expert(e, par, first=False, last=False):
                q = HALVES * e
                gather_half(q + 1, par, TT, e + 1)
                if not first:
                    scatter(q - 1, 1 - par, TT)
                if not last:
                    gather_half(q + 2, 1 - par, 0, e + 2)
                scatter(q, par, 0)

            expert(0, 0, first=True)
            expert(1, 1)
            with pool.Fori(1, E // 2 - 1) as i:
                expert(2 * i, 0)
                expert(2 * i + 1, 1)
            expert(E - 2, 0)
            expert(E - 1, 1, last=True)
            scatter(HALVES * E - 1, 1, TT)
            pool.wait_ge(scattered, 16 * TT * HALVES * E)

        @block.scalar
        def _(act):
            def split_hi(e, u):
                n = UNITS * e + u
                act.wait_ge(w_in[u % 2], 16 * (UNITS // 2 * e + u // 2 + 1))
                if not isinstance(e, int) or e >= 1:
                    if u < FM:
                        act.wait_ge(up3_mm, FM * (HALVES * e - 1) + u + 1)
                    else:
                        act.wait_ge(y_mm, TT * HALVES * e)
                nc.scalar.activation(unit_views(u)[0], raw[:, u % 2, :], ACT.Copy).then_inc(w_hi_ready, 1)

            def xgt_hi_part(q):
                for k in range(KC):
                    act.wait_ge(xgt_mm, KC * q + k + 1)
                    nc.scalar.activation(xgt_hi[:, k, :], ps[:, k, :], ACT.Copy).then_inc(xgt_hi_ready, 1)

            def half(e, q, hf, par, splits, last=False):
                for m in range(FM):
                    n = FM * q + m
                    act.wait_ge(up1_mm, n + 1)
                    if not isinstance(n, int) or n >= 2:
                        act.wait_ge(hm_ready, n - 1)
                    nc.scalar.activation(silu[:, m % 2, :], ps[:, 2 * (m % 2), :], ACT.Silu).then_inc(silu_ready, 1)
                    act.wait_ge(hm_ready, n + 1)
                    if not isinstance(q, int) or q >= 1:
                        if m < FM - 1:
                            act.wait_ge(down_mm, (FM - 1) * (q - 1) + m + 1)
                        else:
                            act.wait_ge(y_mm, TT * q)
                    nc.scalar.activation(h_hi[:, m, :], hm[:, m % 2, :], ACT.Copy).then_inc(h_hi_ready, 1)
                    if m < len(splits):
                        split_hi(*splits[m])
                if not last:
                    xgt_hi_part(q + 1)
                for t in range(TT):
                    act.wait_ge(y_mm, TT * q + t + 1)
                    if t == 0 and isinstance(q, int) and q == 0:
                        act.wait_ge(lists.out_stored, 16 * NCH)
                    elif t == 0:
                        act.wait_ge(scattered, 16 * TT * q)
                    s = TT * hf + t
                    nc.scalar.activation(y[:, t, :], ps[:, DOWN + t, :], ACT.Copy, scale=weight[par][:, s:s + 1]).then_inc(y_ready, 1)

            def expert(e, par, first=False, last=False):
                q = HALVES * e
                half(e, q, 0, par, first_splits(0) if first else [(e, FM + i) for i in range(FM // 2)])
                half(e, q + 1, 1, par, [] if last else [(e + 1, i) for i in range(FM)], last=last)

            split_hi(0, 0)
            split_hi(0, 1)
            xgt_hi_part(0)
            for u in range(2, AHEAD):
                split_hi(0, u)
            expert(0, 0, first=True)
            expert(1, 1)
            with act.Fori(1, E // 2 - 1) as i:
                expert(2 * i, 0)
                expert(2 * i + 1, 1)
            expert(E - 2, 0)
            expert(E - 1, 1, last=True)

        @block.tensor
        def _(pe):
            def xgt(q):
                pe.wait_ge(lists.xg_in, 16 * TT * (q + 1))
                for k in range(KC):
                    if k % 2 == 0 and (not isinstance(q, int) or q >= 1):
                        pe.wait_ge(hm_ready, FM * q - 1 + k // 2)
                    for t in range(TT):
                        i = nc.tensor.transpose(ps[:, k, P * t:P * (t + 1)], xg[:, t, P * k:P * (k + 1)], ident[:, :])
                    i.then_inc(xgt_mm, 1)

            def up(q, e, first_half, next_list=False):
                pe.wait_ge(xgt_ready, KC * (q + 1))
                for m in range(FM):
                    if first_half:
                        pe.wait_ge(w_ready, UNITS * e + m + 1)
                    if m >= 2:
                        pe.wait_ge(hm_ready, FM * q + m - 1)
                    for j, s in ((0, up1_mm), (1, up3_mm)):
                        for k in range(KC):
                            i = split3(nc, ps[:, 2 * (m % 2) + j, :], w13_hi[:, m, j, k, :], w13_lo[:, m, j, k, :],
                                       xgt_hi[:, k, :], xgt_lo[:, k, :], k == 0, k == KC - 1)
                        i.then_inc(s, 1)
                    if next_list and m % 2:
                        if m == 1 and (not isinstance(q, int) or q >= 1):
                            pe.wait_ge(y_ready, TT * q)
                        compact(nc, pe, lists, ps[:, LISTS, :], e + 1, m // 2)

            def down(q, e, first_half, next_list=False):
                if not isinstance(q, int) or q >= 1:
                    pe.wait_ge(y_ready, TT * q)
                if next_list:
                    pe.wait_ge(lists.got_ready, e + 2)
                for k in range(FM):
                    pe.wait_ge(h_ready, FM * q + k + 1)
                    if first_half and k % 2 == 0:
                        pe.wait_ge(w_ready, UNITS * e + FM + k // 2 + 1)
                    for t in range(TT):
                        sl = slice(P * t, P * (t + 1))
                        i = split3(nc, ps[:, DOWN + t, :], h_hi[:, k, sl], h_lo[:, k, sl], w2_hi[:, k, :], w2_lo[:, k, :],
                                   k == 0, k == FM - 1)
                        if k == FM - 1:
                            i.then_inc(y_mm, 1)
                    if k < FM - 1:
                        i.then_inc(down_mm, 1)

            def expert(e, last=False):
                q = HALVES * e
                up(q, e, True, next_list=not last)
                xgt(q + 1)
                down(q, e, True, next_list=not last)
                up(q + 1, e, last)
                if not last:
                    xgt(q + 2)
                down(q + 1, e, False)

            xgt(0)
            expert(0)
            with pe.Fori(1, E - 1) as e:
                expert(e)
            expert(E - 1, last=True)

        @block.vector
        def _(dve):
            v = nc.vector

            def split_lo(e, u):
                n = UNITS * e + u
                dve.wait_ge(w_hi_ready, n + 1)
                hi, lo = unit_views(u)
                v.tensor_tensor(lo, raw[:, u % 2, :], hi.bitcast(F32), ALU.subtract).then_inc(w_ready, 1)

            def xgt_lo_part(q):
                for k in range(KC):
                    dve.wait_ge(xgt_hi_ready, KC * q + k + 1)
                    v.tensor_tensor(xgt_lo[:, k, :], ps[:, k, :], xgt_hi[:, k, :].bitcast(F32), ALU.subtract).then_inc(xgt_ready, 1)

            def half(q, splits, lists_of=None):
                def lo(m):
                    n = FM * q + m
                    dve.wait_ge(h_hi_ready, n + 1)
                    v.tensor_tensor(h_lo[:, m, :], hm[:, m % 2, :], h_hi[:, m, :].bitcast(F32), ALU.subtract).then_inc(h_ready, 1)

                for m in range(FM):
                    n = FM * q + m
                    if lists_of is not None and m % 2 == 0:
                        slots_one_hot_b(nc, dve, lists, lists_of, m // 2)
                    dve.wait_ge(silu_ready, n + 1)
                    dve.wait_ge(up3_mm, n + 1)
                    v.tensor_tensor(hm[:, m % 2, :], ps[:, 2 * (m % 2) + 1, :], silu[:, m % 2, :], ALU.mult).then_inc(hm_ready, 1)
                    lo(m)
                    if m < len(splits):
                        split_lo(*splits[m])

            def expert(e, par, first=False, last=False, second_next=True):
                q = HALVES * e
                half(q, first_splits(0) if first else [(e, FM + i) for i in range(FM // 2)], lists_of=None if last else e + 1)
                if not last:
                    expert_list(nc, dve, lists, ps[:, LISTS, :], e + 1, 1 - par, scattered)
                xgt_lo_part(q + 1)
                if second_next:
                    slots_one_hot_a(nc, dve, lists, e + 2)
                half(q + 1, [] if last else [(e + 1, i) for i in range(FM)])
                if not last:
                    xgt_lo_part(q + 2)

            slots_one_hot_a(nc, dve, lists, 1)
            split_lo(0, 0)
            split_lo(0, 1)
            xgt_lo_part(0)
            for u in range(2, AHEAD):
                split_lo(0, u)
            expert(0, 0, first=True)
            expert(1, 1)
            with dve.Fori(1, E // 2 - 1) as i:
                expert(2 * i, 0)
                expert(2 * i + 1, 1)
            expert(E - 2, 0, second_next=False)
            expert(E - 1, 1, last=True, second_next=False)


def build_kernel(nc, x, wqk, wv, wp, wg, rel, qkb, vb, pb, same, earlier, w13, w2, out):
    ctx = ExitStack()
    with ctx:
        lists = Lists(nc, ctx)
        xn = nc.dram_tensor("xn_rows", [N, C], F32, kind="Internal").ap()
        gate = nc.dram_tensor("gate_rows", [P, T], F32, kind="Internal").ap()
        rows = "(c t p) n -> c p t n"
        d = {"x": x.rearrange(rows, t=TT, p=P), "out": out.rearrange(rows, t=TT, p=P),
             "xn": xn.rearrange(rows, t=TT, p=P), "xn_rows": xn, "gate": gate, "wqk": wqk, "wv": wv, "wp": wp, "wg": wg,
             "rel": rel, "qkb": qkb, "vb": vb, "pb": pb, "same": same, "earlier": earlier}
        attention_block(nc, d, lists)
        expert_block(nc, {"xn": xn, "out": out, "w13": w13, "w2": w2}, lists)


def kernel(L0_attn_x, L0_attn_qkv_w, L0_attn_qkv_b, L0_attn_proj_w, L0_attn_proj_b, L0_attn_rel_bias,
           L0_ffn_Wg, L0_ffn_W1, L0_ffn_W2, L0_ffn_W3):
    import numpy as np
    import concourse.bacc as bacc
    from concourse.bass_utils import run_bass_kernel_spmd

    def rows(w):
        return np.ascontiguousarray(np.asarray(w).reshape(KC, P, -1).transpose(1, 0, 2))

    x = np.asarray(L0_attn_x)
    qkv_b = np.asarray(L0_attn_qkv_b)
    dist = np.arange(W)[:, None] - np.arange(W)[None, :] + W - 1
    rel = np.asarray(L0_attn_rel_bias)[dist].transpose(0, 2, 1)
    w13 = np.stack([np.asarray(L0_ffn_W1), np.asarray(L0_ffn_W3)], 1)
    w13 = w13.reshape(E, 2, FM, P, KC, P).transpose(0, 2, 5, 1, 4, 3)
    w2 = np.asarray(L0_ffn_W2).reshape(E, C, FM // 2, 2, P).transpose(0, 2, 4, 3, 1)
    r = np.arange(P)
    arrays = {
        "x": x.reshape(N, C),
        "wqk": rows(L0_attn_qkv_w)[:, :, :2 * C].reshape(P, KC, 2, G, P).transpose(0, 3, 2, 1, 4).reshape(P, -1),
        "wv": rows(L0_attn_qkv_w)[:, :, 2 * C:].reshape(P, -1),
        "wp": rows(L0_attn_proj_w).reshape(P, -1),
        "wg": np.pad(rows(np.asarray(L0_ffn_Wg).T), ((0, 0), (0, 0), (0, P - E))).reshape(P, -1),
        "rel": np.concatenate([rel, rel], 0),
        "qkb": qkv_b[:2 * C].reshape(2 * G, P).T,
        "vb": np.broadcast_to(qkv_b[2 * C:], (P, C)),
        "pb": np.broadcast_to(np.asarray(L0_attn_proj_b), (P, C)),
        "same": (r[:, None] % E == r[None, :] % E).astype(np.float32),
        "earlier": ((r[:, None] % E == r[None, :] % E) & (r[:, None] < r[None, :])).astype(np.float32),
        "w13": w13.reshape(E, FM, P, 2 * KC * P),
        "w2": w2.reshape(E, FM // 2, P, 2 * C),
    }
    nc = bacc.Bacc("TRN2", target_bir_lowering=False, num_devices=1)
    arrays = {f"in_{name}": np.ascontiguousarray(a) for name, a in arrays.items()}
    args = [nc.dram_tensor(name, a.shape, mybir.dt.from_np(a.dtype), kind="ExternalInput").ap()
            for name, a in arrays.items()]
    args.append(nc.dram_tensor("out_rows", (N, C), F32, kind="ExternalOutput").ap())
    build_kernel(nc, *args)
    result = run_bass_kernel_spmd(nc, [arrays], core_ids=[0])
    return result.results[0]["out_rows"].reshape(x.shape)
```

```python
from contextlib import ExitStack

import concourse.bass as bass
from concourse import mybir
from concourse.alu_op_type import AluOpType as ALU

ACT = mybir.ActivationFunctionType
AX = mybir.AxisListType
F32 = mybir.dt.float32
F32R = mybir.dt.float32r
BF16 = mybir.dt.bfloat16
I32 = mybir.dt.int32
U32 = mybir.dt.uint32

P = 128
N = 8192
C = 512
KC = C // P
T = 512
NCH = N // T
TT = T // P
W = 64
HD = 32
H = C // HD
G = 4
E = 8
F = 1024
FM = F // P
CAP = N // E
NT = N // P
NS = CAP // P
GATE_COLS = 32
HG = 8
GROUPS = NT // HG
SCALE = HD ** -0.5
EPS = 1e-5


def split3(nc, out, w_hi, w_lo, x_hi, x_lo, start, stop):
    nc.tensor.matmul(out, w_hi, x_hi, start=start, stop=False)
    nc.tensor.matmul(out, w_hi, x_lo, start=False, stop=False)
    return nc.tensor.matmul(out, w_lo, x_hi, start=False, stop=stop)


class Lists:

    def __init__(self, nc, ctx):
        def sb(name, shape, dt=F32):
            return ctx.enter_context(nc.sbuf_tensor(name, shape, dt))

        def sem(name):
            return ctx.enter_context(nc.semaphore(name))

        self.slot_a, self.slot_b = sb("slot_a", [P, E, NT], BF16), sb("slot_b", [P, E, NT], BF16)
        self.wgt, self.wgt_parts = sb("wgt", [P, E, NT]), sb("wgt_parts", [P, E, NT, 3], BF16)
        self.ident = sb("ident", [P, P])
        self.iota_b, self.iota_a = sb("iota_b", [P, P], BF16), sb("iota_a", [P, NS], BF16)
        self.iota_p, self.iota_t = sb("iota_p", [P, 1]), sb("iota_t", [P, NT], BF16)
        self.hot_a, self.hot_v = sb("hot_a", [P, NT, NS], BF16), sb("hot_v", [P, NT, 5, NS], BF16)
        self.got, self.idx_f = sb("got", [P, 5, NS]), sb("idx_f", [P, NS])
        self.idx = [sb(f"idx_{i}", [P, NS], U32) for i in range(2)]
        self.weight = [sb(f"weight_{i}", [P, NS]) for i in range(2)]
        self.x_in, self.x_res, self.xn = (sb(n, [P, TT, C]) for n in ("x_in", "x_res", "xn"))
        self.hot_b = self.xn[:, 0:2, :].bitcast(BF16).rearrange("p a (t b) -> p a t b", b=P)
        self.raw = [self.xn[:, 2:4, :].rearrange("p a b -> p (a b)"), sb("raw", [P, 1024])[:, :]]
        self.list_step = sem("list_step")
        self.values_ready, self.hot_ready, self.hot_mm, self.got_ready, self.idx_ready = (sem(n) for n in (
            "values_ready", "hot_ready", "hot_mm", "got_ready", "idx_ready"))
        self.w_in = [sem(f"w_in_{i}") for i in range(2)]
        self.xg_in, self.out_stored = sem("xg_in"), sem("out_stored")


STEPS = 4


def over_slots(a):
    return a.rearrange("p o t -> p (o t)").unsqueeze(2).to_broadcast([P, NT, NS])


def places_one_hot(nc, dve, k, e):
    v = nc.vector
    if not isinstance(e, int) or e >= 1:
        dve.wait_ge(k.hot_mm, GROUPS * e)
    v.tensor_tensor(k.hot_a[:, :, :], over_slots(k.slot_a[:, bass.ds(e, 1), :]),
                    k.iota_a[:, :].unsqueeze(1).to_broadcast([P, NT, NS]), ALU.is_equal).then_inc(k.list_step, 1)
    dve.wait_ge(k.list_step, STEPS * e + 1)
    v.tensor_scalar(k.hot_v[:, :, 0, :], k.hot_a[:, :, :], k.iota_p[:, 0:1], None, ALU.mult)
    v.tensor_tensor(k.hot_v[:, :, 1, :], k.hot_a[:, :, :], k.iota_t[:, :].unsqueeze(2).to_broadcast([P, NT, NS]), ALU.mult)


def weights_one_hot(nc, dve, k, e):
    for j in range(3):
        i = nc.vector.tensor_tensor(k.hot_v[:, :, 2 + j, :], k.hot_a[:, :, :],
                                    over_slots(k.wgt_parts[:, bass.ds(e, 1), :, j]), ALU.mult)
    i.then_inc(k.values_ready, 1)


def slots_one_hot(nc, dve, k, e, g):
    if not isinstance(e, int) or e >= 1 or g >= 2:
        dve.wait_ge(k.hot_mm, GROUPS * e + g - 1)
    nc.vector.tensor_tensor(k.hot_b[:, g % 2, :, :],
                            k.slot_b[:, bass.ds(e, 1), HG * g:HG * (g + 1)].rearrange("p o t -> p (o t)").unsqueeze(2).to_broadcast([P, HG, P]),
                            k.iota_b[:, :].unsqueeze(1).to_broadcast([P, HG, P]), ALU.is_equal).then_inc(k.hot_ready, 1)


def compact(nc, pe, k, bank, e, g):
    if g == 0:
        pe.wait_ge(k.values_ready, e + 1)
    pe.wait_ge(k.hot_ready, GROUPS * e + g + 1)
    for t in range(HG):
        n = HG * g + t
        i = nc.tensor.matmul(bank[:, 0:5 * NS], k.hot_b[:, g % 2, t, :], k.hot_v[:, n, :, :].rearrange("p v a -> p (v a)"),
                             start=(n == 0), stop=(n == NT - 1))
    i.then_inc(k.hot_mm, 1)


def take_sums(nc, dve, k, bank, e):
    dve.wait_ge(k.hot_mm, GROUPS * (e + 1))
    nc.vector.tensor_copy(k.got[:, :, :].rearrange("p v a -> p (v a)"), bank[:, 0:5 * NS]).then_inc(k.got_ready, 1)


def expert_list(nc, dve, k, e, par, scattered=None):
    v = nc.vector
    dve.wait_ge(k.got_ready, e + 1)
    if not isinstance(e, int) or e >= 2:
        dve.wait_ge(scattered, 16 * TT * 2 * (e - 1))
    v.scalar_tensor_tensor(k.idx_f[:, :], k.got[:, 1, :], float(P), k.got[:, 0, :], ALU.mult, ALU.add).then_inc(k.list_step, 1)
    v.tensor_tensor(k.got[:, 2, :], k.got[:, 2, :], k.got[:, 3, :], ALU.add).then_inc(k.list_step, 1)
    dve.wait_ge(k.list_step, STEPS * e + 3)
    v.tensor_copy(k.idx[par][:, :], k.idx_f[:, :]).then_inc(k.idx_ready, 1)
    v.tensor_tensor(k.weight[par][:, :], k.got[:, 2, :], k.got[:, 4, :], ALU.add).then_inc(k.list_step, 1)


def gather(nc, pool, k, xn_rows, par, tile0):
    pool.nop(nofuse=True)
    for t in range(TT):
        nc.gpsimd.indirect_dma_start(
            out=k.x_in[:, t, :], out_offset=None, in_=xn_rows,
            in_offset=bass.IndirectOffsetOnAxis(ap=k.idx[par][:, tile0 + t:tile0 + t + 1], axis=0)).then_inc(k.xg_in, 16)


def attention_block(nc, d, lists):
    ctx = ExitStack()
    with ctx:
        def sb(name, shape, dt=F32):
            return ctx.enter_context(nc.sbuf_tensor(name, shape, dt))

        def sem(name):
            return ctx.enter_context(nc.semaphore(name))

        wqk_hi, wqk_lo = sb("wqk_hi", [P, 2 * G, KC, P], F32R), sb("wqk_lo", [P, 2 * G, KC, P], F32R)
        wv_hi, wv_lo = sb("wv_hi", [P, KC, C], F32R), sb("wv_lo", [P, KC, C], F32R)
        wp_hi, wp_lo = sb("wp_hi", [P, KC, C], F32R), sb("wp_lo", [P, KC, C], F32R)
        wg = sb("wg", [P, KC, GATE_COLS])
        rel = sb("rel", [P, H, W])
        qk_bias, v_bias, p_bias = sb("qk_bias", [P, 2 * G]), sb("v_bias", [P, C]), sb("p_bias", [P, C])
        ident, x_in, x_res, xn = lists.ident, lists.x_in, lists.x_res, lists.xn
        stats, mv = sb("stats", [P, TT, 6]), sb("mv", [P, TT, 2])
        veps, rstd, power = sb("veps", [P, TT]), sb("rstd", [P, TT]), sb("power", [P, TT])
        xt_hi, xt_lo = sb("xt_hi", [P, KC, T], F32R), sb("xt_lo", [P, KC, T], F32R)
        q_sb = sb("q_sb", [P, T])
        k_diag = sb("k_diag", [P, T // W, G, W])
        v_sb = sb("v_sb", [P, TT, C])
        s_sb = sb("s_sb", [P, TT, 4, W])
        p_sb = sb("p_sb", [P, TT, 4, W])
        pn_sb = sb("pn_sb", [P, TT, 4, W])
        pt_diag = sb("pt_diag", [P, TT, 4, P])
        s_max, s_sum, s_rec = sb("s_max", [P, 16]), sb("s_sum", [P, 16]), sb("s_rec", [P, 16])
        ot_hi, ot_lo = sb("ot_hi", [P, G, T], F32R), sb("ot_lo", [P, G, T], F32R)
        g_sb = sb("g_sb", [P, T])
        gate_s, above, ties, upto, exps = (sb(n, [P, T]) for n in ("gate_s", "above", "ties", "upto", "exps"))
        pos = ties
        hits = sb("hits", [P, 3, T], BF16)
        ones_row = sb("ones_row", [P, T])
        same, earlier = sb("same", [P, P]), sb("earlier", [P, P])
        top, top_e, top_row, one = sb("top", [P, 1]), sb("top_e", [1, E]), sb("top_row", [1, P]), sb("one", [1, 1])
        pattern, cand, flip, thr = (sb(n, [P, 3], I32) for n in ("pattern", "cand", "flip", "thr"))
        key, kept_i, kept, reach = sb("key", [P, 1], I32), sb("kept_i", [P, 1], I32), sb("kept", [P, 1]), sb("reach", [P, 3])
        cnt, room, esum = sb("cnt", [P, 3]), sb("room", [P, 2]), sb("esum", [P, 1])
        pos_i = hits[:, 0:2, :].bitcast(I32).rearrange("p a b -> p (a b)")
        part_i = sb("part_i", [P, T], I32)
        RAW = [x_res[:, 0:2, :].rearrange("p a b -> p (a b)"), x_res[:, 2:4, :].rearrange("p a b -> p (a b)"),
               pn_sb[:, :, :, :].rearrange("p t h k -> p (t h k)")]
        ps = ctx.enter_context(nc.psum_tensor("ps", [P, 8, 512], F32))
        QB, KB, SP, OT = 0, 1, 2, 4
        V_BANK, P_BANK, X_BANK, G_BANK = (5, 6, 7, 5), (6, 7, 5, 6), (7, 5, 6, QB), 5
        LAST_BANK = (6, 7, 6, 7)
        SEARCH, TOTAL, POS_T, WGT_T = 5, 6, KB, QB

        def diagonal_blocks(par):
            src = ps[W * par:W * (par + 1), SP:SP + 2, :].rearrange("p b (t hp w q) -> p (b t) hp w q", t=2, hp=2, w=2)
            return [(pt_diag[W * w:W * (w + 1), :, par::2, W * w:W * (w + 1)], src[:, :, :, w, :]) for w in range(2)]

        x_first_in = sem("x_first_in")
        wg_in = sem("wg_in")
        const_in = sem("const_in")
        raw_in = [sem(f"raw_in_{i}") for i in range(3)]
        raw_hi, raw_lo = sem("raw_hi"), sem("raw_lo")
        consts = sem("consts")
        x_loaded, xn_ready, xn_stored = sem("x_loaded"), sem("xn_ready"), sem("xn_stored")
        stat_ready, mv_ready, veps_ready, rstd_ready = sem("stat_ready"), sem("mv_ready"), sem("veps_ready"), sem("rstd_ready")
        xt_mm, xt_hi_ready, xt_ready = sem("xt_mm"), sem("xt_hi_ready"), sem("xt_ready")
        gate_mm, gate_sb_ready, gate_stored, scores_in = sem("gate_mm"), sem("gate_sb_ready"), sem("gate_stored"), sem("scores_in")
        top_rows, top_t_mm, top_row_ready, top_mm, top_ready = (sem(n) for n in (
            "top_rows", "top_t_mm", "top_row_ready", "top_mm", "top_ready"))
        exps_ready, select_step, hits_ready, hits_summed, part_counts, count_mm, gt_eq_ready, room_mm = (sem(n) for n in (
            "exps_ready", "select_step", "hits_ready", "hits_summed", "part_counts", "count_mm", "gt_eq_ready", "room_mm"))
        chosen_ready, base_mm, total_part, total_mm, pos_ready, wgt_ready, pos_t_mm, wgt_t_mm = (sem(n) for n in (
            "chosen_ready", "base_mm", "total_part", "total_mm", "pos_ready", "wgt_ready", "pos_t_mm", "wgt_t_mm"))
        wgt_copied, wgt_part_ready, wgt_rest_ready = sem("wgt_copied"), sem("wgt_part_ready"), sem("wgt_rest_ready")
        q_mm, k_mm, q_ready = sem("q_mm"), sem("k_mm"), sem("q_ready")
        ka_ready, kb_ready = sem("ka_ready"), sem("kb_ready")
        v_mm, v_ready = sem("v_mm"), sem("v_ready")
        s_mm, s_ready, max_ready, sub_ready = sem("s_mm"), sem("s_ready"), sem("max_ready"), sem("sub_ready")
        exp_ready, sum_ready, rec_ready, norm_ready = sem("exp_ready"), sem("sum_ready"), sem("rec_ready"), sem("norm_ready")
        pt_mm, pta_ready, ptb_ready = sem("pt_mm"), sem("pta_ready"), sem("ptb_ready")
        o_mm, o_hi_ready, o_ready = sem("o_mm"), sem("o_hi_ready"), sem("o_ready")
        p_mm, out_ready, out_stored = sem("p_mm"), sem("out_ready"), lists.out_stored
        res_loaded, res_ready = sem("res_loaded"), sem("res_ready")

        def raw_units():
            wqk, wv, wp = ([w[...].rearrange(r) for w in ws] for ws, r in (
                ((wqk_hi, wqk_lo), "p g a b -> p (g a b)"), ((wv_hi, wv_lo), "p a b -> p (a b)"),
                ((wp_hi, wp_lo), "p a b -> p (a b)")))
            order = [(wqk, d["wqk"], 0), (wqk, d["wqk"], 1), (wv, d["wv"], 0), (wv, d["wv"], 1),
                     (wqk, d["wqk"], 2), (wqk, d["wqk"], 3), (wp, d["wp"], 0), (wp, d["wp"], 1)]
            for (hi, lo), src, u in order:
                c0 = slice(1024 * u, 1024 * (u + 1))
                yield src[:, c0], hi[:, c0], lo[:, c0]

        units = list(raw_units())
        Q0_SPLIT, V_SPLIT, ALL_SPLIT = 1, 4, len(units)

        block = ctx.enter_context(nc.Block())

        @block.sync
        def _(sp):
            sp.dma_start(x_in[:, 0:2, :], d["x"][0, :, 0:2, :]).then_inc(x_first_in, 16)
            sp.dma_start(x_in[:, 2:4, :], d["x"][0, :, 2:4, :]).then_inc(x_loaded, 16)
            sp.dma_start(wg[:, :, :].rearrange("p a b -> p (a b)"), d["wg"]).then_inc(wg_in, 16)
            for u, (src, _, _) in enumerate(units):
                if u == 2:
                    for dst, const in ((rel[:, :, :], d["rel"]), (qk_bias[:, :], d["qkb"]),
                                       (v_bias[:, :], d["vb"]), (p_bias[:, :], d["pb"]),
                                       (same[:, :], d["same"]), (earlier[:, :], d["earlier"])):
                        sp.dma_start(dst, const).then_inc(const_in, 16)
                if u >= 3:
                    sp.wait_ge(raw_lo, u - 2)
                sp.dma_start(RAW[u % 3], src).then_inc(raw_in[u % 3], 16)

            def keep_xn(c):
                sp.wait_ge(xn_ready, TT * (c + 1))
                sp.dma_start(d["xn"][c], xn[:, :, :]).then_inc(xn_stored, 16)

            def keep_scores(c):
                sp.wait_ge(gate_sb_ready, c + 1)
                for j in range(4):
                    sp.dma_start(d["gate"][j, bass.ds(E * c, E), :], g_sb[32 * j:32 * j + E, :]).then_inc(gate_stored, 16)

            def load_x(c):
                sp.dma_start(x_in[:, :, :], d["x"][c]).then_inc(x_loaded, 16)

            def store_out(c):
                sp.wait_ge(out_ready, TT * (c + 1))
                sp.dma_start(d["out"][c], x_res[:, :, :]).then_inc(out_stored, 16)
                if not isinstance(c, int) or c < NCH - 1:
                    sp.wait_ge(out_stored, 16 * (c + 1))

            def load_res(c):
                sp.dma_start(x_res[:, :, :], d["x"][c]).then_inc(res_loaded, 16)

            keep_xn(0)
            load_x(1)
            sp.wait_ge(raw_lo, ALL_SPLIT)
            load_res(0)
            keep_scores(0)
            keep_xn(1)
            load_x(2)
            with sp.Fori(1, NCH - 2) as c:
                keep_scores(c)
                keep_xn(c + 1)
                load_x(c + 2)
                store_out(c - 1)
                load_res(c)
            keep_scores(NCH - 2)
            keep_xn(NCH - 1)
            terms, old = (gate_s, above, ties, upto), E * (NCH - 1)
            sp.wait_ge(gate_stored, 64 * (NCH - 1))
            for j, term in enumerate(terms):
                sp.dma_start(term[0:old, :], d["gate"][j, 0:old, :]).then_inc(scores_in, 16)
            store_out(NCH - 3)
            load_res(NCH - 2)
            sp.wait_ge(gate_sb_ready, NCH)
            for j, term in enumerate(terms):
                sp.dma_start(term[old:P, :], g_sb[32 * j:32 * j + E, :]).then_inc(scores_in, 16)
            store_out(NCH - 2)
            load_res(NCH - 1)
            sp.wait_ge(xn_stored, 16 * NCH)
            sp.wait_ge(xt_mm, KC * NCH)
            for u in range(2):
                sp.dma_start(lists.raw[u], d["w13"][0, u]).then_inc(lists.w_in[u], 16)
            store_out(NCH - 1)

        @block.gpsimd
        def _(pool):
            nc.gpsimd.memset(ident[:, :], 0.0).then_inc(consts, 1)
            nc.gpsimd.memset(power[:, :], -0.5).then_inc(consts, 1)
            nc.gpsimd.memset(k_diag[:, :, :, :], 0.0).then_inc(consts, 1)
            nc.gpsimd.memset(pt_diag[:, :, :, :], 0.0).then_inc(consts, 1)
            nc.gpsimd.memset(ones_row[:, :], 1.0).then_inc(consts, 1)
            nc.gpsimd.memset(one[:, :], 1.0).then_inc(consts, 1)
            nc.gpsimd.memset(key[:, :], 0).then_inc(consts, 1)
            for j in range(3):
                nc.gpsimd.memset(pattern[:, j:j + 1], j + 1).then_inc(consts, 1)
            wide = dict(allow_small_or_imprecise_dtypes=True)
            nc.gpsimd.iota(lists.iota_b[:, :], [[1, P]], 0, 0, **wide).then_inc(consts, 1)
            nc.gpsimd.iota(lists.iota_a[:, :], [[1, NS]], 0, 0, **wide).then_inc(consts, 1)
            nc.gpsimd.iota(lists.iota_t[:, :], [[1, NT]], 0, 0, **wide).then_inc(consts, 1)
            nc.gpsimd.iota(lists.iota_p[:, :], [[0, 1]], 0, 1, **wide).then_inc(consts, 1)
            pool.wait_ge(consts, 10)
            nc.gpsimd.affine_select(out=ident[:, :], in_=ident[:, :], compare_op=ALU.not_equal, fill=1.0,
                                    base=0, pattern=[[-1, P]], channel_multiplier=1).then_inc(consts, 1)

            def layernorm_rstd(c):
                pool.wait_ge(veps_ready, c + 1)
                nc.gpsimd.tensor_tensor(rstd[:, :], veps[:, :], power[:, :], ALU.pow).then_inc(rstd_ready, 1)

            def residual(c):
                pool.wait_ge(res_loaded, 16 * (c + 1))
                nc.gpsimd.tensor_tensor(x_res[:, :, :], x_res[:, :, :],
                                        p_bias[:, :].unsqueeze(1).to_broadcast([P, TT, C]), ALU.add).then_inc(res_ready, 1)

            def softmax(s):
                pool.wait_ge(max_ready, s + 1)
                nc.gpsimd.tensor_tensor(s_sb[:, :, :, :], s_sb[:, :, :, :],
                                        s_max[:, :].rearrange("p (t h) -> p t h", t=TT).unsqueeze(3)
                                        .to_broadcast([P, TT, 4, W]), ALU.subtract).then_inc(sub_ready, 1)
                pool.wait_ge(rec_ready, s + 1)
                if not isinstance(s, int) or s >= 1:
                    pool.wait_ge(pt_mm, 2 * s)
                nc.gpsimd.tensor_tensor(pn_sb[:, :, :, :], p_sb[:, :, :, :],
                                        s_rec[:, :].rearrange("p (t h) -> p t h", t=TT).unsqueeze(3)
                                        .to_broadcast([P, TT, 4, W]), ALU.mult).then_inc(norm_ready, 1)

            def chunk(c, first=False, last=False):
                if not first:
                    softmax(G * c - 1)
                if not last:
                    layernorm_rstd(c + 1)
                softmax(G * c)
                if not first:
                    pool.wait_ge(const_in, 96)
                    residual(c - 1)
                softmax(G * c + 1)
                softmax(G * c + 2)

            pool.wait_ge(consts, 15)
            layernorm_rstd(0)
            pool.wait_ge(raw_lo, ALL_SPLIT)
            chunk(0, first=True)
            with pool.Fori(1, NCH - 1) as c:
                chunk(c)
            chunk(NCH - 1, last=True)
            softmax(G * NCH - 1)
            residual(NCH - 1)
            for j in range(2):
                pool.wait_ge(wgt_part_ready, j + 1)
                nc.gpsimd.tensor_tensor(lists.wgt[:, :, :], lists.wgt[:, :, :], lists.wgt_parts[:, :, :, j], ALU.subtract).then_inc(wgt_rest_ready, 1)
            pool.wait_ge(xn_ready, TT * NCH)
            pool.wait_ge(lists.idx_ready, 1)
            gather(nc, pool, lists, d["xn_rows"], 0, 0)

        @block.scalar
        def _(act):
            def split_hi(u):
                act.wait_ge(raw_in[u % 3], 16 * (u // 3 + 1))
                nc.scalar.activation(units[u][1], RAW[u % 3], ACT.Copy).then_inc(raw_hi, 1)

            def xt_hi_part(c):
                for k in range(KC):
                    act.wait_ge(xt_mm, KC * c + k + 1)
                    nc.scalar.activation(xt_hi[:, k, :], ps[:, X_BANK[k], :], ACT.Copy).then_inc(xt_hi_ready, 1)

            def q_part(s, g, scores=True):
                act.wait_ge(q_mm, s + 1)
                if scores:
                    act.wait_ge(s_mm, 2 * s)
                nc.scalar.activation(q_sb[:, :], ps[:, QB, :], ACT.Identity, bias=qk_bias[:, g:g + 1]).then_inc(q_ready, 1)

            def probs_t_part(s, both=False):
                act.wait_ge(pt_mm, 2 * s + 2)
                if not isinstance(s, int) or s >= 1:
                    act.wait_ge(o_mm, s)
                for out, src in diagonal_blocks(0):
                    i = nc.scalar.activation(out, src, ACT.Copy)
                i.then_inc(pta_ready, 1)
                if both:
                    for out, src in diagonal_blocks(1):
                        i = nc.scalar.activation(out, src, ACT.Copy)
                    i.then_inc(ptb_ready, 1)

            def exponentials(s):
                act.wait_ge(sub_ready, s + 1)
                nc.scalar.activation(p_sb[:, :, :, :], s_sb[:, :, :, :], ACT.Exp).then_inc(exp_ready, 1)

            def k_part(s, g, both=False):
                act.wait_ge(k_mm, s + 1)
                for h in range(4 if both else 2):
                    r = slice(HD * h, HD * (h + 1))
                    i = nc.scalar.activation(k_diag[r, :, h, :], ps[r, KB, :].rearrange("p (w k) -> p w k", k=W),
                                             ACT.Identity, bias=qk_bias[r, G + g:G + g + 1])
                    if h == 1:
                        i.then_inc(ka_ready, 1)
                    if h == 3:
                        i.then_inc(kb_ready, 1)

            def o_hi_part(s, m, projected=None):
                act.wait_ge(o_mm, s + 1)
                if projected is not None:
                    act.wait_ge(p_mm, projected)
                nc.scalar.activation(ot_hi[:, m, :], ps[:, OT, :], ACT.Copy).then_inc(o_hi_ready, 1)

            def chunk(c, first=False):
                for g in range(G):
                    s = G * c + g
                    q_part(s, g, scores=not (first and g == 0))
                    if not (first and g < 2):
                        probs_t_part(s - 2)
                    if not (first and g == 0):
                        exponentials(s - 1)
                    k_part(s, g)
                    if g == 3:
                        xt_hi_part(c + 1)
                    if not (first and g < 2):
                        o_hi_part(s - 2, (g + 2) % G, projected=TT * c if g == 2 and not first else None)

            def count_hits(i):
                for j in range(2):
                    act.wait_ge(hits_ready, 2 * i + j + 1)
                    nc.scalar.activation(hits[:, j, :], hits[:, j, :], ACT.Copy, accum_out=cnt[:, j:j + 1]).then_inc(hits_summed, 1)

            def last_chunk():
                c, s = NCH - 1, G * (NCH - 1)
                q_part(s, 0)
                probs_t_part(s - 2, both=True)
                exponentials(s - 1)
                k_part(s, 0)
                o_hi_part(s - 2, 2)
                q_part(s + 1, 1)
                probs_t_part(s - 1, both=True)
                count_hits(0)
                exponentials(s)
                k_part(s + 1, 1, both=True)
                o_hi_part(s - 1, 3)
                for i in range(1, 7):
                    count_hits(i)
                exponentials(s + 1)
                for i in range(7, 10):
                    count_hits(i)
                q_part(s + 2, 2)
                count_hits(10)
                probs_t_part(s, both=True)
                count_hits(11)
                k_part(s + 2, 2, both=True)
                o_hi_part(s, 0, projected=TT * c)
                count_hits(12)
                q_part(s + 3, 3)
                count_hits(13)
                exponentials(s + 2)
                probs_t_part(s + 1, both=True)
                count_hits(14)
                k_part(s + 3, 3, both=True)
                o_hi_part(s + 1, 1)
                count_hits(15)
                act.wait_ge(top_ready, 1)
                nc.scalar.activation(exps[:, :], gate_s[:, :], ACT.Exp, bias=top[:, 0:1]).then_inc(exps_ready, 1)
                probs_t_part(s + 2, both=True)
                exponentials(s + 3)
                o_hi_part(s + 2, 2)
                probs_t_part(s + 3, both=True)
                act.wait_ge(wgt_t_mm, 1)
                for e in range(E):
                    i = nc.scalar.activation(lists.wgt[:, e, :].rearrange("p (c j) -> p c j", j=TT),
                                             ps[:, WGT_T, :].rearrange("p (j c e) -> p e c j", j=TT, e=E)[:, e], ACT.Copy)
                i.then_inc(wgt_copied, 1)
                act.wait_ge(wgt_copied, 1)
                for j in range(3):
                    if j >= 1:
                        act.wait_ge(wgt_rest_ready, j)
                    nc.scalar.activation(lists.wgt_parts[:, :, :, j], lists.wgt[:, :, :], ACT.Copy).then_inc(wgt_part_ready, 1)
                    if j == 0:
                        o_hi_part(s + 3, 3)

            split_hi(0)
            split_hi(1)
            xt_hi_part(0)
            for u in range(2, ALL_SPLIT):
                split_hi(u)
            act.wait_ge(const_in, 96)
            act.wait_ge(consts, 15)
            chunk(0, first=True)
            with act.Fori(1, NCH - 1) as c:
                chunk(c)
            last_chunk()

        @block.tensor
        def _(pe):
            def xt(c):
                pe.wait_ge(xn_ready, TT * (c + 1))
                for k in range(KC):
                    if isinstance(c, int) and c == 1 and k == 0:
                        pe.wait_ge(v_ready, TT)
                    if k < 3 and (not isinstance(c, int) or c >= 2):
                        pe.wait_ge(out_ready, TT * (c - 2) + k + 2)
                    if k == 3 and (not isinstance(c, int) or c >= 1):
                        pe.wait_ge(q_ready, G * c)
                    for t in range(TT):
                        i = nc.tensor.transpose(ps[:, X_BANK[k], P * t:P * (t + 1)], xn[:, t, P * k:P * (k + 1)], ident[:, :])
                    i.then_inc(xt_mm, 1)

            def gate(c):
                pe.wait_ge(xt_ready, KC * (c + 1))
                for k in range(0, KC, 2):
                    for j in range(4):
                        x_part = (xt_hi, xt_lo)[j % 2][:, k + j // 2, :].bitcast(F32)
                        i = nc.tensor.matmul(ps[32 * j:32 * (j + 1), G_BANK, :], wg[:, k + j // 2, :], x_part,
                                             start=(k == 0), stop=(k == KC - 2))
                i.then_inc(gate_mm, 1)

            def scores(s):
                pe.wait_ge(q_ready, s + 1)
                pe.wait_ge(ka_ready, s + 1)
                pe.wait_ge(kb_ready, s + 1)
                if not isinstance(s, int) or s >= 2:
                    pe.wait_ge(pta_ready, s - 1)
                    pe.wait_ge(ptb_ready, s - 1)
                for t in range(TT):
                    for j in range(4):
                        w = 2 * t + j // 2
                        i = nc.tensor.matmul(ps[32 * j:32 * (j + 1), SP + t // 2, 256 * (t % 2):256 * (t % 2 + 1)],
                                             q_sb[:, P * t + 32 * j:P * t + 32 * (j + 1)],
                                             k_diag[:, w, :, :].rearrange("p h k -> p (h k)"), start=True, stop=True)
                    if t % 2:
                        i.then_inc(s_mm, 1)

            def project_q(s, g):
                if not isinstance(s, int) or s >= 1:
                    pe.wait_ge(q_ready, s)
                for k in range(KC):
                    i = split3(nc, ps[:, QB, :], wqk_hi[:, 2 * g, k, :], wqk_lo[:, 2 * g, k, :], xt_hi[:, k, :], xt_lo[:, k, :],
                               k == 0, k == KC - 1)
                i.then_inc(q_mm, 1)

            def project_k(s, g):
                if not isinstance(s, int) or s >= 1:
                    pe.wait_ge(ka_ready, s)
                    pe.wait_ge(kb_ready, s)
                for k in range(KC):
                    i = split3(nc, ps[:, KB, :], wqk_hi[:, 2 * g + 1, k, :], wqk_lo[:, 2 * g + 1, k, :], xt_hi[:, k, :], xt_lo[:, k, :],
                               k == 0, k == KC - 1)
                i.then_inc(k_mm, 1)

            def project_v(c, t, last=False):
                bank = (LAST_BANK if last else V_BANK)[t]
                if t == 0:
                    pe.wait_ge(gate_sb_ready, c + 1)
                if last and t >= 2:
                    pe.wait_ge(v_ready, TT * c + t - 1)
                elif t == 3:
                    pe.wait_ge(v_ready, TT * c + 1)
                for k in range(KC):
                    i = split3(nc, ps[:, bank, :], xt_hi[:, k, P * t:P * (t + 1)], xt_lo[:, k, P * t:P * (t + 1)],
                               wv_hi[:, k, :], wv_lo[:, k, :], k == 0, k == KC - 1)
                i.then_inc(v_mm, 1)

            def probs_t(s):
                pe.wait_ge(norm_ready, s + 1)
                if isinstance(s, int) and s == G * NCH - 1:
                    pe.wait_ge(pta_ready, s)
                    pe.wait_ge(ptb_ready, s)
                else:
                    pe.wait_ge(s_ready, 2 * s + 4)
                for t in range(TT):
                    for hp in range(2):
                        i = nc.tensor.transpose(ps[:, SP + t // 2, 256 * (t % 2) + P * hp:256 * (t % 2) + P * (hp + 1)],
                                                pn_sb[:, t, 2 * hp:2 * hp + 2, :].rearrange("p h k -> p (h k)"), ident[:, :])
                    if t % 2:
                        i.then_inc(pt_mm, 1)

            def pv(s, m):
                pe.wait_ge(pta_ready, s + 1)
                pe.wait_ge(ptb_ready, s + 1)
                if not isinstance(s, int) or s >= 1:
                    pe.wait_ge(o_ready, s)
                for t in range(TT):
                    for h in range(4):
                        col = HD * (4 * m + h)
                        i = nc.tensor.matmul(ps[HD * h:HD * (h + 1), OT, P * t:P * (t + 1)],
                                             v_sb[:, t, col:col + HD], pt_diag[:, t, h, :], start=True, stop=True)
                i.then_inc(o_mm, 1)

            def project_out(c, t, last=False):
                bank = (LAST_BANK if last else P_BANK)[t]
                if t == 0:
                    pe.wait_ge(o_ready, G * (c + 1))
                    if isinstance(c, int) and c == NCH - 1:
                        pe.wait_ge(out_ready, TT * c)
                    else:
                        pe.wait_ge(v_ready, TT * (c + 2))
                elif last and t >= 2:
                    pe.wait_ge(out_ready, TT * c + t - 1)
                elif t == 3:
                    pe.wait_ge(out_ready, TT * c + 1)
                for k in range(KC):
                    i = split3(nc, ps[:, bank, :], ot_hi[:, k, P * t:P * (t + 1)], ot_lo[:, k, P * t:P * (t + 1)],
                               wp_hi[:, k, :], wp_lo[:, k, :], k == 0, k == KC - 1)
                i.then_inc(p_mm, 1)

            def chunk(c, first=False):
                s = G * c
                if not first:
                    scores(s - 1)
                if first:
                    pe.wait_ge(wg_in, 16)
                    gate(c)
                    pe.wait_ge(raw_lo, Q0_SPLIT)
                pe.wait_ge(xt_ready, KC * (c + 1))
                project_q(s, 0)
                if not first:
                    probs_t(s - 2)
                project_k(s, 0)
                if not first:
                    pv(s - 2, 2)
                    gate(c)
                else:
                    pe.wait_ge(raw_lo, V_SPLIT)
                    project_v(c, 0)
                    project_v(c, 1)
                scores(s)
                project_q(s + 1, 1)
                if not first:
                    project_v(c, 0)
                    probs_t(s - 1)
                project_k(s + 1, 1)
                if not first:
                    pv(s - 1, 3)
                    project_v(c, 1)
                else:
                    pe.wait_ge(raw_lo, ALL_SPLIT)
                project_v(c, 2)
                project_v(c, 3)
                scores(s + 1)
                if not first:
                    for t in range(TT - 1):
                        project_out(c - 1, t)
                project_q(s + 2, 2)
                probs_t(s)
                project_k(s + 2, 2)
                pe.wait_ge(v_ready, TT * (c + 1))
                pv(s, 0)
                if not first:
                    project_out(c - 1, TT - 1)
                scores(s + 2)
                project_q(s + 3, 3)
                probs_t(s + 1)
                project_k(s + 3, 3)
                xt(c + 1)
                pv(s + 1, 1)

            def row_matmul(out, lhs, rhs):
                return nc.tensor.matmul(out, lhs, rhs, start=True, stop=True)

            def count(i):
                pe.wait_ge(part_counts, i + 1)
                pe.wait_ge(hits_summed, 2 * (i + 1))
                row_matmul(ps[:, SEARCH, 0:3], same[:, :], cnt[:, :]).then_inc(count_mm, 1)

            def last_chunk():
                c, s = NCH - 1, G * (NCH - 1)
                scores(s - 1)
                gate(c)
                project_q(s, 0)
                probs_t(s - 2)
                project_k(s, 0)
                pv(s - 2, 2)
                scores(s)
                project_q(s + 1, 1)
                probs_t(s - 1)
                project_k(s + 1, 1)
                count(0)
                pe.wait_ge(top_rows, 1)
                nc.tensor.transpose(ps[0:1, SEARCH, P:2 * P], top[:, 0:1], ident[:, :]).then_inc(top_t_mm, 1)
                pv(s - 1, 3)
                project_v(c, 0, last=True)
                count(1)
                pe.wait_ge(top_row_ready, 1)
                row_matmul(ps[:, SEARCH, P:P + 1], top_row[0:1, :], one[0:1, 0:1]).then_inc(top_mm, 1)
                project_v(c, 1, last=True)
                count(2)
                project_v(c, 2, last=True)
                count(3)
                project_v(c, 3, last=True)
                count(4)
                scores(s + 1)
                count(5)
                for t in range(TT):
                    project_out(c - 1, t, last=True)
                    count(6 + t)
                project_q(s + 2, 2)
                count(10)
                probs_t(s)
                project_k(s + 2, 2)
                count(11)
                pe.wait_ge(v_ready, TT * (c + 1))
                pv(s, 0)
                scores(s + 2)
                count(12)
                project_q(s + 3, 3)
                count(13)
                probs_t(s + 1)
                project_k(s + 3, 3)
                count(14)
                pv(s + 1, 1)
                count(15)
                scores(s + 3)
                pe.wait_ge(gt_eq_ready, 2)
                row_matmul(ps[:, SEARCH, 0:1], same[:, :], cnt[:, 0:1]).then_inc(room_mm, 1)
                row_matmul(ps[:, SEARCH, 1:2], earlier[:, :], cnt[:, 1:2]).then_inc(room_mm, 1)
                probs_t(s + 2)
                pv(s + 2, 2)
                pe.wait_ge(chosen_ready, 1)
                row_matmul(ps[:, SEARCH, 2:3], earlier[:, :], cnt[:, 2:3]).then_inc(base_mm, 1)
                pe.wait_ge(ka_ready, G * NCH)
                pe.wait_ge(kb_ready, G * NCH)
                pe.wait_ge(pos_ready, 1)
                for t in range(TT):
                    i = nc.tensor.transpose(ps[:, POS_T, P * t:P * (t + 1)], pos[:, P * t:P * (t + 1)], ident[:, :])
                i.then_inc(pos_t_mm, 1)
                pe.wait_ge(total_part, 1)
                pe.wait_ge(out_ready, TT * c)
                row_matmul(ps[:, TOTAL, 0:1], same[:, :], esum[:, :]).then_inc(total_mm, 1)
                probs_t(s + 3)
                pe.wait_ge(wgt_ready, 1)
                for t in range(TT):
                    i = nc.tensor.transpose(ps[:, WGT_T, P * t:P * (t + 1)], exps[:, P * t:P * (t + 1)], ident[:, :])
                i.then_inc(wgt_t_mm, 1)
                pv(s + 3, 3)
                for t in range(TT):
                    project_out(c, t, last=True)
                    if t == 0:
                        for g in range(GROUPS):
                            compact(nc, pe, lists, ps[:, SEARCH, :], 0, g)

            pe.wait_ge(consts, 15)
            xt(0)
            chunk(0, first=True)
            with pe.Fori(1, NCH - 1) as c:
                chunk(c)
            last_chunk()

        @block.vector
        def _(dve):
            def split_lo(u):
                _, hi, lo = units[u]
                dve.wait_ge(raw_hi, u + 1)
                nc.vector.tensor_tensor(lo, RAW[u % 3], hi.bitcast(F32), ALU.subtract).then_inc(raw_lo, 1)

            def layernorm_stats(c):
                if isinstance(c, int) and c == 0:
                    dve.wait_ge(x_first_in, 16)
                else:
                    dve.wait_ge(x_loaded, 16 * (c + 1))
                for t in range(TT):
                    if isinstance(c, int) and c == 0 and t == 2:
                        dve.wait_ge(x_loaded, 16)
                    i = nc.vector.bn_stats(stats[:, t, :], x_in[:, t, :])
                i.then_inc(stat_ready, 1)
                dve.wait_ge(stat_ready, c + 1)
                dve.nop(nofuse=True)
                for t in range(TT):
                    i = nc.vector.bn_aggr(mv[:, t, :], stats[:, t, :])
                i.then_inc(mv_ready, 1)
                dve.wait_ge(mv_ready, c + 1)
                nc.vector.tensor_scalar(veps[:, :], mv[:, :, 1], EPS, None, ALU.add).then_inc(veps_ready, 1)

            def layernorm_apply(c):
                dve.wait_ge(rstd_ready, c + 1)
                if not isinstance(c, int) or c >= 1:
                    dve.wait_ge(xn_stored, 16 * c)
                    dve.wait_ge(xt_mm, KC * c)
                for t in range(TT):
                    nc.vector.tensor_scalar(xn[:, t, :], x_in[:, t, :], mv[:, t, 0:1], rstd[:, t:t + 1],
                                            ALU.subtract, ALU.mult).then_inc(xn_ready, 1)

            def xt_lo_part(c):
                for k in range(KC):
                    dve.wait_ge(xt_hi_ready, KC * c + k + 1)
                    nc.vector.tensor_tensor(xt_lo[:, k, :], ps[:, X_BANK[k], :], xt_hi[:, k, :].bitcast(F32),
                                            ALU.subtract).then_inc(xt_ready, 1)

            def gate_rows(c):
                dve.wait_ge(gate_mm, c + 1)
                if not isinstance(c, int) or c >= 1:
                    dve.wait_ge(gate_stored, 64 * c)
                nc.vector.tensor_copy(g_sb[:, :], ps[:, G_BANK, :]).then_inc(gate_sb_ready, 1)

            def scale_and_bias(s, m):
                for b in range(2):
                    dve.wait_ge(s_mm, 2 * s + b + 1)
                    if b == 0 and (not isinstance(s, int) or s >= 1):
                        dve.wait_ge(exp_ready, s)
                    nc.vector.scalar_tensor_tensor(
                        s_sb[:, 2 * b:2 * b + 2, :, :].rearrange("p t h k -> p t (h k)"),
                        ps[:, SP + b, :].rearrange("p (t n) -> p t n", t=2), SCALE,
                        rel[:, 4 * m:4 * m + 4, :].rearrange("p h k -> p (h k)").unsqueeze(1).to_broadcast([P, 2, 4 * W]),
                        ALU.mult, ALU.add).then_inc(s_ready, 1)
                dve.wait_ge(s_ready, 2 * s + 2)
                nc.vector.tensor_reduce(s_max[:, :], s_sb[:, :, :, :].rearrange("p t h k -> p (t h) k"), AX.X, ALU.max).then_inc(max_ready, 1)

            def normaliser(s):
                dve.wait_ge(exp_ready, s + 1)
                nc.vector.tensor_reduce(s_sum[:, :], p_sb[:, :, :, :].rearrange("p t h k -> p (t h) k"), AX.X, ALU.add).then_inc(sum_ready, 1)
                dve.wait_ge(sum_ready, s + 1)
                if not isinstance(s, int) or s >= 1:
                    dve.wait_ge(norm_ready, s)
                nc.vector.reciprocal(s_rec[:, :], s_sum[:, :]).then_inc(rec_ready, 1)

            def finish_rows(c, t, last=False):
                if t == 0:
                    dve.wait_ge(res_ready, c + 1)
                dve.wait_ge(p_mm, TT * c + t + 1)
                nc.vector.tensor_tensor(x_res[:, t, :], ps[:, (LAST_BANK if last else P_BANK)[t], :], x_res[:, t, :],
                                        ALU.add).then_inc(out_ready, 1)

            def probs_t_part(s):
                dve.wait_ge(pt_mm, 2 * s + 2)
                if not isinstance(s, int) or s >= 1:
                    dve.wait_ge(o_mm, s)
                for out, src in diagonal_blocks(1):
                    i = nc.vector.tensor_copy(out, src)
                i.then_inc(ptb_ready, 1)

            def k_part(s, g):
                dve.wait_ge(k_mm, s + 1)
                for h in (2, 3):
                    r = slice(HD * h, HD * (h + 1))
                    i = nc.vector.tensor_scalar(k_diag[r, :, h, :], ps[r, KB, :].rearrange("p (w k) -> p w k", k=W),
                                                qk_bias[r, G + g:G + g + 1], None, ALU.add)
                i.then_inc(kb_ready, 1)

            def v_part(c, t, last=False):
                if t == 0 and (not isinstance(c, int) or c >= 1):
                    dve.wait_ge(o_mm, G * c)
                dve.wait_ge(v_mm, TT * c + t + 1)
                nc.vector.tensor_tensor(v_sb[:, t, :], ps[:, (LAST_BANK if last else V_BANK)[t], :], v_bias[:, :],
                                        ALU.add).then_inc(v_ready, 1)

            def o_lo_part(s, m):
                dve.wait_ge(o_hi_ready, s + 1)
                nc.vector.tensor_tensor(ot_lo[:, m, :], ps[:, OT, :], ot_hi[:, m, :].bitcast(F32), ALU.subtract).then_inc(o_ready, 1)

            def chunk(c, first=False):
                s = G * c
                if not first:
                    scale_and_bias(s - 1, 3)
                    probs_t_part(s - 2)
                    normaliser(s - 1)
                k_part(s, 0)
                if first:
                    v_part(c, 0)
                    v_part(c, 1)
                else:
                    o_lo_part(s - 2, 2)
                    gate_rows(c)
                layernorm_stats(c + 1)
                scale_and_bias(s, 0)
                if not first:
                    probs_t_part(s - 1)
                normaliser(s)
                k_part(s + 1, 1)
                layernorm_apply(c + 1)
                if not first:
                    o_lo_part(s - 1, 3)
                for t in range(2 if first else 0, TT):
                    v_part(c, t)
                scale_and_bias(s + 1, 1)
                if not first:
                    for t in range(TT - 1):
                        finish_rows(c - 1, t)
                probs_t_part(s)
                normaliser(s + 1)
                k_part(s + 2, 2)
                o_lo_part(s, 0)
                if not first:
                    finish_rows(c - 1, TT - 1)
                scale_and_bias(s + 2, 2)
                probs_t_part(s + 1)
                normaliser(s + 2)
                k_part(s + 3, 3)
                xt_lo_part(c + 1)
                o_lo_part(s + 1, 1)

            steps = [0]

            def then(i):
                steps[0] += 1
                i.then_inc(select_step, 1)
                dve.wait_ge(select_step, steps[0])

            v = nc.vector

            def threshold_float():
                then(v.tensor_scalar(flip[:, :], cand[:, :], 31, 0x7FFFFFFF, ALU.arith_shift_right, ALU.bitwise_and))
                then(v.scalar_tensor_tensor(thr[:, :], cand[:, :], -1, flip[:, :], ALU.bitwise_xor, ALU.bitwise_xor))

            def take_bits(i):
                dve.wait_ge(count_mm, i + 1)
                then(v.tensor_scalar(reach[:, :], ps[:, SEARCH, 0:3], float(CAP), 0.0, ALU.is_ge, ALU.add, accum_out=kept[:, :]))
                then(v.tensor_copy(kept_i[:, :], kept[:, :]))
                then(v.scalar_tensor_tensor(key[:, :], kept_i[:, :], 30 - 2 * i, key[:, :], ALU.logical_shift_left, ALU.bitwise_or))

            def search(i):
                if i > 0:
                    take_bits(i - 1)
                then(v.scalar_tensor_tensor(cand[:, :], pattern[:, :], 30 - 2 * i, key[:, 0:1].to_broadcast([P, 3]),
                                            ALU.logical_shift_left, ALU.bitwise_or))
                threshold_float()
                for j in range(2):
                    v.tensor_scalar(hits[:, j, :], gate_s[:, :], thr[:, j:j + 1].bitcast(F32), None, ALU.is_ge).then_inc(hits_ready, 1)
                v.tensor_scalar(hits[:, 2, :], gate_s[:, :], thr[:, 2:3].bitcast(F32), 0.0, ALU.is_ge, ALU.add,
                                accum_out=cnt[:, 2:3]).then_inc(part_counts, 1)

            def last_chunk():
                c, s = NCH - 1, G * (NCH - 1)
                scale_and_bias(s - 1, 3)
                gate_rows(c)
                k_part(s, 0)
                normaliser(s - 1)
                o_lo_part(s - 2, 2)
                dve.wait_ge(scores_in, 128)
                then(v.tensor_tensor(gate_s[:, :], gate_s[:, :], above[:, :], ALU.add))
                then(v.tensor_tensor(ties[:, :], ties[:, :], upto[:, :], ALU.add))
                then(v.tensor_tensor(gate_s[:, :], gate_s[:, :], ties[:, :], ALU.add))
                scale_and_bias(s, 0)
                search(0)
                v.tensor_reduce(top[:, :], gate_s[:, :], AX.X, ALU.max).then_inc(top_rows, 1)
                normaliser(s)
                dve.wait_ge(top_t_mm, 1)
                then(v.tensor_reduce(top_e[0:1, :], ps[0:1, SEARCH, P:2 * P].rearrange("p (c e) -> p e c", e=E), AX.X, ALU.max))
                v.tensor_copy(top_row[0:1, :].rearrange("p (c e) -> p c e", e=E),
                              top_e[0:1, :].unsqueeze(1).to_broadcast([1, NCH, E])).then_inc(top_row_ready, 1)
                search(1)
                o_lo_part(s - 1, 3)
                v_part(c, 0, last=True)
                dve.wait_ge(top_mm, 1)
                v.tensor_scalar(top[:, :], ps[:, SEARCH, P:P + 1], -1.0, None, ALU.mult).then_inc(top_ready, 1)
                search(2)
                for t in range(1, TT):
                    v_part(c, t, last=True)
                    search(2 + t)
                scale_and_bias(s + 1, 1)
                search(6)
                for t in range(TT):
                    finish_rows(c - 1, t, last=True)
                    search(7 + t)
                search(11)
                normaliser(s + 1)
                search(12)
                o_lo_part(s, 0)
                scale_and_bias(s + 2, 2)
                search(13)
                search(14)
                normaliser(s + 2)
                search(15)
                take_bits(15)
                then(v.tensor_copy(cand[:, :], key[:, 0:1].to_broadcast([P, 3])))
                threshold_float()
                bound = thr[:, 0:1].bitcast(F32)
                v.tensor_scalar(above[:, :], gate_s[:, :], bound, 0.0, ALU.is_gt, ALU.add, accum_out=cnt[:, 0:1]).then_inc(gt_eq_ready, 1)
                v.tensor_scalar(ties[:, :], gate_s[:, :], bound, 0.0, ALU.is_equal, ALU.add, accum_out=cnt[:, 1:2]).then_inc(gt_eq_ready, 1)
                o_lo_part(s + 1, 1)
                scale_and_bias(s + 3, 3)
                dve.wait_ge(gt_eq_ready, 2)
                then(v.tensor_tensor_scan(upto[:, :], ones_row[:, :], ties[:, :], 0.0, ALU.mult, ALU.add))
                dve.wait_ge(room_mm, 2)
                then(v.tensor_scalar(room[:, 0:1], ps[:, SEARCH, 0:1], -1.0, float(CAP), ALU.mult, ALU.add))
                then(v.tensor_tensor(room[:, 1:2], room[:, 0:1], ps[:, SEARCH, 1:2], ALU.subtract))
                then(v.scalar_tensor_tensor(ties[:, :], upto[:, :], room[:, 1:2], ties[:, :], ALU.is_le, ALU.mult))
                v.scalar_tensor_tensor(above[:, :], above[:, :], 1.0, ties[:, :], ALU.mult, ALU.add,
                                       accum_out=cnt[:, 2:3]).then_inc(chosen_ready, 1)
                normaliser(s + 3)
                dve.wait_ge(chosen_ready, 1)
                then(v.tensor_tensor_scan(upto[:, :], ones_row[:, :], above[:, :], 0.0, ALU.mult, ALU.add))
                dve.wait_ge(base_mm, 1)
                then(v.tensor_scalar(room[:, 0:1], ps[:, SEARCH, 2:3], -1.0 - N, None, ALU.add))
                then(v.scalar_tensor_tensor(upto[:, :], upto[:, :], room[:, 0:1], above[:, :], ALU.add, ALU.mult))
                v.tensor_scalar(pos[:, :], upto[:, :], float(N), None, ALU.add).then_inc(pos_ready, 1)
                dve.wait_ge(exps_ready, 1)
                v.scalar_tensor_tensor(exps[:, :], exps[:, :], 1.0, above[:, :], ALU.mult, ALU.mult,
                                       accum_out=esum[:, :]).then_inc(total_part, 1)
                o_lo_part(s + 2, 2)
                by_expert = "p (j c e) -> p e c j"
                dve.wait_ge(pos_t_mm, 1)
                then(v.tensor_copy(pos_i[:, :], ps[:, POS_T, :]))
                then(v.tensor_scalar(part_i[:, :], pos_i[:, :], P - 1, None, ALU.bitwise_and))

                def to_experts(out, flat):
                    for e in range(E):
                        n = v.tensor_copy(out[:, e, :].rearrange("p (c j) -> p c j", j=TT),
                                          flat.rearrange(by_expert, j=TT, e=E)[:, e])
                    return n

                then(to_experts(lists.slot_b, part_i[:, :]))
                dve.wait_ge(total_mm, 1)
                dve.wait_ge(total_part, 1)
                then(v.tensor_copy(room[:, 1:2], ps[:, TOTAL, 0:1]))
                then(v.reciprocal(room[:, 1:2], room[:, 1:2]))
                v.tensor_scalar(exps[:, :], exps[:, :], room[:, 1:2], None, ALU.mult).then_inc(wgt_ready, 1)
                then(v.tensor_scalar(part_i[:, :], pos_i[:, :], 7, None, ALU.logical_shift_right))
                then(to_experts(lists.slot_a, part_i[:, :]))
                dve.wait_ge(xn_stored, 16 * NCH)
                dve.wait_ge(xt_mm, KC * NCH)
                slots_one_hot(nc, dve, lists, 0, 0)
                o_lo_part(s + 3, 3)
                slots_one_hot(nc, dve, lists, 0, 1)
                places_one_hot(nc, dve, lists, 0)
                dve.wait_ge(wgt_part_ready, 3)
                weights_one_hot(nc, dve, lists, 0)
                for g in range(2, GROUPS):
                    slots_one_hot(nc, dve, lists, 0, g)
                take_sums(nc, dve, lists, ps[:, SEARCH, :], 0)
                expert_list(nc, dve, lists, 0, 0)
                finish_rows(c, 0, last=True)
                places_one_hot(nc, dve, lists, 1)
                finish_rows(c, 1, last=True)
                weights_one_hot(nc, dve, lists, 1)
                finish_rows(c, 2, last=True)
                slots_one_hot(nc, dve, lists, 1, 0)
                slots_one_hot(nc, dve, lists, 1, 1)
                finish_rows(c, 3, last=True)

            layernorm_stats(0)
            layernorm_apply(0)
            split_lo(0)
            split_lo(1)
            xt_lo_part(0)
            for u in range(2, V_SPLIT):
                split_lo(u)
            gate_rows(0)
            for u in range(V_SPLIT, ALL_SPLIT):
                split_lo(u)
            dve.wait_ge(const_in, 96)
            dve.wait_ge(consts, 15)
            chunk(0, first=True)
            with dve.Fori(1, NCH - 1) as c:
                chunk(c)
            last_chunk()


def expert_block(nc, d, lists):
    ctx = ExitStack()
    with ctx:
        def sb(name, shape, dt=F32):
            return ctx.enter_context(nc.sbuf_tensor(name, shape, dt))

        def sem(name):
            return ctx.enter_context(nc.semaphore(name))

        HALVES = 2
        w13_hi, w13_lo = sb("w13_hi", [P, FM, 2, KC, P], F32R), sb("w13_lo", [P, FM, 2, KC, P], F32R)
        w2_hi, w2_lo = sb("w2_hi", [P, FM, C], F32R), sb("w2_lo", [P, FM, C], F32R)
        h_hi, h_lo = sb("h_hi", [P, FM, T], F32R), sb("h_lo", [P, FM, T], F32R)
        xg, y, ident = lists.x_in, lists.x_res, lists.ident
        weight, raw, w_in = lists.weight, lists.raw, lists.w_in
        xgt_hi, xgt_lo = sb("xgt_hi", [P, KC, T], F32R), sb("xgt_lo", [P, KC, T], F32R)
        silu, hm = sb("silu", [P, 2, T]), sb("hm", [P, 2, T])
        ps = ctx.enter_context(nc.psum_tensor("ps_e", [P, 8, 512], F32))
        DOWN, LISTS = 4, 7

        w_hi_ready, w_ready = sem("w_hi_ready"), sem("w_ready")
        xgt_mm, xgt_hi_ready, xgt_ready = sem("xgt_mm"), sem("xgt_hi_ready"), sem("xgt_ready")
        up1_mm, up3_mm, silu_ready, hm_ready = sem("up1_mm"), sem("up3_mm"), sem("silu_ready"), sem("hm_ready")
        h_hi_ready, h_ready = sem("h_hi_ready"), sem("h_ready")
        down_mm, y_mm, y_ready, scattered = sem("down_mm"), sem("y_mm"), sem("y_ready"), sem("scattered")

        block = ctx.enter_context(nc.Block())
        UNITS = FM + FM // 2

        def unit_views(u):
            if u < FM:
                return [w[:, u, :, :, :].rearrange("p a b c -> p (a b c)") for w in (w13_hi, w13_lo)]
            v = 2 * (u - FM)
            return [w[:, v:v + 2, :].rearrange("p a b -> p (a b)") for w in (w2_hi, w2_lo)]

        AHEAD = UNITS - FM

        FIRST_SPLITS = [(0, u) for u in range(AHEAD, UNITS)]


        @block.sync
        def _(sp):
            def load_unit(e, u):
                n = UNITS * e + u
                if not isinstance(n, int) or n >= 2:
                    sp.wait_ge(w_ready, n - 1)
                src = d["w13"][e, u] if u < FM else d["w2"][e, u - FM]
                sp.dma_start(raw[u % 2], src).then_inc(w_in[u % 2], 16)

            for u in range(2, UNITS):
                load_unit(0, u)
            with sp.Fori(1, E) as e:
                for u in range(UNITS):
                    load_unit(e, u)

        @block.gpsimd
        def _(pool):
            def gather_half(q, par, tile0, e_idx):
                pool.wait_ge(lists.idx_ready, e_idx)
                pool.wait_ge(xgt_mm, KC * q)
                gather(nc, pool, lists, d["xn"], par, tile0)

            def scatter(q, par, tile0):
                for t in range(TT):
                    pool.wait_ge(y_ready, TT * q + t + 1)
                    if t == 0 and (not isinstance(q, int) or q >= 1):
                        pool.wait_ge(scattered, 16 * TT * q)
                    pool.nop(nofuse=True)
                    nc.gpsimd.indirect_dma_start(
                        out=d["out"], out_offset=bass.IndirectOffsetOnAxis(ap=lists.idx[par][:, tile0 + t:tile0 + t + 1], axis=0),
                        in_=y[:, t, :], in_offset=None, compute_op=ALU.add).then_inc(scattered, 16)

            pool.wait_ge(lists.out_stored, 16 * NCH)

            def expert(e, par, first=False, last=False):
                q = HALVES * e
                gather_half(q + 1, par, TT, e + 1)
                if not first:
                    scatter(q - 1, 1 - par, TT)
                if not last:
                    gather_half(q + 2, 1 - par, 0, e + 2)
                scatter(q, par, 0)

            expert(0, 0, first=True)
            expert(1, 1)
            with pool.Fori(1, E // 2 - 1) as i:
                expert(2 * i, 0)
                expert(2 * i + 1, 1)
            expert(E - 2, 0)
            expert(E - 1, 1, last=True)
            scatter(HALVES * E - 1, 1, TT)
            pool.wait_ge(scattered, 16 * TT * HALVES * E)

        @block.scalar
        def _(act):
            def split_hi(e, u):
                n = UNITS * e + u
                act.wait_ge(w_in[u % 2], 16 * (UNITS // 2 * e + u // 2 + 1))
                if not isinstance(e, int) or e >= 1:
                    if u < FM:
                        act.wait_ge(up3_mm, FM * (HALVES * e - 1) + u + 1)
                    else:
                        act.wait_ge(y_mm, TT * HALVES * e)
                nc.scalar.activation(unit_views(u)[0], raw[u % 2], ACT.Copy).then_inc(w_hi_ready, 1)

            def xgt_hi_part(q):
                for k in range(KC):
                    act.wait_ge(xgt_mm, KC * q + k + 1)
                    nc.scalar.activation(xgt_hi[:, k, :], ps[:, k, :], ACT.Copy).then_inc(xgt_hi_ready, 1)

            def half(e, q, hf, par, splits, last=False):
                for m in range(FM):
                    n = FM * q + m
                    act.wait_ge(up1_mm, n + 1)
                    if not isinstance(n, int) or n >= 2:
                        act.wait_ge(hm_ready, n - 1)
                    nc.scalar.activation(silu[:, m % 2, :], ps[:, 2 * (m % 2), :], ACT.Silu).then_inc(silu_ready, 1)
                    act.wait_ge(hm_ready, n + 1)
                    if not isinstance(q, int) or q >= 1:
                        if m < FM - 1:
                            act.wait_ge(down_mm, (FM - 1) * (q - 1) + m + 1)
                        else:
                            act.wait_ge(y_mm, TT * q)
                    nc.scalar.activation(h_hi[:, m, :], hm[:, m % 2, :], ACT.Copy).then_inc(h_hi_ready, 1)
                    if m < len(splits):
                        split_hi(*splits[m])
                if not last:
                    xgt_hi_part(q + 1)
                for t in range(TT):
                    act.wait_ge(y_mm, TT * q + t + 1)
                    if t == 0 and isinstance(q, int) and q == 0:
                        act.wait_ge(lists.out_stored, 16 * NCH)
                    elif t == 0:
                        act.wait_ge(scattered, 16 * TT * q)
                    s = TT * hf + t
                    nc.scalar.activation(y[:, t, :], ps[:, DOWN + t, :], ACT.Copy, scale=weight[par][:, s:s + 1]).then_inc(y_ready, 1)

            def expert(e, par, first=False, last=False):
                q = HALVES * e
                half(e, q, 0, par, FIRST_SPLITS if first else [(e, FM + i) for i in range(FM // 2)])
                half(e, q + 1, 1, par, [] if last else [(e + 1, i) for i in range(FM)], last=last)

            split_hi(0, 0)
            xgt_hi_part(0)
            for u in range(1, AHEAD):
                split_hi(0, u)
            expert(0, 0, first=True)
            expert(1, 1)
            with act.Fori(1, E // 2 - 1) as i:
                expert(2 * i, 0)
                expert(2 * i + 1, 1)
            expert(E - 2, 0)
            expert(E - 1, 1, last=True)

        @block.tensor
        def _(pe):
            def xgt(q):
                pe.wait_ge(lists.xg_in, 16 * TT * (q + 1))
                for k in range(KC):
                    if k % 2 == 0 and (not isinstance(q, int) or q >= 1):
                        pe.wait_ge(hm_ready, FM * q - 1 + k // 2)
                    for t in range(TT):
                        i = nc.tensor.transpose(ps[:, k, P * t:P * (t + 1)], xg[:, t, P * k:P * (k + 1)], ident[:, :])
                    i.then_inc(xgt_mm, 1)

            def up(q, e, first_half, next_list=False):
                pe.wait_ge(xgt_ready, KC * (q + 1))
                for m in range(FM):
                    if first_half:
                        pe.wait_ge(w_ready, UNITS * e + m + 1)
                    if m >= 2:
                        pe.wait_ge(hm_ready, FM * q + m - 1)
                    for j, s in ((0, up1_mm), (1, up3_mm)):
                        for k in range(KC):
                            i = split3(nc, ps[:, 2 * (m % 2) + j, :], w13_hi[:, m, j, k, :], w13_lo[:, m, j, k, :],
                                       xgt_hi[:, k, :], xgt_lo[:, k, :], k == 0, k == KC - 1)
                        i.then_inc(s, 1)
                        if next_list and j == 0:
                            if m == 0 and (not isinstance(q, int) or q >= 1):
                                pe.wait_ge(y_ready, TT * q)
                            compact(nc, pe, lists, ps[:, LISTS, :], e + 1, m)

            def down(q, e, first_half, next_list=False, tiles=(range(TT),)):
                if not isinstance(q, int) or q >= 1:
                    pe.wait_ge(y_ready, TT * q)
                if next_list:
                    pe.wait_ge(lists.got_ready, e + 2)
                for some in tiles:
                    for k in range(FM):
                        pe.wait_ge(h_ready, FM * q + k + 1)
                        if first_half and k % 2 == 0:
                            pe.wait_ge(w_ready, UNITS * e + FM + k // 2 + 1)
                        for t in some:
                            sl = slice(P * t, P * (t + 1))
                            i = split3(nc, ps[:, DOWN + t, :], h_hi[:, k, sl], h_lo[:, k, sl], w2_hi[:, k, :], w2_lo[:, k, :],
                                       k == 0, k == FM - 1)
                            if k == FM - 1:
                                i.then_inc(y_mm, 1)
                        if k < FM - 1:
                            i.then_inc(down_mm, 1)

            def expert(e, last=False):
                q = HALVES * e
                up(q, e, True, next_list=not last)
                xgt(q + 1)
                down(q, e, True, next_list=not last)
                up(q + 1, e, False)
                if not last:
                    xgt(q + 2)
                down(q + 1, e, False, tiles=((0, 1), (2, 3)) if last else (range(TT),))

            xgt(0)
            expert(0)
            with pe.Fori(1, E - 1) as e:
                expert(e)
            expert(E - 1, last=True)

        @block.vector
        def _(dve):
            v = nc.vector

            def split_lo(e, u):
                n = UNITS * e + u
                dve.wait_ge(w_hi_ready, n + 1)
                hi, lo = unit_views(u)
                v.tensor_tensor(lo, raw[u % 2], hi.bitcast(F32), ALU.subtract).then_inc(w_ready, 1)

            def xgt_lo_part(q):
                for k in range(KC):
                    dve.wait_ge(xgt_hi_ready, KC * q + k + 1)
                    v.tensor_tensor(xgt_lo[:, k, :], ps[:, k, :], xgt_hi[:, k, :].bitcast(F32), ALU.subtract).then_inc(xgt_ready, 1)

            def half(q, splits, lists_of=None, first=False):
                def lo(m):
                    n = FM * q + m
                    dve.wait_ge(h_hi_ready, n + 1)
                    v.tensor_tensor(h_lo[:, m, :], hm[:, m % 2, :], h_hi[:, m, :].bitcast(F32), ALU.subtract).then_inc(h_ready, 1)

                for m in range(FM):
                    n = FM * q + m
                    if lists_of is not None:
                        if m == 0 and not first:
                            slots_one_hot(nc, dve, lists, lists_of, 0)
                            slots_one_hot(nc, dve, lists, lists_of, 1)
                        elif 0 < m < GROUPS - 1:
                            slots_one_hot(nc, dve, lists, lists_of, m + 1)
                        elif m == GROUPS - 1:
                            take_sums(nc, dve, lists, ps[:, LISTS, :], lists_of)
                    dve.wait_ge(silu_ready, n + 1)
                    dve.wait_ge(up3_mm, n + 1)
                    v.tensor_tensor(hm[:, m % 2, :], ps[:, 2 * (m % 2) + 1, :], silu[:, m % 2, :], ALU.mult).then_inc(hm_ready, 1)
                    lo(m)
                    if m < len(splits):
                        split_lo(*splits[m])

            def expert(e, par, first=False, last=False, second_next=True):
                q = HALVES * e
                half(q, FIRST_SPLITS if first else [(e, FM + i) for i in range(FM // 2)],
                     lists_of=None if last else e + 1, first=first)
                if not last:
                    expert_list(nc, dve, lists, e + 1, 1 - par, scattered)
                xgt_lo_part(q + 1)
                if second_next:
                    places_one_hot(nc, dve, lists, e + 2)
                    weights_one_hot(nc, dve, lists, e + 2)
                half(q + 1, [] if last else [(e + 1, i) for i in range(FM)])
                if not last:
                    xgt_lo_part(q + 2)

            split_lo(0, 0)
            xgt_lo_part(0)
            for u in range(1, AHEAD):
                split_lo(0, u)
            expert(0, 0, first=True)
            expert(1, 1)
            with dve.Fori(1, E // 2 - 1) as i:
                expert(2 * i, 0)
                expert(2 * i + 1, 1)
            expert(E - 2, 0, second_next=False)
            expert(E - 1, 1, last=True, second_next=False)


def build_kernel(nc, x, wqk, wv, wp, wg, rel, qkb, vb, pb, same, earlier, w13, w2, out):
    ctx = ExitStack()
    with ctx:
        lists = Lists(nc, ctx)
        xn = nc.dram_tensor("xn_rows", [N, C], F32, kind="Internal").ap()
        gate = nc.dram_tensor("gate_rows", [4, P, T], F32, kind="Internal").ap()
        rows = "(c t p) n -> c p t n"
        d = {"x": x.rearrange(rows, t=TT, p=P), "out": out.rearrange(rows, t=TT, p=P),
             "xn": xn.rearrange(rows, t=TT, p=P), "xn_rows": xn, "gate": gate, "wqk": wqk, "wv": wv, "wp": wp, "wg": wg,
             "w13": w13, "rel": rel, "qkb": qkb, "vb": vb, "pb": pb, "same": same, "earlier": earlier}
        attention_block(nc, d, lists)
        expert_block(nc, {"xn": xn, "out": out, "w13": w13, "w2": w2}, lists)


def kernel(L0_attn_x, L0_attn_qkv_w, L0_attn_qkv_b, L0_attn_proj_w, L0_attn_proj_b, L0_attn_rel_bias,
           L0_ffn_Wg, L0_ffn_W1, L0_ffn_W2, L0_ffn_W3):
    import numpy as np
    import concourse.bacc as bacc
    from concourse.bass_utils import run_bass_kernel_spmd

    def rows(w):
        return np.ascontiguousarray(np.asarray(w).reshape(KC, P, -1).transpose(1, 0, 2))

    x = np.asarray(L0_attn_x)
    qkv_b = np.asarray(L0_attn_qkv_b)
    dist = np.arange(W)[:, None] - np.arange(W)[None, :] + W - 1
    rel = np.asarray(L0_attn_rel_bias)[dist].transpose(0, 2, 1)
    w13 = np.stack([np.asarray(L0_ffn_W1), np.asarray(L0_ffn_W3)], 1)
    w13 = w13.reshape(E, 2, FM, P, KC, P).transpose(0, 2, 5, 1, 4, 3)
    w2 = np.asarray(L0_ffn_W2).reshape(E, C, FM // 2, 2, P).transpose(0, 2, 4, 3, 1)
    r = np.arange(P)
    arrays = {
        "x": x.reshape(N, C),
        "wqk": rows(L0_attn_qkv_w)[:, :, :2 * C].reshape(P, KC, 2, G, P).transpose(0, 3, 2, 1, 4).reshape(P, -1),
        "wv": rows(L0_attn_qkv_w)[:, :, 2 * C:].reshape(P, -1),
        "wp": rows(L0_attn_proj_w).reshape(P, -1),
        "wg": np.pad(rows(np.asarray(L0_ffn_Wg).T), ((0, 0), (0, 0), (0, GATE_COLS - E))).reshape(P, -1),
        "rel": np.concatenate([rel, rel], 0),
        "qkb": qkv_b[:2 * C].reshape(2 * G, P).T,
        "vb": np.broadcast_to(qkv_b[2 * C:], (P, C)),
        "pb": np.broadcast_to(np.asarray(L0_attn_proj_b), (P, C)),
        "same": (r[:, None] % E == r[None, :] % E).astype(np.float32),
        "earlier": ((r[:, None] % E == r[None, :] % E) & (r[:, None] < r[None, :])).astype(np.float32),
        "w13": w13.reshape(E, FM, P, 2 * KC * P),
        "w2": w2.reshape(E, FM // 2, P, 2 * C),
    }
    nc = bacc.Bacc("TRN2", target_bir_lowering=False, num_devices=1)
    arrays = {f"in_{name}": np.ascontiguousarray(a) for name, a in arrays.items()}
    args = [nc.dram_tensor(name, a.shape, mybir.dt.from_np(a.dtype), kind="ExternalInput").ap()
            for name, a in arrays.items()]
    args.append(nc.dram_tensor("out_rows", (N, C), F32, kind="ExternalOutput").ap())
    build_kernel(nc, *args)
    result = run_bass_kernel_spmd(nc, [arrays], core_ids=[0])
    return result.results[0]["out_rows"].reshape(x.shape)
```
